# Optimizing a Trainium2 kernel written in Bass

```python
import numpy as np
import jax
import jax.numpy as jnp

def _softmax(x, axis=-1):
    return jax.nn.softmax(x, axis=axis)

def _gelu(x):
    return jax.nn.gelu(x, approximate=True)

def _silu(x):
    return jax.nn.silu(x)

def _sigmoid(x):
    return jax.nn.sigmoid(x)

def _layernorm(x, axis=-1, eps=1e-05):
    m = jnp.mean(x, axis=axis, keepdims=True)
    v = jnp.var(x, axis=axis, keepdims=True)
    return (x - m) / jnp.sqrt(v + eps)

def _scatter_add(tgt, idx, src, axis=0):
    return tgt.at[idx].add(src)

def _segment_sum(src, seg, n):
    return jax.ops.segment_sum(src, seg, n)
kernel_name = 'mk_hybrid_d2_jaxref_r8_2926e0'

def setup_inputs(seed: int=0):
    np.random.seed(seed)
    _w = jnp.asarray

    def _L0_attn_a_setup():
        import jax, jax.numpy as jnp
        import numpy as np
        EPS = 1e-06
        ROPE_BASE = 10000.0

        def _rope(t):
            B, T, H, D = t.shape
            half = D // 2
            inv_freq = 1.0 / ROPE_BASE ** (jnp.arange(0, half, dtype=jnp.float32) * 2.0 / D)
            ang = jnp.arange(T, dtype=jnp.float32)[:, None] * inv_freq[None, :]
            cos = jnp.cos(ang)[None, :, None, :]
            sin = jnp.sin(ang)[None, :, None, :]
            x1, x2 = (t[..., :half], t[..., half:])
            return jnp.concatenate([x1 * cos - x2 * sin, x2 * cos + x1 * sin], axis=-1)

        def _rmsnorm(t, w):
            ms = jnp.mean(t * t, axis=-1, keepdims=True)
            return t * jax.lax.rsqrt(ms + EPS) * w
        key = jax.random.key(seed)
        k1, k2, k3 = jax.random.split(key, 3)
        B, T, C, H = (2, 256, 128, 16)
        D = C // H
        s = 1.0 / np.sqrt(C)
        return {'x': jax.random.normal(k1, (B, T, C), dtype=jnp.float32), 'w_qkv': jax.random.normal(k2, (3 * C, C), dtype=jnp.float32) * s, 'w_out': jax.random.normal(k3, (C, C), dtype=jnp.float32) * s, 'q_norm_w': jnp.ones((D,), dtype=jnp.float32), 'k_norm_w': jnp.ones((D,), dtype=jnp.float32)}
    _L0_attn_a_in = _L0_attn_a_setup()

    def _L0_attn_b_setup():
        import jax, jax.numpy as jnp
        import numpy as np
        B, T, C, H, VBD = (2, 256, 128, 16, 256)
        KD = C // H
        VD = VBD // H
        EPS = float(np.finfo(np.float32).eps)

        def _inner_mask(seq_len):
            gamma = jnp.log(1.0 - 2.0 ** (-5.0 - jnp.arange(H, dtype=jnp.float32)))
            idx = jnp.arange(seq_len, dtype=jnp.float32)
            diff = idx[:, None] - idx[None, :]
            causal = diff >= 0
            decay = jnp.where(causal, jnp.exp(gamma[:, None, None] * diff), 0.0)
            scale = jnp.sqrt(decay.sum(-1, keepdims=True))
            return decay / scale
        key = jax.random.key(seed)
        ks = jax.random.split(key, 9)
        s = 0.02
        return {'x': jax.random.normal(ks[0], (B, T, C), dtype=jnp.float32), 'W_qk': jax.random.normal(ks[1], (C, 2 * C), dtype=jnp.float32) * s, 'b_qk': jnp.zeros((2 * C,), dtype=jnp.float32), 'W_v': jax.random.normal(ks[2], (C, VBD), dtype=jnp.float32) * s, 'b_v': jnp.zeros((VBD,), dtype=jnp.float32), 'W_g': jax.random.normal(ks[3], (C, VBD), dtype=jnp.float32) * s, 'b_g': jnp.zeros((VBD,), dtype=jnp.float32), 'W_o': jax.random.normal(ks[4], (VBD, C), dtype=jnp.float32) * s, 'b_o': jnp.zeros((C,), dtype=jnp.float32)}
    _L0_attn_b_in = _L0_attn_b_setup()

    def _L0_ffn_setup():
        import jax, jax.numpy as jnp
        import numpy as np
        D_MODEL = 128
        M = 64
        INNER = 16
        key = jax.random.key(seed)
        ks = jax.random.split(key, 9)

        def init(k, shape, fan_in):
            bound = 1.0 / np.sqrt(fan_in)
            return jax.random.uniform(k, shape, jnp.float32, -bound, bound)
        x = jax.random.normal(ks[0], (16, 512, D_MODEL), dtype=jnp.float32)
        Win = init(ks[1], (D_MODEL, M), D_MODEL)
        bin_ = init(ks[2], (M,), D_MODEL)
        W1 = init(ks[3], (M, INNER), 1)
        b1 = init(ks[4], (M, INNER), 1)
        W2 = init(ks[5], (M, INNER), INNER)
        b2 = init(ks[6], (M,), INNER)
        Wout = init(ks[7], (M, D_MODEL), M)
        bout = init(ks[8], (D_MODEL,), M)
        return {'x': x, 'Win': Win, 'bin_': bin_, 'W1': W1, 'b1': b1, 'W2': W2, 'b2': b2, 'Wout': Wout, 'bout': bout}
    _L0_ffn_in = _L0_ffn_setup()

    def _L1_attn_a_setup():
        import jax, jax.numpy as jnp
        import numpy as np
        B, L, E, H = (2, 512, 128, 16)
        D = E // H
        CHUNK = 32

        def _linear_attention(x, W_qkv, W_out):
            Bz, Lz, Ez = x.shape
            scale = D ** (-0.5)
            qkv = x @ W_qkv.T
            qkv = qkv.reshape(Bz, Lz, 3, H, D).transpose(2, 0, 3, 1, 4)
            q, k, v = (qkv[0], qkv[1], qkv[2])
            q = (jax.nn.elu(q) + 1.0) * scale
            k = jax.nn.elu(k) + 1.0
            nc = Lz // CHUNK

            def to_chunks(t):
                return t.reshape(Bz, H, nc, CHUNK, D).transpose(2, 0, 1, 3, 4)
            qc, kc, vc = (to_chunks(q), to_chunks(k), to_chunks(v))
            causal = jnp.tril(jnp.ones((CHUNK, CHUNK), dtype=x.dtype))

            def step(carry, inp):
                S, Z = carry
                qi, ki, vi = inp
                attn = jnp.einsum('bhld,bhmd->bhlm', qi, ki) * causal
                num = jnp.einsum('bhlm,bhme->bhle', attn, vi) + jnp.einsum('bhld,bhde->bhle', qi, S)
                den = attn.sum(-1) + jnp.einsum('bhld,bhd->bhl', qi, Z)
                S = S + jnp.einsum('bhmd,bhme->bhde', ki, vi)
                Z = Z + ki.sum(axis=2)
                return ((S, Z), (num, den))
            S0 = jnp.zeros((Bz, H, D, D), dtype=x.dtype)
            Z0 = jnp.zeros((Bz, H, D), dtype=x.dtype)
            _, (num, den) = jax.lax.scan(step, (S0, Z0), (qc, kc, vc))
            num = num.transpose(1, 2, 0, 3, 4).reshape(Bz, H, Lz, D)
            den = den.transpose(1, 2, 0, 3).reshape(Bz, H, Lz)
            den = jnp.maximum(den, 1e-06)
            out = num / den[..., None]
            out = out.transpose(0, 2, 1, 3).reshape(Bz, Lz, Ez)
            return out @ W_out.T
        key = jax.random.key(seed)
        k1, k2, k3 = jax.random.split(key, 3)
        x = jax.random.normal(k1, (B, L, E), dtype=jnp.float32)
        W_qkv = jax.random.normal(k2, (3 * E, E), dtype=jnp.float32) * 0.02
        W_out = jax.random.normal(k3, (E, E), dtype=jnp.float32) * 0.02
        return {'x': x, 'W_qkv': W_qkv, 'W_out': W_out}
    _L1_attn_a_in = _L1_attn_a_setup()

    def _L1_attn_b_setup():
        import jax, jax.numpy as jnp
        import numpy as np
        B, T, C = (8, 256, 128)
        NEG_INF = -1e+38

        def wkv(w, u, k, v):
            kt = jnp.swapaxes(k, 0, 1)
            vt = jnp.swapaxes(v, 0, 1)
            Bn, Cn = (k.shape[0], k.shape[2])
            aa = jnp.zeros((Bn, Cn), k.dtype)
            bb = jnp.zeros((Bn, Cn), k.dtype)
            pp = jnp.full((Bn, Cn), NEG_INF, k.dtype)

            def step(carry, kv):
                aa, bb, pp = carry
                kk, vv = kv
                ww = u + kk
                p = jnp.maximum(pp, ww)
                e1 = jnp.exp(pp - p)
                e2 = jnp.exp(ww - p)
                y = (e1 * aa + e2 * vv) / (e1 * bb + e2)
                ww2 = pp + w
                p2 = jnp.maximum(ww2, kk)
                e1 = jnp.exp(ww2 - p2)
                e2 = jnp.exp(kk - p2)
                return ((e1 * aa + e2 * vv, e1 * bb + e2, p2), y)
            _, y = jax.lax.scan(step, (aa, bb, pp), (kt, vt))
            return jnp.swapaxes(y, 0, 1)
        key = jax.random.key(seed)
        ks = jax.random.split(key, 10)
        s = 1.0 / np.sqrt(C)
        return {'x': jax.random.normal(ks[0], (B, T, C), jnp.float32), 'time_decay': jax.random.normal(ks[1], (C,), jnp.float32), 'time_first': jax.random.normal(ks[2], (C,), jnp.float32), 'time_mix_k': jax.random.uniform(ks[3], (1, 1, C), jnp.float32), 'time_mix_v': jax.random.uniform(ks[4], (1, 1, C), jnp.float32), 'time_mix_r': jax.random.uniform(ks[5], (1, 1, C), jnp.float32), 'Wk': jax.random.normal(ks[6], (C, C), jnp.float32) * s, 'Wv': jax.random.normal(ks[7], (C, C), jnp.float32) * s, 'Wr': jax.random.normal(ks[8], (C, C), jnp.float32) * s, 'Wo': jax.random.normal(ks[9], (C, C), jnp.float32) * s}
    _L1_attn_b_in = _L1_attn_b_setup()

    def _L1_ffn_setup():
        import jax, jax.numpy as jnp
        import numpy as np
        EPS = 1e-05

        def _layernorm(x, w, b):
            mu = jnp.mean(x, axis=-1, keepdims=True)
            var = jnp.mean((x - mu) ** 2, axis=-1, keepdims=True)
            return (x - mu) * jax.lax.rsqrt(var + EPS) * w + b

        def _rope_tables(T, D, base=10000.0):
            inv_freq = 1.0 / base ** (jnp.arange(0, D, 2, dtype=jnp.float32) / D)
            t = jnp.arange(T, dtype=jnp.float32)
            freqs = jnp.einsum('i,j->ij', t, inv_freq)
            emb = jnp.concatenate([freqs, freqs], axis=-1)
            return (jnp.cos(emb), jnp.sin(emb))

        def _rotate_half(x):
            x1, x2 = (x[..., :x.shape[-1] // 2], x[..., x.shape[-1] // 2:])
            return jnp.concatenate([-x2, x1], axis=-1)

        def _attn(x, ln_w, ln_b, conv_w, attn_w, proj_w, n_head):
            B, T, C = x.shape
            D = C // n_head
            h = _layernorm(x, ln_w, ln_b)
            hc = jnp.transpose(h, (0, 2, 1))
            hc = jnp.pad(hc, ((0, 0), (0, 0), (2, 0)))
            hc = jax.lax.conv_general_dilated(hc, conv_w, window_strides=(1,), padding='VALID', dimension_numbers=('NCH', 'OIH', 'NCH'), feature_group_count=C)
            h = jnp.transpose(hc, (0, 2, 1))
            qkv = h @ attn_w
            q, k, v = jnp.split(qkv, 3, axis=-1)
            q = q.reshape(B, T, n_head, D)
            k = k.reshape(B, T, n_head, D)
            v = v.reshape(B, T, n_head, D)
            cos, sin = _rope_tables(T, D)
            cos = cos[None, :, None, :]
            sin = sin[None, :, None, :]
            q = q * cos + _rotate_half(q) * sin
            k = k * cos + _rotate_half(k) * sin
            scores = jnp.einsum('bqhd,bkhd->bhqk', q, k) / jnp.sqrt(jnp.float32(D))
            causal = jnp.tril(jnp.ones((T, T), dtype=bool))
            scores = jnp.where(causal, scores, jnp.float32(-1e+30))
            p = jax.nn.softmax(scores, axis=-1)
            y = jnp.einsum('bhqk,bkhd->bqhd', p, v).reshape(B, T, C)
            return y @ proj_w

        def _moe(x, ln_w, ln_b, router_w, expert_wv, expert_proj):
            h = _layernorm(x, ln_w, ln_b)
            logits = h @ router_w
            expert_idx = jnp.argmax(logits, axis=-1)
            E = router_w.shape[-1]
            out = jnp.zeros_like(x)
            for e in range(E):
                gv = h @ expert_wv[e]
                gate_raw, value = jnp.split(gv, 2, axis=-1)
                y = gate_raw * jax.nn.sigmoid(gate_raw) * value @ expert_proj[e]
                out = out + jnp.where((expert_idx == e)[..., None], y, 0.0)
            return out
        C, H, E, B, T = (128, 16, 4, 4, 128)
        Dff = 4 * C
        key = jax.random.key(seed)
        ks = jax.random.split(key, 8)
        s = 0.02
        return {'x': jax.random.normal(ks[0], (B, T, C), dtype=jnp.float32), 'ln1_w': jnp.ones((C,), jnp.float32), 'ln1_b': jnp.zeros((C,), jnp.float32), 'ln2_w': jnp.ones((C,), jnp.float32), 'ln2_b': jnp.zeros((C,), jnp.float32), 'conv_w': jax.random.normal(ks[1], (C, 1, 3), dtype=jnp.float32) * 0.1, 'attn_w': jax.random.normal(ks[2], (C, 3 * C), dtype=jnp.float32) * s, 'proj_w': jax.random.normal(ks[3], (C, C), dtype=jnp.float32) * s, 'router_w': jax.random.normal(ks[4], (C, E), dtype=jnp.float32) * s, 'expert_wv': jax.random.normal(ks[5], (E, C, 2 * Dff), dtype=jnp.float32) * s, 'expert_proj': jax.random.normal(ks[6], (E, Dff, C), dtype=jnp.float32) * s}
    _L1_ffn_in = _L1_ffn_setup()
    _d = {'L0_attn_a_x': _L0_attn_a_in['x'], 'L0_attn_a_w_qkv': _L0_attn_a_in['w_qkv'], 'L0_attn_a_w_out': _L0_attn_a_in['w_out'], 'L0_attn_a_q_norm_w': _L0_attn_a_in['q_norm_w'], 'L0_attn_a_k_norm_w': _L0_attn_a_in['k_norm_w'], 'L0_attn_b_W_qk': _L0_attn_b_in['W_qk'], 'L0_attn_b_b_qk': _L0_attn_b_in['b_qk'], 'L0_attn_b_W_v': _L0_attn_b_in['W_v'], 'L0_attn_b_b_v': _L0_attn_b_in['b_v'], 'L0_attn_b_W_g': _L0_attn_b_in['W_g'], 'L0_attn_b_b_g': _L0_attn_b_in['b_g'], 'L0_attn_b_W_o': _L0_attn_b_in['W_o'], 'L0_attn_b_b_o': _L0_attn_b_in['b_o'], 'L0_ffn_Win': _L0_ffn_in['Win'], 'L0_ffn_bin_': _L0_ffn_in['bin_'], 'L0_ffn_W1': _L0_ffn_in['W1'], 'L0_ffn_b1': _L0_ffn_in['b1'], 'L0_ffn_W2': _L0_ffn_in['W2'], 'L0_ffn_b2': _L0_ffn_in['b2'], 'L0_ffn_Wout': _L0_ffn_in['Wout'], 'L0_ffn_bout': _L0_ffn_in['bout'], 'L1_attn_a_W_qkv': _L1_attn_a_in['W_qkv'], 'L1_attn_a_W_out': _L1_attn_a_in['W_out'], 'L1_attn_b_time_decay': _L1_attn_b_in['time_decay'], 'L1_attn_b_time_first': _L1_attn_b_in['time_first'], 'L1_attn_b_time_mix_k': _L1_attn_b_in['time_mix_k'], 'L1_attn_b_time_mix_v': _L1_attn_b_in['time_mix_v'], 'L1_attn_b_time_mix_r': _L1_attn_b_in['time_mix_r'], 'L1_attn_b_Wk': _L1_attn_b_in['Wk'], 'L1_attn_b_Wv': _L1_attn_b_in['Wv'], 'L1_attn_b_Wr': _L1_attn_b_in['Wr'], 'L1_attn_b_Wo': _L1_attn_b_in['Wo'], 'L1_ffn_ln1_w': _L1_ffn_in['ln1_w'], 'L1_ffn_ln1_b': _L1_ffn_in['ln1_b'], 'L1_ffn_ln2_w': _L1_ffn_in['ln2_w'], 'L1_ffn_ln2_b': _L1_ffn_in['ln2_b'], 'L1_ffn_conv_w': _L1_ffn_in['conv_w'], 'L1_ffn_attn_w': _L1_ffn_in['attn_w'], 'L1_ffn_proj_w': _L1_ffn_in['proj_w'], 'L1_ffn_router_w': _L1_ffn_in['router_w'], 'L1_ffn_expert_wv': _L1_ffn_in['expert_wv'], 'L1_ffn_expert_proj': _L1_ffn_in['expert_proj']}
    _x0 = _d['L0_attn_a_x']
    _d['L0_attn_a_x'] = jax.random.normal(jax.random.fold_in(jax.random.key(seed), 1), (1, 2048, 128), dtype=_x0.dtype)
    del _x0
    return _d

def reference(L0_attn_a_x, L0_attn_a_w_qkv, L0_attn_a_w_out, L0_attn_a_q_norm_w, L0_attn_a_k_norm_w, L0_attn_b_W_qk, L0_attn_b_b_qk, L0_attn_b_W_v, L0_attn_b_b_v, L0_attn_b_W_g, L0_attn_b_b_g, L0_attn_b_W_o, L0_attn_b_b_o, L0_ffn_Win, L0_ffn_bin_, L0_ffn_W1, L0_ffn_b1, L0_ffn_W2, L0_ffn_b2, L0_ffn_Wout, L0_ffn_bout, L1_attn_a_W_qkv, L1_attn_a_W_out, L1_attn_b_time_decay, L1_attn_b_time_first, L1_attn_b_time_mix_k, L1_attn_b_time_mix_v, L1_attn_b_time_mix_r, L1_attn_b_Wk, L1_attn_b_Wv, L1_attn_b_Wr, L1_attn_b_Wo, L1_ffn_ln1_w, L1_ffn_ln1_b, L1_ffn_ln2_w, L1_ffn_ln2_b, L1_ffn_conv_w, L1_ffn_attn_w, L1_ffn_proj_w, L1_ffn_router_w, L1_ffn_expert_wv, L1_ffn_expert_proj):

    def _L0_attn_a_ref(x, w_qkv, w_out, q_norm_w, k_norm_w):
        import jax, jax.numpy as jnp
        import numpy as np
        EPS = 1e-06
        ROPE_BASE = 10000.0

        def _rope(t):
            B, T, H, D = t.shape
            half = D // 2
            inv_freq = 1.0 / ROPE_BASE ** (jnp.arange(0, half, dtype=jnp.float32) * 2.0 / D)
            ang = jnp.arange(T, dtype=jnp.float32)[:, None] * inv_freq[None, :]
            cos = jnp.cos(ang)[None, :, None, :]
            sin = jnp.sin(ang)[None, :, None, :]
            x1, x2 = (t[..., :half], t[..., half:])
            return jnp.concatenate([x1 * cos - x2 * sin, x2 * cos + x1 * sin], axis=-1)

        def _rmsnorm(t, w):
            ms = jnp.mean(t * t, axis=-1, keepdims=True)
            return t * jax.lax.rsqrt(ms + EPS) * w
        B, T, C = x.shape
        H = 16
        D = C // H
        qkv = x @ w_qkv.T
        q, k, v = jnp.split(qkv, 3, axis=-1)
        q = q.reshape(B, T, H, D)
        k = k.reshape(B, T, H, D)
        v = v.reshape(B, T, H, D)
        q = _rmsnorm(_rope(q), q_norm_w)
        k = _rmsnorm(_rope(k), k_norm_w)
        scale = 1.0 / np.sqrt(D)
        attn = jnp.einsum('bqhd,bkhd->bhqk', q, k) * scale
        causal = jnp.tril(jnp.ones((T, T), dtype=bool))
        attn = jnp.where(causal[None, None], attn, -jnp.inf)
        attn = jax.nn.softmax(attn, axis=-1)
        out = jnp.einsum('bhqk,bkhd->bqhd', attn, v).reshape(B, T, C)
        return out @ w_out.T

    def _L0_attn_b_ref(x, W_qk, b_qk, W_v, b_v, W_g, b_g, W_o, b_o):
        import jax, jax.numpy as jnp
        import numpy as np
        B, T, C, H, VBD = (2, 256, 128, 16, 256)
        KD = C // H
        VD = VBD // H
        EPS = float(np.finfo(np.float32).eps)

        def _inner_mask(seq_len):
            gamma = jnp.log(1.0 - 2.0 ** (-5.0 - jnp.arange(H, dtype=jnp.float32)))
            idx = jnp.arange(seq_len, dtype=jnp.float32)
            diff = idx[:, None] - idx[None, :]
            causal = diff >= 0
            decay = jnp.where(causal, jnp.exp(gamma[:, None, None] * diff), 0.0)
            scale = jnp.sqrt(decay.sum(-1, keepdims=True))
            return decay / scale
        Bx, Tx, _ = x.shape
        qk = x @ W_qk + b_qk
        q, k = jnp.split(qk, 2, axis=-1)
        v = x @ W_v + b_v
        q = q.reshape(Bx, Tx, H, KD).transpose(0, 2, 1, 3)
        k = k.reshape(Bx, Tx, H, KD).transpose(0, 2, 1, 3)
        v = v.reshape(Bx, Tx, H, VD).transpose(0, 2, 1, 3)
        mask = _inner_mask(Tx)
        scores = jnp.einsum('bhtd,bhsd->bhts', q, k) * mask
        denom = jnp.clip(jnp.abs(scores).sum(-1, keepdims=True), 1.0, 50000.0)
        scores = scores / denom
        ret = jnp.einsum('bhts,bhsv->bthv', scores, v)
        ret = ret * jax.lax.rsqrt(jnp.mean(ret * ret, axis=-1, keepdims=True) + EPS)
        y = ret.reshape(Bx, Tx, H * VD)
        gated = (x @ W_g + b_g) * y
        return gated @ W_o + b_o

    def _L0_ffn_ref(x, Win, bin_, W1, b1, W2, b2, Wout, bout):
        import jax, jax.numpy as jnp
        import numpy as np
        D_MODEL = 128
        M = 64
        INNER = 16
        s = jnp.einsum('btd,dm->btm', x, Win) + bin_
        h = jax.nn.relu(s[..., None] * W1 + b1)
        g = jnp.einsum('btmh,mh->btm', h, W2) + b2
        out = jnp.einsum('btm,md->btd', g, Wout) + bout
        return out

    def _L1_attn_a_ref(x, W_qkv, W_out):
        import jax, jax.numpy as jnp
        import numpy as np
        B, L, E, H = (2, 512, 128, 16)
        D = E // H
        CHUNK = 32

        def _linear_attention(x, W_qkv, W_out):
            Bz, Lz, Ez = x.shape
            scale = D ** (-0.5)
            qkv = x @ W_qkv.T
            qkv = qkv.reshape(Bz, Lz, 3, H, D).transpose(2, 0, 3, 1, 4)
            q, k, v = (qkv[0], qkv[1], qkv[2])
            q = (jax.nn.elu(q) + 1.0) * scale
            k = jax.nn.elu(k) + 1.0
            nc = Lz // CHUNK

            def to_chunks(t):
                return t.reshape(Bz, H, nc, CHUNK, D).transpose(2, 0, 1, 3, 4)
            qc, kc, vc = (to_chunks(q), to_chunks(k), to_chunks(v))
            causal = jnp.tril(jnp.ones((CHUNK, CHUNK), dtype=x.dtype))

            def step(carry, inp):
                S, Z = carry
                qi, ki, vi = inp
                attn = jnp.einsum('bhld,bhmd->bhlm', qi, ki) * causal
                num = jnp.einsum('bhlm,bhme->bhle', attn, vi) + jnp.einsum('bhld,bhde->bhle', qi, S)
                den = attn.sum(-1) + jnp.einsum('bhld,bhd->bhl', qi, Z)
                S = S + jnp.einsum('bhmd,bhme->bhde', ki, vi)
                Z = Z + ki.sum(axis=2)
                return ((S, Z), (num, den))
            S0 = jnp.zeros((Bz, H, D, D), dtype=x.dtype)
            Z0 = jnp.zeros((Bz, H, D), dtype=x.dtype)
            _, (num, den) = jax.lax.scan(step, (S0, Z0), (qc, kc, vc))
            num = num.transpose(1, 2, 0, 3, 4).reshape(Bz, H, Lz, D)
            den = den.transpose(1, 2, 0, 3).reshape(Bz, H, Lz)
            den = jnp.maximum(den, 1e-06)
            out = num / den[..., None]
            out = out.transpose(0, 2, 1, 3).reshape(Bz, Lz, Ez)
            return out @ W_out.T
        return _linear_attention(x, W_qkv, W_out)

    def _L1_attn_b_ref(x, time_decay, time_first, time_mix_k, time_mix_v, time_mix_r, Wk, Wv, Wr, Wo):
        import jax, jax.numpy as jnp
        import numpy as np
        B, T, C = (8, 256, 128)
        NEG_INF = -1e+38

        def wkv(w, u, k, v):
            kt = jnp.swapaxes(k, 0, 1)
            vt = jnp.swapaxes(v, 0, 1)
            Bn, Cn = (k.shape[0], k.shape[2])
            aa = jnp.zeros((Bn, Cn), k.dtype)
            bb = jnp.zeros((Bn, Cn), k.dtype)
            pp = jnp.full((Bn, Cn), NEG_INF, k.dtype)

            def step(carry, kv):
                aa, bb, pp = carry
                kk, vv = kv
                ww = u + kk
                p = jnp.maximum(pp, ww)
                e1 = jnp.exp(pp - p)
                e2 = jnp.exp(ww - p)
                y = (e1 * aa + e2 * vv) / (e1 * bb + e2)
                ww2 = pp + w
                p2 = jnp.maximum(ww2, kk)
                e1 = jnp.exp(ww2 - p2)
                e2 = jnp.exp(kk - p2)
                return ((e1 * aa + e2 * vv, e1 * bb + e2, p2), y)
            _, y = jax.lax.scan(step, (aa, bb, pp), (kt, vt))
            return jnp.swapaxes(y, 0, 1)
        xx = jnp.pad(x, ((0, 0), (1, 0), (0, 0)))[:, :-1, :]
        xk = x * time_mix_k + xx * (1.0 - time_mix_k)
        xv = x * time_mix_v + xx * (1.0 - time_mix_v)
        xr = x * time_mix_r + xx * (1.0 - time_mix_r)
        k = jnp.einsum('btc,dc->btd', xk, Wk)
        v = jnp.einsum('btc,dc->btd', xv, Wv)
        r = jnp.einsum('btc,dc->btd', xr, Wr)
        w = -jnp.exp(time_decay)
        rwkv = jax.nn.sigmoid(r) * wkv(w, time_first, k, v)
        return jnp.einsum('btc,dc->btd', rwkv, Wo)

    def _L1_ffn_ref(x, ln1_w, ln1_b, ln2_w, ln2_b, conv_w, attn_w, proj_w, router_w, expert_wv, expert_proj):
        import jax, jax.numpy as jnp
        import numpy as np
        EPS = 1e-05

        def _layernorm(x, w, b):
            mu = jnp.mean(x, axis=-1, keepdims=True)
            var = jnp.mean((x - mu) ** 2, axis=-1, keepdims=True)
            return (x - mu) * jax.lax.rsqrt(var + EPS) * w + b

        def _rope_tables(T, D, base=10000.0):
            inv_freq = 1.0 / base ** (jnp.arange(0, D, 2, dtype=jnp.float32) / D)
            t = jnp.arange(T, dtype=jnp.float32)
            freqs = jnp.einsum('i,j->ij', t, inv_freq)
            emb = jnp.concatenate([freqs, freqs], axis=-1)
            return (jnp.cos(emb), jnp.sin(emb))

        def _rotate_half(x):
            x1, x2 = (x[..., :x.shape[-1] // 2], x[..., x.shape[-1] // 2:])
            return jnp.concatenate([-x2, x1], axis=-1)

        def _attn(x, ln_w, ln_b, conv_w, attn_w, proj_w, n_head):
            B, T, C = x.shape
            D = C // n_head
            h = _layernorm(x, ln_w, ln_b)
            hc = jnp.transpose(h, (0, 2, 1))
            hc = jnp.pad(hc, ((0, 0), (0, 0), (2, 0)))
            hc = jax.lax.conv_general_dilated(hc, conv_w, window_strides=(1,), padding='VALID', dimension_numbers=('NCH', 'OIH', 'NCH'), feature_group_count=C)
            h = jnp.transpose(hc, (0, 2, 1))
            qkv = h @ attn_w
            q, k, v = jnp.split(qkv, 3, axis=-1)
            q = q.reshape(B, T, n_head, D)
            k = k.reshape(B, T, n_head, D)
            v = v.reshape(B, T, n_head, D)
            cos, sin = _rope_tables(T, D)
            cos = cos[None, :, None, :]
            sin = sin[None, :, None, :]
            q = q * cos + _rotate_half(q) * sin
            k = k * cos + _rotate_half(k) * sin
            scores = jnp.einsum('bqhd,bkhd->bhqk', q, k) / jnp.sqrt(jnp.float32(D))
            causal = jnp.tril(jnp.ones((T, T), dtype=bool))
            scores = jnp.where(causal, scores, jnp.float32(-1e+30))
            p = jax.nn.softmax(scores, axis=-1)
            y = jnp.einsum('bhqk,bkhd->bqhd', p, v).reshape(B, T, C)
            return y @ proj_w

        def _moe(x, ln_w, ln_b, router_w, expert_wv, expert_proj):
            h = _layernorm(x, ln_w, ln_b)
            logits = h @ router_w
            expert_idx = jnp.argmax(logits, axis=-1)
            E = router_w.shape[-1]
            out = jnp.zeros_like(x)
            for e in range(E):
                gv = h @ expert_wv[e]
                gate_raw, value = jnp.split(gv, 2, axis=-1)
                y = gate_raw * jax.nn.sigmoid(gate_raw) * value @ expert_proj[e]
                out = out + jnp.where((expert_idx == e)[..., None], y, 0.0)
            return out
        n_head = 16
        x = x + _attn(x, ln1_w, ln1_b, conv_w, attn_w, proj_w, n_head)
        x = x + _moe(x, ln2_w, ln2_b, router_w, expert_wv, expert_proj)
        return x
    x = L0_attn_a_x
    x = x + _L0_attn_a_ref(_layernorm(x, axis=-1), L0_attn_a_w_qkv, L0_attn_a_w_out, L0_attn_a_q_norm_w, L0_attn_a_k_norm_w)
    x = x + _L0_ffn_ref(_layernorm(x, axis=-1), L0_ffn_Win, L0_ffn_bin_, L0_ffn_W1, L0_ffn_b1, L0_ffn_W2, L0_ffn_b2, L0_ffn_Wout, L0_ffn_bout)
    x = x + _L0_attn_b_ref(_layernorm(x, axis=-1), L0_attn_b_W_qk, L0_attn_b_b_qk, L0_attn_b_W_v, L0_attn_b_b_v, L0_attn_b_W_g, L0_attn_b_b_g, L0_attn_b_W_o, L0_attn_b_b_o)
    x = x + _L0_ffn_ref(_layernorm(x, axis=-1), L0_ffn_Win, L0_ffn_bin_, L0_ffn_W1, L0_ffn_b1, L0_ffn_W2, L0_ffn_b2, L0_ffn_Wout, L0_ffn_bout)
    x = x + _L1_attn_a_ref(_layernorm(x, axis=-1), L1_attn_a_W_qkv, L1_attn_a_W_out)
    x = x + _L1_ffn_ref(_layernorm(x, axis=-1), L1_ffn_ln1_w, L1_ffn_ln1_b, L1_ffn_ln2_w, L1_ffn_ln2_b, L1_ffn_conv_w, L1_ffn_attn_w, L1_ffn_proj_w, L1_ffn_router_w, L1_ffn_expert_wv, L1_ffn_expert_proj)
    x = x + _L1_attn_b_ref(_layernorm(x, axis=-1), L1_attn_b_time_decay, L1_attn_b_time_first, L1_attn_b_time_mix_k, L1_attn_b_time_mix_v, L1_attn_b_time_mix_r, L1_attn_b_Wk, L1_attn_b_Wv, L1_attn_b_Wr, L1_attn_b_Wo)
    x = x + _L1_ffn_ref(_layernorm(x, axis=-1), L1_ffn_ln1_w, L1_ffn_ln1_b, L1_ffn_ln2_w, L1_ffn_ln2_b, L1_ffn_conv_w, L1_ffn_attn_w, L1_ffn_proj_w, L1_ffn_router_w, L1_ffn_expert_wv, L1_ffn_expert_proj)
    return x

_drawn_inputs = setup_inputs


def setup_inputs(seed=0):
    import zlib

    import numpy as np

    out = dict(_drawn_inputs(seed))
    spreads = {'L0_attn_a_q_norm_w': (1.0, 0.6),
     'L0_attn_a_k_norm_w': (1.0, 0.6),
     'L0_attn_b_b_qk': (0.0, 0.1),
     'L0_attn_b_b_v': (0.0, 0.1),
     'L0_attn_b_b_g': (0.0, 0.274),
     'L0_attn_b_b_o': (0.0, 0.1),
     'L1_ffn_ln1_w': (1.0, 0.6),
     'L1_ffn_ln1_b': (0.0, 0.8),
     'L1_ffn_ln2_w': (1.0, 0.6),
     'L1_ffn_ln2_b': (0.0, 0.8)}
    factors = {'L0_ffn_bin_': 4.897,
     'L1_attn_a_W_qkv': 3.449,
     'L1_attn_a_W_out': 3.673,
     'L1_ffn_conv_w': 8.0,
     'L1_ffn_attn_w': 8.0,
     'L1_ffn_proj_w': 8.0,
     'L1_ffn_router_w': 6.521,
     'L1_ffn_expert_wv': 5.739,
     'L1_ffn_expert_proj': 5.713}
    for name, (base, spread) in spreads.items():
        noise = np.random.default_rng([zlib.crc32(name.encode()), seed]).standard_normal(out[name].shape)
        drawn = base * np.exp(spread * noise) if base else spread * noise
        out[name] = jnp.asarray(drawn.astype(out[name].dtype))
    for name, factor in factors.items():
        out[name] = (out[name] * factor).astype(out[name].dtype)
    return out
```

```python
import numpy as np
import concourse.bass as bass
from concourse import mybir
from contextlib import ExitStack

F32 = mybir.dt.float32
BF16 = mybir.dt.bfloat16
ACT = mybir.ActivationFunctionType
ALU = mybir.AluOpType
AX = mybir.AxisListType

T, C, H = 2048, 128, 16
P = 128
NT = T // P
D = C // H
BANK = 512
QC = BANK // P
NQ = T // BANK
NEG = -1e30
PARTS = 3
KROWS = PARTS * PARTS * D
SHIFT = 2
VD = 16
M0, INNER = 64, 16
E, DFF = 4, 512


class Counter:

    def __init__(self, sem):
        self.sem, self.sent = sem, 0

    def at(self, n):
        return n + self.sent if self.sent else n

    def done(self, n):
        self.sent += n


class Kernel:

    def __init__(self, nc, ctx):
        self.nc, self.ctx, self.counters, self.count = nc, ctx, {}, 0

    def counter(self, name):
        if name not in self.counters:
            self.counters[name] = Counter(self.ctx.enter_context(self.nc.semaphore(name)))
        return self.counters[name]

    def sb(self, name, shape, dtype=F32, ctx=None):
        self.count += 1
        return (ctx or self.ctx).enter_context(self.nc.sbuf_tensor(f"{name}_{self.count}", shape, dtype))

    def ps(self, name, shape, ctx, dtype=F32):
        self.count += 1
        return ctx.enter_context(self.nc.psum_tensor(f"{name}_{self.count}", shape, dtype))


class Chain:

    def __init__(self, eng, counter):
        self.eng, self.counter, self.n = eng, counter, 0

    def __call__(self, ins):
        self.n += 1
        ins.then_inc(self.counter.sem, 1)
        self.eng.wait_ge(self.counter.sem, self.counter.at(self.n))


def bcast(ap, axis, n):
    a = ap.unsqueeze(axis)
    shape = list(a.shape)
    shape[axis] = n
    return a.broadcast_to(shape)




def load_stage(k, d, w):
    nc = k.nc
    with ExitStack() as ctx:
        raw = k.sb("raw_w", [P, 12, C], F32, ctx)
        maskf = k.sb("mask_f32", [P, 3, P], F32, ctx)
        tp = k.ps("weight_t", [P, 3, BANK], ctx)
        loaded, turned, kept = k.counter("loaded"), k.counter("weights_turned"), k.counter("weights_kept")
        plain = [
            (w["X"][:], d["x"].rearrange("o (t p) c -> p (o t) c", p=P)),
            (raw[:, 0:3, :], d["L0_attn_a_w_qkv"].rearrange("(b p) c -> p b c", p=P)),
            (raw[:, 3, :], d["L0_attn_a_w_out"]),
            (raw[:, 4:7, :], d["L1_attn_a_W_qkv"].rearrange("(b p) c -> p b c", p=P)),
            (raw[:, 7, :], d["L1_attn_a_W_out"]),
            (raw[:, 8, :], d["L1_attn_b_Wk"]),
            (raw[:, 9, :], d["L1_attn_b_Wv"]),
            (raw[:, 10, :], d["L1_attn_b_Wr"]),
            (raw[:, 11, :], d["L1_attn_b_Wo"]),
            (maskf[:, 0, :], d["c_mask_qk"]),
            (maskf[:, 1, :], d["c_mask_kq"]),
            (maskf[:, 2, :], d["c_ident"]),
            (w["ident"][:], d["c_ident"]),
            (w["keep_kq"][:], d["c_keep_kq"]),
            (w["cos"][:], d["c_cos"]),
            (w["sin"][:], d["c_sin"]),
            (w["headmask"][:], d["c_headmask"]),
            (w["bd16"][:], d["c_bd16"]),
            (w["bd9"][:], d["c_bd9"]),
            (w["qdecay"][:], d["c_qdecay"]),
            (w["kdecay"][:], d["c_kdecay"]),
            (w["qn"][:], d["L0_attn_a_q_norm_w"].partition_broadcast(P)),
            (w["kn"][:], d["L0_attn_a_k_norm_w"].partition_broadcast(P)),
            (w["w_qkv_r"][:, 0:2 * C], d["L0_attn_b_W_qk"]),
            (w["w_qkv_r"][:, 2 * C:], d["L0_attn_b_W_v"]),
            (w["b_qkv_r"][:, 0:2 * C], d["L0_attn_b_b_qk"].partition_broadcast(P)),
            (w["b_qkv_r"][:, 2 * C:], d["L0_attn_b_b_v"].partition_broadcast(P)),
            (w["w_g"][:], d["L0_attn_b_W_g"]),
            (w["b_g"][:], d["L0_attn_b_b_g"].partition_broadcast(P)),
            (w["w_o_r"][:], d["L0_attn_b_W_o"].rearrange("(b p) c -> p b c", p=P)),
            (w["b_o"][:], d["L0_attn_b_b_o"].partition_broadcast(P)),
            (w["Win"][:], d["L0_ffn_Win"]),
            (w["bout"][:], d["L0_ffn_bout"].partition_broadcast(P)),
            (w["mix"][:, 0:1], d["L1_attn_b_time_mix_k"].rearrange("a b c -> c (a b)")),
            (w["mix"][:, 1:2], d["L1_attn_b_time_mix_v"].rearrange("a b c -> c (a b)")),
            (w["mix"][:, 2:3], d["L1_attn_b_time_mix_r"].rearrange("a b c -> c (a b)")),
            (w["decay"][:], d["L1_attn_b_time_decay"].rearrange("(c o) -> c o", o=1)),
            (w["first"][:], d["L1_attn_b_time_first"].rearrange("(c o) -> c o", o=1)),
            (w["ln1_w"][:], d["L1_ffn_ln1_w"].partition_broadcast(P)),
            (w["ln1_b"][:], d["L1_ffn_ln1_b"].partition_broadcast(P)),
            (w["ln2_w"][:], d["L1_ffn_ln2_w"].partition_broadcast(P)),
            (w["ln2_b"][:], d["L1_ffn_ln2_b"].partition_broadcast(P)),
            (w["conv_w"][:], d["L1_ffn_conv_w"].rearrange("c o j -> c (o j)")),
            (w["attn_w"][:], d["L1_ffn_attn_w"]),
            (w["proj_w"][:], d["L1_ffn_proj_w"]),
            (w["router"][:], d["L1_ffn_router_w"]),
            (w["expert_wv"][:], d["L1_ffn_expert_wv"].rearrange("e c f -> c e f")),
            (w["expert_proj"][:], d["L1_ffn_expert_proj"].rearrange("e (b p) c -> p e b c", p=P)),
        ]
        for half in range(2):
            at = slice(half * M0, half * M0 + M0)
            plain += [
                (w["bin"][at, :], d["L0_ffn_bin_"].rearrange("(m o) -> m o", o=1)),
                (w["W1"][at, :], d["L0_ffn_W1"]),
                (w["b1"][at, :], d["L0_ffn_b1"]),
                (w["W2"][at, :], d["L0_ffn_W2"]),
                (w["b2"][at, :], d["L0_ffn_b2"].rearrange("(m o) -> m o", o=1)),
                (w["Wout"][at, :], d["L0_ffn_Wout"]),
            ]
        with nc.Block() as block:

            @block.sync
            def _(sp):
                with nc.allow_non_contiguous_dma(reason="per-channel vectors"):
                    for dst, src in plain:
                        sp.dma_start(dst, src).then_inc(loaded.sem, 16)
                sp.wait_ge(loaded.sem, loaded.at(16 * len(plain)))

            @block.tensor
            def _(pe):
                pe.wait_ge(loaded.sem, loaded.at(16 * len(plain)))
                for b in range(12):
                    ins = nc.tensor.transpose(tp[:, b // 4, (b % 4) * P:(b % 4 + 1) * P], raw[:, b, :], w["ident"][:])
                    if b % 4 == 3:
                        ins.then_inc(turned.sem, 1)

            @block.scalar
            def _(act):
                for n in range(3):
                    act.wait_ge(turned.sem, turned.at(n + 1))
                    nc.scalar.copy(w["wT"][:, 4 * n:4 * n + 4, :].rearrange("p a b -> p (a b)"), tp[:, n, :]).then_inc(kept.sem, 1)

            @block.vector
            def _(dve):
                dve.wait_ge(loaded.sem, loaded.at(16 * len(plain)))
                nc.vector.tensor_copy(w["mask_qk"][:], maskf[:, 0, :]).then_inc(kept.sem, 1)
                nc.vector.tensor_copy(w["mask_kq"][:], maskf[:, 1, :]).then_inc(kept.sem, 1)
                nc.vector.tensor_copy(w["ident16"][:], maskf[:, 2, :]).then_inc(kept.sem, 1)
                nc.vector.memset(w["ones"][:], 1.0).then_inc(kept.sem, 1)

        loaded.done(16 * len(plain))
        turned.done(3)
        kept.done(7)




def layer_norm(k, src, dst, ident, dst_t=None, affine=None, eps=1e-5):
    nc = k.nc
    with ExitStack() as ctx:
        stats = k.sb("ln_stats", [P, NT, 6], F32, ctx)
        mv = k.sb("ln_mean_var", [P, NT, 2], F32, ctx)
        std = k.sb("ln_std", [P, NT], F32, ctx)
        rstd = k.sb("ln_rstd", [P, NT], F32, ctx)
        tp = k.ps("ln_t", [P, NQ, BANK], ctx)
        step, var_ready, std_ready = k.counter("ln_step"), k.counter("ln_var"), k.counter("ln_std")
        rows, turned, kept = k.counter("ln_rows"), k.counter("ln_turned"), k.counter("ln_kept")
        with nc.Block() as block:

            @block.vector
            def _(dve):
                chain = Chain(dve, step)
                for i in range(NT):
                    ins = nc.vector.bn_stats(stats[:, i, :], src[:, i, :])
                chain(ins)
                for i in range(NT):
                    ins = nc.vector.bn_aggr(mv[:, i, :], stats[:, i, :])
                chain(ins)
                nc.vector.tensor_scalar(std[:], mv[:, :, 1], eps, None, ALU.add).then_inc(var_ready.sem, 1)
                dve.wait_ge(std_ready.sem, std_ready.at(1))
                chain(nc.vector.reciprocal(rstd[:], std[:]))
                for q in range(NQ):
                    for i in range(QC * q, QC * q + QC):
                        ins = nc.vector.tensor_scalar(dst[:, i, :], src[:, i, :], mv[:, i, 0:1], rstd[:, i:i + 1],
                                                      ALU.subtract, ALU.mult)
                    if affine is None:
                        ins.then_inc(rows.sem, 1)
                    else:
                        chain(ins)
                        part = dst[:, QC * q:QC * q + QC, :]
                        chain(nc.vector.tensor_tensor(part, part, bcast(affine[0][:], 1, QC), ALU.mult))
                        nc.vector.tensor_tensor(part, part, bcast(affine[1][:], 1, QC), ALU.add).then_inc(rows.sem, 1)

            @block.scalar
            def _(act):
                act.wait_ge(var_ready.sem, var_ready.at(1))
                nc.scalar.sqrt(std[:], std[:]).then_inc(std_ready.sem, 1)
                if dst_t is not None:
                    for q in range(NQ):
                        act.wait_ge(turned.sem, turned.at(q + 1))
                        nc.scalar.copy(dst_t[:, q * BANK:(q + 1) * BANK], tp[:, q, :]).then_inc(kept.sem, 1)

            @block.tensor
            def _(pe):
                if dst_t is not None:
                    for q in range(NQ):
                        pe.wait_ge(rows.sem, rows.at(q + 1))
                        for i in range(QC):
                            ins = nc.tensor.transpose(tp[:, q, i * P:(i + 1) * P], dst[:, QC * q + i, :], ident[:])
                        ins.then_inc(turned.sem, 1)

        step.done(2 + 1 + (0 if affine is None else 2 * NQ))
        var_ready.done(1)
        std_ready.done(1)
        rows.done(NQ)
        if dst_t is not None:
            turned.done(NQ)
            kept.done(NQ)


def transpose_stage(k, jobs, ident):
    nc = k.nc
    with ExitStack() as ctx:
        tp = k.ps("turn", [P, 4, BANK], ctx)
        turned, kept = k.counter("turned"), k.counter("turn_kept")
        units = [(src, dst, q) for src, dst in jobs for q in range(NQ)]
        with nc.Block() as block:

            @block.tensor
            def _(pe):
                for n, (src, dst, q) in enumerate(units):
                    if n >= 4:
                        pe.wait_ge(kept.sem, kept.at(n - 3))
                    for i in range(QC):
                        ins = nc.tensor.transpose(tp[:, n % 4, i * P:(i + 1) * P], src[:, QC * q + i, :], ident[:])
                    ins.then_inc(turned.sem, 1)

            @block.scalar
            def _(act):
                for n, (src, dst, q) in enumerate(units):
                    act.wait_ge(turned.sem, turned.at(n + 1))
                    nc.scalar.copy(dst[:, q * BANK:(q + 1) * BANK], tp[:, n % 4, :]).then_inc(kept.sem, 1)

        turned.done(len(units))
        kept.done(len(units))


def project_stage(k, jobs, add_to=False):
    nc = k.nc
    with ExitStack() as ctx:
        out = k.ps("project", [P, 8, BANK], ctx)
        ready, kept = k.counter("projected"), k.counter("project_kept")
        units = [(job, i) for i in range(NT) for job in jobs]
        with nc.Block() as block:

            @block.tensor
            def _(pe):
                for n, ((chunks, dst, bias), i) in enumerate(units):
                    if n >= 8:
                        pe.wait_ge(kept.sem, kept.at(n - 7))
                    width = chunks[0][1].shape[-1]
                    for c, (x_t, wgt) in enumerate(chunks):
                        ins = nc.tensor.matmul(out[:, n % 8, 0:width], x_t[:, i * P:(i + 1) * P], wgt,
                                               start=(c == 0), stop=(c == len(chunks) - 1))
                    ins.then_inc(ready.sem, 1)

            @block.vector
            def _(dve):
                for n, ((chunks, dst, bias), i) in enumerate(units):
                    width = chunks[0][1].shape[-1]
                    dve.wait_ge(ready.sem, ready.at(n + 1))
                    o = out[:, n % 8, 0:width]
                    if add_to:
                        ins = nc.vector.tensor_tensor(dst[:, i, :], o, dst[:, i, :], ALU.add)
                    elif bias is not None:
                        ins = nc.vector.tensor_tensor(dst[:, i, :], o, bias, ALU.add)
                    else:
                        ins = nc.vector.tensor_copy(dst[:, i, :], o)
                    ins.then_inc(kept.sem, 1)

        ready.done(len(units))
        kept.done(len(units))


def rope_stage(k, w, qkv, norm):
    nc = k.nc
    half = D // 2
    with ExitStack() as ctx:
        names = ("q", "k")
        work = [k.sb(f"rope_{n}", [P, NT, C], F32, ctx) for n in names]
        ms = [k.sb(f"rms_{n}", [P, NT * H], F32, ctx) for n in names]
        done = [k.counter(f"rope_{n}_step") for n in names]
        ms_ready, std_ready = k.counter("rms_ready"), k.counter("rms_std")
        counts = [0, 0]

        def rotate(eng, s):
            chain = Chain(eng, done[s])
            x = qkv[:, :, s * C:(s + 1) * C]
            xs = x.rearrange("p t (h d) -> p t h d", d=D)
            ws = work[s][:].rearrange("p t (h d) -> p t h d", d=D)
            eng.tensor_tensor(ws[:, :, :, 0:half], xs[:, :, :, half:], bcast(w["sin"][:, :, 0:half], 2, H), ALU.mult)
            chain(eng.tensor_tensor(ws[:, :, :, half:], xs[:, :, :, 0:half], bcast(w["sin"][:, :, half:], 2, H), ALU.mult))
            chain(eng.tensor_tensor(xs, xs, bcast(w["cos"][:], 2, H), ALU.mult))
            chain(eng.tensor_tensor(x, x, work[s][:], ALU.add))
            return chain

        with nc.Block() as block:

            @block.vector
            def _(dve):
                chain = rotate(nc.vector, 0)
                if norm:
                    for s in range(2):
                        if s == 1:
                            dve.wait_ge(done[1].sem, done[1].at(4))
                        else:
                            chain(nc.vector.tensor_tensor(work[0][:], qkv[:, :, 0:C], qkv[:, :, 0:C], ALU.mult))
                        chain(nc.vector.tensor_reduce(ms[s][:], work[s][:].rearrange("p t (h d) -> p (t h) d", d=D), AX.X, ALU.add))
                        nc.vector.tensor_scalar(ms[s][:], ms[s][:], 1.0 / D, 1e-6, ALU.mult, ALU.add).then_inc(ms_ready.sem, 1)
                    for s in range(2):
                        dve.wait_ge(std_ready.sem, std_ready.at(s + 1))
                        chain(nc.vector.reciprocal(ms[s][:], ms[s][:]))
                        xs = qkv[:, :, s * C:(s + 1) * C].rearrange("p t (h d) -> p t h d", d=D)
                        r = bcast(ms[s][:].rearrange("p (t h) -> p t h", h=H), 3, D)
                        chain(nc.vector.tensor_tensor(xs, xs, r, ALU.mult))
                        xt = qkv[:, :, s * C:(s + 1) * C].rearrange("p t (h d) -> p t h d", d=D)
                        for i in range(NT):
                            ins = nc.vector.tensor_tensor(xt[:, i], xt[:, i], bcast(w["qn" if s == 0 else "kn"][:], 1, H), ALU.mult)
                        chain(ins)
                counts[0] = chain.n

            @block.gpsimd
            def _(pool):
                chain = rotate(nc.gpsimd, 1)
                if norm:
                    chain(nc.gpsimd.tensor_tensor(work[1][:], qkv[:, :, C:2 * C], qkv[:, :, C:2 * C], ALU.mult))
                counts[1] = chain.n

            if norm:
                @block.scalar
                def _(act):
                    for s in range(2):
                        act.wait_ge(ms_ready.sem, ms_ready.at(s + 1))
                        nc.scalar.sqrt(ms[s][:], ms[s][:]).then_inc(std_ready.sem, 1)

        done[0].done(counts[0])
        done[1].done(counts[1])
        if norm:
            ms_ready.done(2)
            std_ready.done(2)




def split_stage(k, w, qkv, parts_dram):
    nc = k.nc
    with ExitStack() as ctx:
        parts = [k.sb(f"parts_{n}", [P, PARTS, NT, C], BF16, ctx) for n in "qk"]
        rest = [k.sb(f"rest_{n}", [P, NT, C], F32, ctx) for n in "qk"]
        turned_sb = [k.sb(f"parts_t_{n}", [P, PARTS, T], BF16, ctx) for n in "qk"]
        tp = k.ps("parts_turn", [P, 4, 2 * BANK], ctx, BF16)
        rounded = [k.counter(f"part_rounded_{n}") for n in "qk"]
        subbed = [k.counter(f"part_rest_{n}") for n in "qk"]
        turned, kept, stored = k.counter("parts_turned"), k.counter("parts_kept"), k.counter("parts_stored")
        half = 2 * QC
        units = [(s, a, u) for a in range(PARTS) for s in range(2) for u in range(NT // half)]
        with nc.Block() as block:

            def subtract(eng, s):
                x = qkv[:, :, s * C:(s + 1) * C]
                eng.wait_ge(rounded[s].sem, rounded[s].at(1))
                eng.tensor_tensor(rest[s][:], x, parts[s][:, 0], ALU.subtract).then_inc(subbed[s].sem, 1)
                eng.wait_ge(rounded[s].sem, rounded[s].at(2))
                eng.tensor_tensor(parts[s][:, 2], rest[s][:], parts[s][:, 1], ALU.subtract).then_inc(subbed[s].sem, 1)

            @block.vector
            def _(dve):
                subtract(nc.vector, 0)

            @block.gpsimd
            def _(pool):
                subtract(nc.gpsimd, 1)

            @block.scalar
            def _(act):
                for s in range(2):
                    nc.scalar.copy(parts[s][:, 0], qkv[:, :, s * C:(s + 1) * C]).then_inc(rounded[s].sem, 1)
                for s in range(2):
                    act.wait_ge(subbed[s].sem, subbed[s].at(1))
                    nc.scalar.copy(parts[s][:, 1], rest[s][:]).then_inc(rounded[s].sem, 1)
                for n, (s, a, u) in enumerate(units):
                    act.wait_ge(turned.sem, turned.at(n + 1))
                    nc.scalar.copy(turned_sb[s][:, a, u * 2 * BANK:(u + 1) * 2 * BANK], tp[:, n % 4, :]).then_inc(kept.sem, 1)

            @block.tensor
            def _(pe):
                for n, (s, a, u) in enumerate(units):
                    if a < 2:
                        pe.wait_ge(rounded[s].sem, rounded[s].at(a + 1))
                    else:
                        pe.wait_ge(subbed[s].sem, subbed[s].at(2))
                    if n >= 4:
                        pe.wait_ge(kept.sem, kept.at(n - 3))
                    for i in range(half):
                        ins = nc.tensor.transpose(tp[:, n % 4, i * P:(i + 1) * P], parts[s][:, a, u * half + i, :], w["ident16"][:])
                    ins.then_inc(turned.sem, 1)

            @block.sync
            def _(sp):
                for n, (s, a, u) in enumerate(units):
                    if u == NT // half - 1:
                        sp.wait_ge(kept.sem, kept.at(n + 1))
                        sp.dma_start(parts_dram[s][a], turned_sb[s][:, a, :]).then_inc(stored.sem, 16)
                sp.wait_ge(stored.sem, stored.at(16 * 2 * PARTS))

        for s in range(2):
            rounded[s].done(2)
            subbed[s].done(2)
        turned.done(len(units))
        kept.done(len(units))
        stored.done(16 * 2 * PARTS)


def attention_stage(k, w, v, parts_dram, scale, y):
    nc = k.nc
    MAXU = [(i, c) for i in range(NT) for c in range(i // QC + 1)]
    EXPU = []
    for j in range(NQ):
        for u in range(2 * j):
            EXPU.append((j, [(2 * u, 0), (2 * u + 1, 0)]))
        EXPU.append((j, [(QC * j, 0), (QC * j + 1, 1)]))
        EXPU.append((j, [(QC * j + 2, 2), (QC * j + 3, 3)]))
    NM, NE = len(MAXU), len(EXPU)
    STATU = NM + 2
    PRE = 2 * NM + 1
    RING, PSLOTS = 3, 4
    assert STATU % RING == 0 and NE % PSLOTS == 0 and NE % 2 == 0
    M_AT = {e: (2 * e, 2 * e + 2) for e in range(NE)}
    SHIFT_AT = 2
    LOOPED = H - 2
    TAIL = PRE + LOOPED * STATU
    counts = []
    with ExitStack() as ctx:
        qm = k.sb("q_max", [P, 2, T], BF16, ctx)
        km = k.sb("k_max", [P, 2, T], BF16, ctx)
        qe = k.sb("q_exp", [P, 2, T], BF16, ctx)
        ke = k.sb("k_exp", [P, 2, T], BF16, ctx)
        probs = k.sb("probs", [P, PSLOTS, 2 * BANK], F32, ctx)
        vh = k.sb("v_head", [P, 2, NT, 32], F32, ctx)
        mpart = k.sb("max_part", [P, 2, NT, NQ], F32, ctx)
        mx = k.sb("row_max", [P, 2, NT], F32, ctx)
        mxb = k.sb("row_max_parts", [P, 2, SHIFT * NT], BF16, ctx)
        mxt = k.sb("row_max_turned", [SHIFT * NT, 2, P], BF16, ctx)
        ot = k.sb("out_turned", [P, 2, BANK], F32, ctx)
        rden = k.sb("inv_denominator", [P, 2, NT], F32, ctx)
        ring = [k.ps(f"stat{n}", [P, BANK], ctx) for n in range(RING)]
        sc = [k.ps(f"score{n}", [P, 2 * BANK], ctx) for n in range(2)]
        acc = k.ps("pv", [P, BANK], ctx)

        cleared = k.counter("attn_cleared")
        m_loaded = [k.counter(f"max_rows_loaded{n}") for n in range(2)]
        e_loaded = [k.counter(f"exp_rows_loaded{n}") for n in range(2)]
        shift_in = [k.counter(f"shift_rows_loaded{n}") for n in range(2)]
        stat_full, stat_used = k.counter("stat_bank_full"), k.counter("stat_bank_used")
        max_step, max_ready = k.counter("max_step"), k.counter("row_max_ready")
        scored, expd, pv_done = k.counter("scores_ready"), k.counter("probs_ready"), k.counter("pv_done")
        out_copied, v_ready = k.counter("pv_copied_out"), k.counter("v_head_ready")
        q_rows, k_rows = (parts_dram[s].rearrange("a (h d) t -> h a d t", d=D) for s in range(2))

        def load_rows(sp, qt, kt, par, h, loaded):
            for a in range(PARTS):
                at = slice(a * PARTS * D, (a + 1) * PARTS * D)
                for b in range(PARTS):
                    r = a * PARTS * D + b * D
                    sp.dma_start(qt[r:r + D, par, :], q_rows[h, a]).then_inc(loaded.sem, 16)
                sp.dma_start(kt[at, par, :], k_rows[h]).then_inc(loaded.sem, 16)

        NL = (PARTS + 1) * PARTS * 16

        with nc.Block() as block:

            @block.sync
            def _(sp):
                def load_max(h, par):
                    load_rows(sp, qm, km, par, h, m_loaded[par])

                def load_exp(h, par, prev):
                    if prev is not None:
                        sp.wait_ge(scored.sem, scored.at(NE * prev + NE))
                    load_rows(sp, qe, ke, par, h, e_loaded[par])

                def load_shift(h, par, unit):
                    sp.wait_ge(stat_used.sem, stat_used.at(unit))
                    for n in range(SHIFT):
                        r = KROWS + n
                        sp.dma_start(qe[r:r + 1, par, :].rearrange("o (i q) -> o i q", q=P),
                                     mxt[n * NT:(n + 1) * NT, par, :]).then_inc(shift_in[par].sem, 16)

                sp.wait_ge(cleared.sem, cleared.at(1))
                load_max(0, 0)
                load_max(1, 1)
                load_exp(0, 0, None)
                sp.wait_ge(stat_full.sem, stat_full.at(NM))
                load_max(2, 0)
                load_shift(0, 0, NM + 1)

                def body(h, par, max_load=True, prev=True, shift_at=2 * SHIFT_AT):
                    nxt = 1 - par
                    if max_load:
                        if isinstance(h, int) and h == 0:
                            sp.wait_ge(stat_full.sem, stat_full.at(PRE))
                        else:
                            sp.wait_ge(stat_full.sem, stat_full.at(h * STATU + (PRE + NM + 1 - STATU)))
                        load_max(h + 3, nxt)
                    load_exp(h + 1, nxt, h - 1 if prev else None)
                    load_shift(h + 1, nxt, h * STATU + (PRE + shift_at + 1))

                body(0, 0, prev=False)
                body(1, 1)
                with sp.Fori(1, 6) as i:
                    for par in range(2):
                        body(2 * i + par, par)
                body(12, 0)
                body(13, 1, max_load=False)
                body(14, 0, max_load=False, shift_at=0)

            @block.gpsimd
            def _(pool):
                nc.gpsimd.memset(ke[64:P, :, :], -1.0).then_inc(cleared.sem, 1)
                pool.wait_ge(cleared.sem, cleared.at(1))
                nc.gpsimd.memset(vh[:], 0.0).then_inc(v_ready.sem, 1)
                pool.wait_ge(v_ready.sem, v_ready.at(1))
                nc.gpsimd.memset(vh[:, :, :, D:D + 1], 1.0).then_inc(v_ready.sem, 1)
                pool.wait_ge(v_ready.sem, v_ready.at(2))

                def gather(h, par):
                    nc.gpsimd.tensor_copy(vh[:, par, :, 0:D], v[:, :, bass.ds(2 * C + h * D, D)]).then_inc(v_ready.sem, 1)

                gather(0, 0)
                gather(1, 1)
                with pool.Fori(1, H // 2) as i:
                    for par in range(2):
                        h = 2 * i + par
                        pool.wait_ge(pv_done.sem, pv_done.at(NE * h - NE))
                        gather(h, par)

            @block.scalar
            def _(act):
                def body(h, par, first=False, first_two=False):
                    for e, (j, tiles) in enumerate(EXPU):
                        n = NE * h + e
                        act.wait_ge(scored.sem, scored.at(n + 1))
                        if not first or e >= PSLOTS:
                            act.wait_ge(pv_done.sem, pv_done.at(n + 1 - PSLOTS))
                        width = sum(BANK - f * P for _, f in tiles)
                        nc.scalar.activation(probs[:, e % PSLOTS, 0:width], sc[e % 2][:, 0:width], ACT.Exp,
                                             scale=scale).then_inc(expd.sem, 1)
                    act.wait_ge(pv_done.sem, pv_done.at(NE * h + NE))
                    if not first_two:
                        act.wait_ge(stat_full.sem, stat_full.at(h * STATU + (PRE - STATU)))
                    nc.scalar.copy(ot[:, par, :], acc[:]).then_inc(out_copied.sem, 1)

                body(0, 0, first=True, first_two=True)
                body(1, 1, first_two=True)
                with act.Fori(1, H // 2) as i:
                    for par in range(2):
                        body(2 * i + par, par)

            @block.tensor
            def _(pe):
                def max_unit(n, unit, par):
                    i, c = MAXU[unit]
                    width = BANK if c < i // QC else (i % QC + 1) * P
                    out = ring[n % RING]
                    last = nc.tensor.matmul(out[:, 0:width], qm[0:KROWS, par, i * P:(i + 1) * P],
                                            km[0:KROWS, par, c * BANK:c * BANK + width], start=True, stop=c < i // QC)
                    if c == i // QC:
                        last = nc.tensor.matmul(out[:, width - P:width], w["ident16"][:], w["mask_qk"][:], start=False, stop=True)
                    last.then_inc(stat_full.sem, 1)

                def shift_unit(n, par):
                    out = ring[n % RING]
                    nc.tensor.transpose(out[0:SHIFT * NT, 0:P // 2].bitcast(BF16), mxb[:, par, :], w["ident16"][:]).then_inc(stat_full.sem, 1)

                def out_unit(n, par):
                    for j in range(NQ):
                        last = nc.tensor.transpose(ring[n % RING][:, j * P:(j + 1) * P], ot[:, par, j * P:(j + 1) * P], w["ident"][:])
                    last.then_inc(stat_full.sem, 1)

                def scores(e, par):
                    j, tiles = EXPU[e]
                    at = 0
                    for kt, f in tiles:
                        width = BANK - f * P
                        out = sc[e % 2][:, at:at + width]
                        diag = kt >= QC * j
                        last = nc.tensor.matmul(out, ke[0:KROWS + SHIFT, par, kt * P:(kt + 1) * P],
                                                qe[0:KROWS + SHIFT, par, j * BANK + f * P:(j + 1) * BANK],
                                                start=True, stop=not diag)
                        if diag:
                            last = nc.tensor.matmul(out[:, 0:P], w["ident16"][:], w["mask_kq"][:], start=False, stop=True)
                        at += width
                    last.then_inc(scored.sem, 1)

                def pv(e, par):
                    j, tiles = EXPU[e]
                    at = 0
                    for kt, f in tiles:
                        for c in range(f, QC):
                            last = nc.tensor.matmul(acc[32 * c:32 * c + 32, j * P:(j + 1) * P], vh[:, par, kt, :],
                                                    probs[:, e % PSLOTS, at:at + P], start=kt == 0, stop=kt == QC * j + c,
                                                    tile_position=(0, 32 * c))
                            at += P
                    last.then_inc(pv_done.sem, 1)

                pe.wait_ge(cleared.sem, cleared.at(1))
                pe.wait_ge(m_loaded[0].sem, m_loaded[0].at(NL))
                n = 0
                for u in range(NM):
                    if n >= RING:
                        pe.wait_ge(stat_used.sem, stat_used.at(n + 1 - RING))
                    max_unit(n, u, 0)
                    n += 1
                pe.wait_ge(max_ready.sem, max_ready.at(1))
                pe.wait_ge(stat_used.sem, stat_used.at(n + 1 - RING))
                shift_unit(n, 0)
                n += 1
                pe.wait_ge(m_loaded[1].sem, m_loaded[1].at(NL))
                for u in range(NM):
                    pe.wait_ge(stat_used.sem, stat_used.at(n + 1 - RING))
                    max_unit(n, u, 1)
                    n += 1
                assert n == PRE
                pe.wait_ge(e_loaded[0].sem, e_loaded[0].at(NL))
                pe.wait_ge(shift_in[0].sem, shift_in[0].at(SHIFT * 16))
                scores(0, 0)
                scores(1, 0)

                def body(h, turn, par, base, ring_at, maxes=True, more=True):
                    nxt = 1 - par
                    n = 0

                    def free_bank():
                        pe.wait_ge(stat_used.sem, stat_used.at(base + (n + 1 - RING)))

                    pe.wait_ge(v_ready.sem, v_ready.at(h + 3))
                    if maxes:
                        pe.wait_ge(m_loaded[par].sem, m_loaded[par].at(turn * NL + 2 * NL))
                    for e in range(NE):
                        pe.wait_ge(expd.sem, expd.at(h * NE + (e + 1)))
                        if e + 2 < NE:
                            scores(e + 2, par)
                        elif more:
                            if e + 2 == NE:
                                pe.wait_ge(e_loaded[nxt].sem, e_loaded[nxt].at(turn * NL + (1 + par) * NL))
                                pe.wait_ge(shift_in[nxt].sem, shift_in[nxt].at(turn * (SHIFT * 16) + (1 + par) * SHIFT * 16))
                            scores(e + 2 - NE, nxt)
                        pv(e, par)
                        if e == SHIFT_AT and more:
                            pe.wait_ge(max_ready.sem, max_ready.at(h + 2))
                            free_bank()
                            shift_unit(ring_at + n, nxt)
                            n += 1
                        if maxes:
                            for u in range(*M_AT[e]):
                                free_bank()
                                max_unit(ring_at + n, u, par)
                                n += 1
                    pe.wait_ge(out_copied.sem, out_copied.at(h + 1))
                    free_bank()
                    out_unit(ring_at + n, par)

                with pe.Fori(0, LOOPED // 2) as i:
                    for par in range(2):
                        body(2 * i + par, i, par, i * (2 * STATU) + (PRE + par * STATU), PRE)
                body(H - 2, H // 2 - 1, 0, TAIL, TAIL, maxes=False)
                body(H - 1, H // 2 - 1, 1, TAIL + 2, TAIL + 2, maxes=False, more=False)

            @block.vector
            def _(dve):
                chain = Chain(dve, max_step)

                def max_unit(n, at, unit, par):
                    i, c = MAXU[unit]
                    width = BANK if c < i // QC else (i % QC + 1) * P
                    dve.wait_ge(stat_full.sem, stat_full.at(n + 1))
                    nc.vector.reduce_max(mpart[:, par, i, c:c + 1], ring[at % RING][:, 0:width], AX.X).then_inc(stat_used.sem, 1)

                def row_max(n, par, turn):
                    dve.wait_ge(stat_used.sem, stat_used.at(n))
                    step(nc.vector.tensor_reduce(mx[:, par, :], mpart[:, par], AX.X, ALU.max))
                    step(nc.vector.tensor_copy(mxb[:, par, 0:NT], mx[:, par, :]))
                    nc.vector.tensor_tensor(mxb[:, par, NT:], mx[:, par, :], mxb[:, par, 0:NT], ALU.subtract).then_inc(max_ready.sem, 1)

                steps = [0, 0]

                def step(ins):
                    steps[1] += 1
                    ins.then_inc(max_step.sem, 1)
                    dve.wait_ge(max_step.sem, max_step.at(steps[0] + steps[1]))

                def shift_unit(n, at, par, earlier):
                    if earlier is not None:
                        dve.wait_ge(shift_in[par].sem, shift_in[par].at(earlier))
                    dve.wait_ge(stat_full.sem, stat_full.at(n + 1))
                    nc.vector.tensor_copy(mxt[:, par, :], ring[at % RING][0:SHIFT * NT, 0:P // 2].bitcast(BF16)).then_inc(stat_used.sem, 1)

                def out_unit(n, at, h, par):
                    dve.wait_ge(stat_full.sem, stat_full.at(n + 1))
                    o = ring[at % RING][:].rearrange("p (t x) -> p t x", x=32)
                    step(nc.vector.reciprocal(rden[:, par, :], o[:, :, D]))
                    nc.vector.tensor_tensor(y[:, :, bass.ds(h * D, D)], o[:, :, 0:D], bcast(rden[:, par, :], 2, D),
                                            ALU.mult).then_inc(stat_used.sem, 1)

                nc.vector.memset(mpart[:], -3e38).then_inc(max_step.sem, 1)
                steps[1] = 1
                dve.wait_ge(max_step.sem, max_step.at(1))
                n = 0
                for u in range(NM):
                    max_unit(n, n, u, 0)
                    n += 1
                row_max(n, 0, 0)
                shift_unit(n, n, 0, None)
                n += 1
                for u in range(NM):
                    max_unit(n, n, u, 1)
                    n += 1
                row_max(n, 1, 0)

                def body(h, par, base, ring_at, earlier, maxes=True, more=True):
                    n = 0
                    for e in range(NE):
                        if e == SHIFT_AT and more:
                            shift_unit(base + n, ring_at + n, 1 - par, earlier)
                            n += 1
                        if maxes:
                            for u in range(*M_AT[e]):
                                max_unit(base + n, ring_at + n, u, par)
                                n += 1
                    if maxes:
                        row_max(base + n, par, None)
                    out_unit(base + n, ring_at + n, h, par)

                first_steps = steps[1]
                with dve.Fori(0, LOOPED // 2) as i:
                    for par in range(2):
                        steps[0], steps[1] = i * (2 * 3) + first_steps, par * 3
                        body(2 * i + par, par, i * (2 * STATU) + (PRE + par * STATU), PRE,
                             i * (SHIFT * 16) + par * SHIFT * 16)
                steps[0], steps[1] = first_steps + LOOPED * 3, 0
                body(H - 2, 0, TAIL, TAIL, (H // 2 - 1) * SHIFT * 16, maxes=False)
                body(H - 1, 1, TAIL + 2, TAIL + 2, None, maxes=False, more=False)
                counts.append(steps[0] + steps[1])

        cleared.done(1)
        for par in range(2):
            m_loaded[par].done(NL * H // 2)
            e_loaded[par].done(NL * H // 2)
            shift_in[par].done(SHIFT * 16 * H // 2)
        stat_full.done(TAIL + 3)
        stat_used.done(TAIL + 3)
        max_step.done(counts[0])
        max_ready.done(H)
        scored.done(NE * H)
        expd.done(NE * H)
        pv_done.done(NE * H)
        out_copied.done(H)
        v_ready.done(2 + H)




def spline_ffn_stage(k, w, xn_t, x):
    nc = k.nc
    HALF = T // 2
    with ExitStack() as ctx:
        s2 = k.sb("spline_in", [P, HALF], F32, ctx)
        knot = k.sb("spline_knot", [P, 4, HALF], F32, ctx)
        g = k.sb("spline_sum", [P, 2, HALF], F32, ctx)
        sp_in = k.ps("spline_in_ps", [P, 2, BANK], ctx)
        out = k.ps("spline_out_ps", [P, 4, BANK], ctx)
        fed, s_ready, knots, summed = k.counter("spline_fed"), k.counter("spline_s"), k.counter("spline_knots"), k.counter("spline_summed")
        out_ready, biased, out_used = k.counter("spline_out"), k.counter("spline_biased"), k.counter("spline_out_used")
        with nc.Block() as block:

            @block.tensor
            def _(pe):
                for c in range(2):
                    for half in range(2):
                        ins = nc.tensor.matmul(sp_in[half * M0:half * M0 + M0, c, :], w["Win"][:],
                                               xn_t[:, half * HALF + c * BANK:half * HALF + (c + 1) * BANK], start=True, stop=True,
                                               tile_position=(0, half * M0))
                    ins.then_inc(fed.sem, 1)
                pe.wait_ge(summed.sem, summed.at(INNER))
                for q in range(NQ):
                    half = q // 2
                    at = slice(half * M0, half * M0 + M0)
                    for i in range(QC):
                        t0 = (q % 2) * BANK + i * P
                        ins = nc.tensor.matmul(out[:, q, i * P:(i + 1) * P], g[at, (INNER - 1) % 2, t0:t0 + P], w["Wout"][at, :],
                                               start=True, stop=True)
                    ins.then_inc(out_ready.sem, 1)

            @block.scalar
            def _(act):
                for c in range(2):
                    act.wait_ge(fed.sem, fed.at(c + 1))
                    nc.scalar.activation(s2[:, c * BANK:(c + 1) * BANK], sp_in[:, c, :], ACT.Identity,
                                         bias=w["bin"][:, 0:1]).then_inc(s_ready.sem, 1)
                act.wait_ge(s_ready.sem, s_ready.at(2))
                for h in range(INNER):
                    if h >= 4:
                        act.wait_ge(summed.sem, summed.at(h - 3))
                    nc.scalar.activation(knot[:, h % 4, :], s2[:], ACT.Relu, bias=w["b1"][:, h:h + 1],
                                         scale=w["W1"][:, h:h + 1]).then_inc(knots.sem, 1)

            @block.gpsimd
            def _(pool):
                nc.gpsimd.tensor_tensor(x[:], x[:], bcast(w["bout"][:], 1, NT), ALU.add).then_inc(biased.sem, 1)

            @block.vector
            def _(dve):
                for h in range(INNER):
                    dve.wait_ge(knots.sem, knots.at(h + 1))
                    if h == 0:
                        ins = nc.vector.tensor_scalar(g[:, 0, :], knot[:, 0, :], w["W2"][:, 0:1], w["b2"][:, 0:1], ALU.mult, ALU.add)
                    else:
                        dve.wait_ge(summed.sem, summed.at(h))
                        ins = nc.vector.scalar_tensor_tensor(g[:, h % 2, :], knot[:, h % 4, :], w["W2"][:, h:h + 1],
                                                             g[:, (h - 1) % 2, :], ALU.mult, ALU.add)
                    ins.then_inc(summed.sem, 1)
                dve.wait_ge(biased.sem, biased.at(1))
                for q in range(NQ):
                    dve.wait_ge(out_ready.sem, out_ready.at(q + 1))
                    part = x[:, QC * q:QC * q + QC, :]
                    nc.vector.tensor_tensor(part, out[:, q, :].rearrange("p (i c) -> p i c", c=C), part, ALU.add).then_inc(out_used.sem, 1)

        fed.done(2)
        s_ready.done(2)
        knots.done(INNER)
        summed.done(INNER)
        out_ready.done(NQ)
        biased.done(1)
        out_used.done(NQ)




def chunk_stage(k, w, q, kk, v, q_t, k_t, width, keep, out, absum=None):
    nc = k.nc
    VW = H * width
    G = H // QC
    with ExitStack() as ctx:
        kts = k.sb("tile_k_t", [P, 2, P], F32, ctx)
        qts = k.sb("tile_q_t", [P, 2, P], F32, ctx)
        ks = k.sb("tile_k", [P, 2, P], F32, ctx)
        vs = k.sb("tile_v", [P, 2, VW], F32, ctx)
        qx = k.sb("tile_q_heads", [P, 2, QC, P], F32, ctx)
        sm = k.sb("tile_scores", [P, 2, G, BANK], F32, ctx)
        sa = k.sb("tile_abs", [P, 2, G, BANK], F32, ctx) if absum is not None else None
        state = k.sb("state", [P, 2, VW], F32, ctx)
        st_ps = [k.ps(f"tile_scores_ps{g}", [P, BANK], ctx) for g in range(G)]
        o_ps = [k.ps(f"tile_out_ps{n}", [P, BANK], ctx) for n in range(2)]
        u_ps = k.ps("state_ps", [P, BANK], ctx)
        staged, masked, absd, s_full = k.counter("tile_staged"), k.counter("tile_masked"), k.counter("tile_abs"), k.counter("tile_scored")
        o_ready, o_used, u_ready, u_kept = k.counter("tile_out"), k.counter("tile_out_used"), k.counter("state_grown"), k.counter("state_kept")
        NS = 5
        NU = 2 if absum is not None else 1
        with nc.Block() as block:

            @block.gpsimd
            def _(pool):
                def body(i, par, wait_for):
                    if wait_for is not None:
                        pool.wait_ge(u_ready.sem, u_ready.at(wait_for))
                        pool.wait_ge(o_ready.sem, o_ready.at(wait_for))
                    nc.gpsimd.tensor_copy(qts[:, par, :], q_t[:, bass.ds(i * P, P)]).then_inc(staged.sem, 1)
                    nc.gpsimd.tensor_copy(kts[:, par, :], k_t[:, bass.ds(i * P, P)]).then_inc(staged.sem, 1)
                    nc.gpsimd.tensor_copy(ks[:, par, :], kk[:, bass.ds(i, 1), :]).then_inc(staged.sem, 1)
                    nc.gpsimd.tensor_copy(vs[:, par, :], v[:, bass.ds(i, 1), :]).then_inc(staged.sem, 1)
                    pool.wait_ge(staged.sem, staged.at(i * NS + 1))
                    nc.gpsimd.tensor_tensor(qx[:, par], bcast(qts[:, par, :], 1, QC), bcast(w["headmask"][:], 2, P), ALU.mult).then_inc(staged.sem, 1)

                body(0, 0, None)
                body(1, 1, None)
                with pool.Fori(1, NT // 2) as n:
                    for par in range(2):
                        body(2 * n + par, par, 2 * n + (par - 1))

            @block.tensor
            def _(pe):
                def body(i, par, first=False, first_two=False):
                    pe.wait_ge(staged.sem, staged.at(i * NS + NS))
                    if not first:
                        pe.wait_ge(masked.sem, masked.at(i * G))
                    for g in range(G):
                        at = slice(32 * g, 32 * g + 32)
                        ins = nc.tensor.matmul(st_ps[g][:], kts[at, par, :], qx[at, par].rearrange("p j t -> p (j t)"),
                                               start=True, stop=True, tile_position=(32 * g, 0))
                    ins.then_inc(s_full.sem, 1)
                    pe.wait_ge(u_kept.sem, u_kept.at(i + 1))
                    if not first_two:
                        pe.wait_ge(o_used.sem, o_used.at(i * NU - NU))
                    o = o_ps[par]
                    nc.tensor.matmul(o[:, 0:VW], qts[:, par, :], state[:, par, :], start=True, stop=False)
                    pe.wait_ge(masked.sem, masked.at(i * G + G))
                    for h in range(H):
                        ins = nc.tensor.matmul(o[:, h * width:(h + 1) * width], sm[:, par, h // QC, (h % QC) * P:(h % QC + 1) * P],
                                               vs[:, par, h * width:(h + 1) * width], start=False, stop=h == H - 1)
                    if absum is not None:
                        pe.wait_ge(absd.sem, absd.at(i * G + G))
                        for h in range(H):
                            ins = nc.tensor.matmul(o[:, VW + h:VW + h + 1], sa[:, par, h // QC, (h % QC) * P:(h % QC + 1) * P],
                                                   w["ones"][:, 0:1], start=False, stop=True, skip_group_check=True)
                    ins.then_inc(o_ready.sem, 1)
                    nc.tensor.matmul(u_ps[:, 0:VW], ks[:, par, :], vs[:, par, :], start=first, stop=True, skip_group_check=True).then_inc(u_ready.sem, 1)

                body(0, 0, first=True, first_two=True)
                body(1, 1, first_two=True)
                with pe.Fori(1, NT // 2) as n:
                    for par in range(2):
                        body(2 * n + par, par)

            @block.vector
            def _(dve):
                nc.vector.memset(state[:, 0, :], 0.0).then_inc(u_kept.sem, 1)

                def body(i, par, last=False):
                    dve.wait_ge(s_full.sem, s_full.at(i + 1))
                    for g in range(G):
                        nc.vector.tensor_tensor(sm[:, par, g, :].rearrange("p (j t) -> p j t", t=P), st_ps[g][:].rearrange("p (j t) -> p j t", t=P),
                                                bcast(w["keep_kq"][:], 1, QC), ALU.mult).then_inc(masked.sem, 1)
                    dve.wait_ge(o_ready.sem, o_ready.at(i + 1))
                    nc.vector.tensor_copy(out[:, bass.ds(i, 1), :], o_ps[par][:, 0:VW]).then_inc(o_used.sem, 1)
                    if absum is not None:
                        nc.vector.tensor_copy(absum[:, bass.ds(i, 1), :], o_ps[par][:, VW:VW + H]).then_inc(o_used.sem, 1)
                    if not last:
                        dve.wait_ge(u_ready.sem, u_ready.at(i + 1))
                        nc.vector.tensor_tensor(state[:, 1 - par, :], u_ps[:, 0:VW], keep, ALU.mult).then_inc(u_kept.sem, 1)

                with dve.Fori(0, NT // 2 - 1) as n:
                    for par in range(2):
                        body(2 * n + par, par)
                body(NT - 2, 0)
                body(NT - 1, 1, last=True)

            if absum is not None:
                @block.scalar
                def _(act):
                    def body(i, par):
                        for g in range(G):
                            act.wait_ge(masked.sem, masked.at(i * G + (g + 1)))
                            nc.scalar.activation(sa[:, par, g, :], sm[:, par, g, :], ACT.Abs).then_inc(absd.sem, 1)

                    with act.Fori(0, NT // 2) as n:
                        for par in range(2):
                            body(2 * n + par, par)

        staged.done(NS * NT)
        s_full.done(NT)
        masked.done(G * NT)
        if absum is not None:
            absd.done(G * NT)
        o_ready.done(NT)
        o_used.done(NU * NT)
        u_ready.done(NT)
        u_kept.done(NT)


def linear_features_stage(k, w, qkv, v9):
    nc = k.nc
    with ExitStack() as ctx:
        low = k.sb("elu_exp", [P, NT, 2 * C], F32, ctx)
        clipped, exped, step, v_step = k.counter("elu_clipped"), k.counter("elu_exp"), k.counter("elu_step"), k.counter("v9_step")
        counts = []
        with nc.Block() as block:

            @block.vector
            def _(dve):
                chain = Chain(dve, step)
                nc.vector.tensor_scalar(low[:], qkv[:, :, 0:2 * C], 0.0, None, ALU.min).then_inc(clipped.sem, 1)
                dve.wait_ge(exped.sem, exped.at(1))
                chain(nc.vector.scalar_tensor_tensor(qkv[:, :, 0:2 * C], qkv[:, :, 0:2 * C], 0.0, low[:], ALU.max, ALU.add))
                chain(nc.vector.tensor_scalar(qkv[:, :, 0:C], qkv[:, :, 0:C], float(D) ** -0.5, None, ALU.mult))
                counts.append(chain.n)

            @block.scalar
            def _(act):
                act.wait_ge(clipped.sem, clipped.at(1))
                nc.scalar.activation(low[:], low[:], ACT.Exp).then_inc(exped.sem, 1)

            @block.gpsimd
            def _(pool):
                nc.gpsimd.memset(v9[:], 1.0).then_inc(v_step.sem, 1)
                pool.wait_ge(v_step.sem, v_step.at(1))
                for i in range(NT):
                    ins = nc.gpsimd.tensor_copy(v9[:, i, :].rearrange("p (h e) -> p h e", e=D + 1)[:, :, 0:D],
                                                qkv[:, i, 2 * C:3 * C].rearrange("p (h d) -> p h d", d=D))
                ins.then_inc(v_step.sem, 1)

        clipped.done(1)
        exped.done(1)
        step.done(counts[0])
        v_step.done(2)


def linear_divide_stage(k, num, y):
    nc = k.nc
    with ExitStack() as ctx:
        den = k.sb("linear_den", [P, NT * H], F32, ctx)
        step = k.counter("linear_divide")
        counts = []
        with nc.Block() as block:

            @block.vector
            def _(dve):
                chain = Chain(dve, step)
                n = num[:].rearrange("p t (h e) -> p (t h) e", e=D + 1)
                chain(nc.vector.tensor_scalar(den[:], n[:, :, D], 1e-6, None, ALU.max))
                chain(nc.vector.reciprocal(den[:], den[:]))
                chain(nc.vector.tensor_tensor(y[:].rearrange("p t (h d) -> p (t h) d", d=D), n[:, :, 0:D], bcast(den[:], 2, D), ALU.mult))
                counts.append(chain.n)

        step.done(counts[0])




def retention_decay_stage(k, w, qkv):
    nc = k.nc
    done = k.counter("decayed")
    with nc.Block() as block:

        def scale(eng, s, table):
            x = qkv[:, :, s * C:(s + 1) * C].rearrange("p t (h d) -> p t h d", d=D)
            eng.tensor_tensor(x, x, bcast(table[:], 3, D), ALU.mult).then_inc(done.sem, 1)

        @block.vector
        def _(dve):
            scale(nc.vector, 0, w["qdecay"])

        @block.gpsimd
        def _(pool):
            scale(nc.gpsimd, 1, w["kdecay"])

    done.done(2)


def abs_sum_stage(k, w, q_t, k_t, part):
    nc = k.nc
    G = H // QC
    UNITS = [(i, c) for i in range(1, NT) for c in range((i * P + BANK - 1) // BANK)]
    NU = len(UNITS)
    assert NU % 2 == 0
    with ExitStack() as ctx:
        qj = k.sb("q_heads", [P, 2, T], F32, ctx)
        ps = [[k.ps(f"abs_ps{s}{g}", [P, BANK], ctx) for g in range(G)] for s in range(2)]
        picked, scored, a_used, d_used = k.counter("abs_q_ready"), k.counter("abs_scored"), k.counter("abs_act_used"), k.counter("abs_dve_used")
        cleared = k.counter("abs_cleared")
        with nc.Block() as block:

            @block.gpsimd
            def _(pool):
                nc.gpsimd.memset(part[:], 0.0).then_inc(cleared.sem, 1)

                def body(j, par, before):
                    if before is not None:
                        pool.wait_ge(scored.sem, scored.at(before))
                    nc.gpsimd.tensor_scalar(qj[:, par, :], q_t[:], w["headmask"][:, bass.ds(j, 1)], None, ALU.mult).then_inc(picked.sem, 1)

                body(0, 0, None)
                body(1, 1, None)
                with pool.Fori(1, QC // 2) as n:
                    for par in range(2):
                        body(2 * n + par, par, n * (2 * NU) + (par - 1) * NU)

            def width(u):
                i, c = UNITS[u]
                return min(BANK, i * P - c * BANK)

            @block.tensor
            def _(pe):
                def body(j, par, first=False):
                    pe.wait_ge(picked.sem, picked.at(j + 1))
                    for u, (i, c) in enumerate(UNITS):
                        if not first or u >= 2:
                            pe.wait_ge(a_used.sem, a_used.at(j * (2 * NU) + (2 * u - 2)))
                            pe.wait_ge(d_used.sem, d_used.at(j * (2 * NU) + (2 * u - 2)))
                        for g in range(G):
                            at = slice(32 * g, 32 * g + 32)
                            ins = nc.tensor.matmul(ps[u % 2][g][:, 0:width(u)], qj[at, par, i * P:(i + 1) * P],
                                                   k_t[at, c * BANK:c * BANK + width(u)], start=True, stop=True, tile_position=(32 * g, 0))
                        ins.then_inc(scored.sem, 1)

                body(0, 0, first=True)
                body(1, 1)
                with pe.Fori(1, QC // 2) as n:
                    for par in range(2):
                        body(2 * n + par, par)

            @block.scalar
            def _(act):
                act.wait_ge(cleared.sem, cleared.at(1))

                def body(j, par):
                    for u, (i, c) in enumerate(UNITS):
                        act.wait_ge(scored.sem, scored.at(j * NU + (u + 1)))
                        for g in range(2):
                            nc.scalar.activation(ps[u % 2][g][:, 0:width(u)], ps[u % 2][g][:, 0:width(u)], ACT.Abs,
                                                 accum_out=part[:, bass.ds(j, 1), g, i, c:c + 1]).then_inc(a_used.sem, 1)

                with act.Fori(0, QC // 2) as n:
                    for par in range(2):
                        body(2 * n + par, par)

            @block.vector
            def _(dve):
                dve.wait_ge(cleared.sem, cleared.at(1))

                def body(j, par):
                    for u, (i, c) in enumerate(UNITS):
                        dve.wait_ge(scored.sem, scored.at(j * NU + (u + 1)))
                        for g in range(2, G):
                            nc.vector.tensor_reduce(part[:, bass.ds(j, 1), g, i, c:c + 1], ps[u % 2][g][:, 0:width(u)], AX.X, ALU.add,
                                                    apply_absolute_value=True).then_inc(d_used.sem, 1)

                with dve.Fori(0, QC // 2) as n:
                    for par in range(2):
                        body(2 * n + par, par)

        cleared.done(1)
        picked.done(QC)
        scored.done(QC * NU)
        a_used.done(2 * QC * NU)
        d_used.done(2 * QC * NU)


def retention_norm_stage(k, w, part, absum, ret, gate):
    nc = k.nc
    eps = float(np.finfo(np.float32).eps)
    with ExitStack() as ctx:
        den = k.sb("ret_den", [P, NT, H], F32, ctx)
        sq = k.sb("ret_sq", [P, NT, H * VD], F32, ctx)
        ms = k.sb("ret_ms", [P, NT, H], F32, ctx)
        step, squared, ms_ready, std_ready, gated = (k.counter("ret_" + n) for n in ("step", "squared", "ms", "std", "gated"))
        counts = []
        with nc.Block() as block:

            @block.scalar
            def _(act):
                nc.scalar.activation(sq[:], ret[:], ACT.Square).then_inc(squared.sem, 1)
                act.wait_ge(ms_ready.sem, ms_ready.at(1))
                nc.scalar.sqrt(ms[:], ms[:]).then_inc(std_ready.sem, 1)

            @block.gpsimd
            def _(pool):
                nc.gpsimd.tensor_tensor(gate[:], gate[:], ret[:], ALU.mult).then_inc(gated.sem, 1)

            @block.vector
            def _(dve):
                chain = Chain(dve, step)
                for j in range(QC):
                    for g in range(H // QC):
                        ins = nc.vector.tensor_reduce(den[:, :, g * QC + j], part[:, j, g], AX.X, ALU.add)
                chain(ins)
                chain(nc.vector.tensor_tensor(den[:], den[:], absum[:], ALU.add))
                chain(nc.vector.tensor_scalar(den[:], den[:], 1.0, 50000.0, ALU.max, ALU.min))
                chain(nc.vector.reciprocal(den[:], den[:]))
                dve.wait_ge(squared.sem, squared.at(1))
                chain(nc.vector.tensor_reduce(ms[:], sq[:].rearrange("p t (h v) -> p t h v", v=VD), AX.X, ALU.add))
                chain(nc.vector.scalar_tensor_tensor(ms[:], ms[:], 1.0 / VD, den[:], ALU.mult, ALU.mult))
                chain(nc.vector.tensor_tensor(ms[:], ms[:], den[:], ALU.mult))
                nc.vector.tensor_scalar(ms[:], ms[:], eps, None, ALU.add).then_inc(ms_ready.sem, 1)
                dve.wait_ge(std_ready.sem, std_ready.at(1))
                chain(nc.vector.reciprocal(ms[:], ms[:]))
                chain(nc.vector.tensor_tensor(ms[:], ms[:], den[:], ALU.mult))
                dve.wait_ge(gated.sem, gated.at(1))
                gv = gate[:].rearrange("p t (h v) -> p t h v", v=VD)
                chain(nc.vector.tensor_tensor(gv, gv, bcast(ms[:], 3, VD), ALU.mult))
                counts.append(chain.n)

        step.done(counts[0])
        for s in (squared, ms_ready, std_ready, gated):
            s.done(1)


def add_row_stage(k, x, row):
    nc = k.nc
    done = k.counter("row_added")
    with nc.Block() as block:

        @block.gpsimd
        def _(pool):
            nc.gpsimd.tensor_tensor(x[:], x[:], bcast(row[:], 1, NT), ALU.add).then_inc(done.sem, 1)

    done.done(1)




def rwkv_stage(k, w, xn_t, out_t):
    nc = k.nc
    with ExitStack() as ctx:
        xm = k.sb("mixed", [P, 3, T], F32, ctx)
        om = k.sb("one_minus_mix", [P, 3], F32, ctx)
        kvr = k.sb("kvr", [P, 3, T], F32, ctx)
        wneg = k.sb("neg_decay", [P, 1], F32, ctx)
        pmax = k.sb("exp_max", [P, T + 1], F32, ctx)
        num = k.sb("wkv_num", [P, T + 1], F32, ctx)
        den = k.sb("wkv_den", [P, T + 1], F32, ctx)
        grow = k.sb("carry_factor", [P, T], F32, ctx)
        add = k.sb("new_factor", [P, T], F32, ctx)
        e1 = k.sb("read_carry", [P, T], F32, ctx)
        e2 = k.sb("read_new", [P, T], F32, ctx)
        wt = k.sb("decay_row", [P, T], F32, ctx)
        ps = k.ps("kvr_ps", [P, 4, BANK], ctx)
        step, mixed, fed, kept, w_ready = (k.counter("rwkv_" + n) for n in ("step", "mixed", "fed", "kept", "w"))
        args, exps, sig = k.counter("rwkv_args"), k.counter("rwkv_exps"), k.counter("rwkv_sig")
        counts = []
        kk, vv, rr = kvr[:, 0, :], kvr[:, 1, :], kvr[:, 2, :]
        with nc.Block() as block:

            @block.vector
            def _(dve):
                chain = Chain(dve, step)
                chain(nc.vector.tensor_scalar(om[:], w["mix"][:], -1.0, 1.0, ALU.mult, ALU.add))
                for n in range(3):
                    chain(nc.vector.tensor_scalar(xm[:, n, :], xn_t[:], w["mix"][:, n:n + 1], None, ALU.mult))
                    nc.vector.scalar_tensor_tensor(xm[:, n, 1:], xn_t[:, 0:T - 1], om[:, n:n + 1], xm[:, n, 1:],
                                                   ALU.mult, ALU.add).then_inc(mixed.sem, 1)
                nc.vector.memset(pmax[:, 0:1], -1e38)
                nc.vector.memset(num[:, 0:1], 0.0)
                nc.vector.memset(den[:, 0:1], 0.0)
                chain(nc.vector.memset(wt[:], 0.0))
                dve.wait_ge(w_ready.sem, w_ready.at(1))
                chain(nc.vector.tensor_scalar(wneg[:], wneg[:], -1.0, None, ALU.mult))
                chain(nc.vector.tensor_scalar(wt[:], wt[:], wneg[:, 0:1], None, ALU.add))
                dve.wait_ge(kept.sem, kept.at(4))
                chain(nc.vector.tensor_tensor_scan(pmax[:, 1:], wt[:], kk, -1e38, ALU.add, ALU.max))
                chain(nc.vector.scalar_tensor_tensor(grow[:], pmax[:, 0:T], wneg[:, 0:1], pmax[:, 1:], ALU.add, ALU.subtract))
                nc.vector.tensor_tensor(add[:], kk, pmax[:, 1:], ALU.subtract).then_inc(args.sem, 1)
                chain(nc.vector.scalar_tensor_tensor(wt[:], kk, w["first"][:, 0:1], pmax[:, 0:T], ALU.add, ALU.max))
                chain(nc.vector.tensor_tensor(e1[:], pmax[:, 0:T], wt[:], ALU.subtract))
                nc.vector.scalar_tensor_tensor(e2[:], kk, w["first"][:, 0:1], wt[:], ALU.add, ALU.subtract).then_inc(args.sem, 1)
                dve.wait_ge(exps.sem, exps.at(2))
                chain(nc.vector.tensor_tensor_scan(den[:, 1:], grow[:], add[:], 0.0, ALU.mult, ALU.add))
                dve.wait_ge(kept.sem, kept.at(8))
                chain(nc.vector.tensor_tensor(add[:], add[:], vv, ALU.mult))
                chain(nc.vector.tensor_tensor_scan(num[:, 1:], grow[:], add[:], 0.0, ALU.mult, ALU.add))
                dve.wait_ge(exps.sem, exps.at(4))
                chain(nc.vector.tensor_tensor(grow[:], e1[:], den[:, 0:T], ALU.mult))
                chain(nc.vector.tensor_tensor(grow[:], grow[:], e2[:], ALU.add))
                chain(nc.vector.tensor_tensor(e1[:], e1[:], num[:, 0:T], ALU.mult))
                chain(nc.vector.tensor_tensor(e2[:], e2[:], vv, ALU.mult))
                chain(nc.vector.tensor_tensor(e1[:], e1[:], e2[:], ALU.add))
                dve.wait_ge(sig.sem, sig.at(1))
                chain(nc.vector.scalar_tensor_tensor(grow[:], rr, 1.0, grow[:], ALU.add, ALU.mult))
                chain(nc.vector.reciprocal(grow[:], grow[:]))
                chain(nc.vector.tensor_tensor(out_t[:], e1[:], grow[:], ALU.mult))
                counts.append(chain.n)

            @block.tensor
            def _(pe):
                for n in range(3):
                    pe.wait_ge(mixed.sem, mixed.at(n + 1))
                    for q in range(NQ):
                        u = n * NQ + q
                        if u >= 4:
                            pe.wait_ge(kept.sem, kept.at(u - 3))
                        nc.tensor.matmul(ps[:, u % 4, :], w["wT"][:, 8 + n, :], xm[:, n, q * BANK:(q + 1) * BANK],
                                         start=True, stop=True).then_inc(fed.sem, 1)

            @block.scalar
            def _(act):
                nc.scalar.activation(wneg[:], w["decay"][:], ACT.Exp).then_inc(w_ready.sem, 1)
                for u in range(3 * NQ):
                    act.wait_ge(fed.sem, fed.at(u + 1))
                    dst = kvr[:, u // NQ, (u % NQ) * BANK:(u % NQ + 1) * BANK]
                    if u < 2 * NQ:
                        nc.scalar.copy(dst, ps[:, u % 4, :]).then_inc(kept.sem, 1)
                    else:
                        nc.scalar.activation(dst, ps[:, u % 4, :], ACT.Exp, scale=-1.0).then_inc(kept.sem, 1)
                act.wait_ge(kept.sem, kept.at(3 * NQ))
                nc.scalar.copy(xm[:, 0, 0:1], rr[:, 0:1]).then_inc(sig.sem, 1)
                act.wait_ge(args.sem, args.at(1))
                for a in (grow, add):
                    nc.scalar.activation(a[:], a[:], ACT.Exp).then_inc(exps.sem, 1)
                act.wait_ge(args.sem, args.at(2))
                for a in (e1, e2):
                    nc.scalar.activation(a[:], a[:], ACT.Exp).then_inc(exps.sem, 1)

        step.done(counts[0])
        mixed.done(3)
        fed.done(3 * NQ)
        kept.done(3 * NQ)
        w_ready.done(1)
        args.done(2)
        exps.done(4)
        sig.done(1)




def conv_stage(k, w, h_t, hc_t):
    nc = k.nc
    step = k.counter("conv_step")
    counts = []
    with nc.Block() as block:

        @block.vector
        def _(dve):
            chain = Chain(dve, step)
            chain(nc.vector.tensor_scalar(hc_t[:], h_t[:], w["conv_w"][:, 2:3], None, ALU.mult))
            for tap in (1, 0):
                lag = 2 - tap
                chain(nc.vector.scalar_tensor_tensor(hc_t[:, lag:], h_t[:, 0:T - lag], w["conv_w"][:, tap:tap + 1], hc_t[:, lag:], ALU.mult, ALU.add))
            counts.append(chain.n)

    step.done(counts[0])


def experts_stage(k, w, h_t, x):
    nc = k.nc
    NF = DFF // P
    with ExitStack() as ctx:
        logits = k.sb("logits", [P, NT, E], F32, ctx)
        best = k.sb("best", [P, NT], F32, ctx)
        pick = k.sb("pick", [P, NT, E], F32, ctx)
        free = k.sb("not_picked", [P, NT], F32, ctx)
        gate = k.sb("gate", [P, 4, BANK], F32, ctx)
        hid = k.sb("hidden", [P, 2, NF, BANK], F32, ctx)
        lp = k.ps("logits_ps", [P, BANK], ctx)
        gp = [k.ps(f"gate_ps{n}", [P, BANK], ctx) for n in range(2)]
        vp = [k.ps(f"value_ps{n}", [P, BANK], ctx) for n in range(2)]
        op = [k.ps(f"expert_ps{n}", [P, BANK], ctx) for n in range(2)]
        routed, step = k.counter("routed"), k.counter("route_step")
        upped, gated, hid_ready, downed, out_used = (k.counter("expert_" + n) for n in ("up", "gate", "hidden", "down", "used"))
        counts = []
        with nc.Block() as block:

            @block.tensor
            def _(pe):
                for i in range(NT):
                    ins = nc.tensor.matmul(lp[:, i * E:(i + 1) * E], h_t[:, i * P:(i + 1) * P], w["router"][:], start=True, stop=True)
                ins.then_inc(routed.sem, 1)

                def down(n, e):
                    u = n * E + e
                    pe.wait_ge(hid_ready.sem, hid_ready.at(n * (E * NF) + (e + 1) * NF))
                    for s in range(QC):
                        for f in range(NF):
                            ins = nc.tensor.matmul(op[e % 2][:, s * P:(s + 1) * P], hid[:, e % 2, f, s * P:(s + 1) * P],
                                                   w["expert_proj"][:, e, f, :], start=f == 0, stop=f == NF - 1)
                    ins.then_inc(downed.sem, 1)

                def body(n, first=False):
                    for e in range(E):
                        for f in range(NF):
                            g = e * NF + f
                            if not first or g >= 2:
                                pe.wait_ge(hid_ready.sem, hid_ready.at(n * (E * NF) + (g - 1)))
                            rhs = h_t[:, bass.ds(n * BANK, BANK)]
                            nc.tensor.matmul(gp[g % 2][:], w["expert_wv"][:, e, f * P:(f + 1) * P], rhs, start=True, stop=True).then_inc(upped.sem, 1)
                            nc.tensor.matmul(vp[g % 2][:], w["expert_wv"][:, e, DFF + f * P:DFF + (f + 1) * P], rhs, start=True, stop=True).then_inc(upped.sem, 1)
                        if not first or e >= 2:
                            pe.wait_ge(out_used.sem, out_used.at(n * (E * QC) + (e - 1) * QC))
                        down(n, e)

                body(0, first=True)
                with pe.Fori(1, NQ) as n:
                    body(n)

            @block.scalar
            def _(act):
                def body(n, first=False):
                    for g in range(E * NF):
                        act.wait_ge(upped.sem, upped.at(n * (2 * E * NF) + (2 * g + 1)))
                        if not first or g >= 4:
                            act.wait_ge(hid_ready.sem, hid_ready.at(n * (E * NF) + (g - 3)))
                        nc.scalar.activation(gate[:, g % 4, :], gp[g % 2][:], ACT.Silu).then_inc(gated.sem, 1)

                body(0, first=True)
                with act.Fori(1, NQ) as n:
                    body(n)

            @block.vector
            def _(dve):
                chain = Chain(dve, step)
                dve.wait_ge(routed.sem, routed.at(1))
                lv = lp[:, 0:NT * E].rearrange("p (t e) -> p t e", e=E)
                chain(nc.vector.tensor_copy(logits[:], lv))
                nc.vector.memset(free[:], 1.0)
                chain(nc.vector.tensor_reduce(best[:], logits[:], AX.X, ALU.max))
                for e in range(E):
                    chain(nc.vector.tensor_tensor(pick[:, :, e], logits[:, :, e], best[:], ALU.is_equal))
                    chain(nc.vector.tensor_tensor(pick[:, :, e], pick[:, :, e], free[:], ALU.mult))
                    chain(nc.vector.tensor_tensor(free[:], free[:], pick[:, :, e], ALU.subtract))

                def add_out(n, e):
                    dve.wait_ge(downed.sem, downed.at(n * E + (e + 1)))
                    for s in range(QC):
                        i = n * QC + s
                        if e > 0:
                            dve.wait_ge(out_used.sem, out_used.at(n * (E * QC) + ((e - 1) * QC + s + 1)))
                        xi = x[:, bass.ds(i, 1), :].rearrange("p o c -> p (o c)")
                        nc.vector.scalar_tensor_tensor(xi, op[e % 2][:, s * P:(s + 1) * P], pick[:, bass.ds(i, 1), e], xi,
                                                       ALU.mult, ALU.add).then_inc(out_used.sem, 1)

                def body(n, first=False):
                    for e in range(E):
                        for f in range(NF):
                            g = e * NF + f
                            dve.wait_ge(gated.sem, gated.at(n * (E * NF) + (g + 1)))
                            dve.wait_ge(upped.sem, upped.at(n * (2 * E * NF) + (2 * g + 2)))
                            if f == 0 and (not first or e >= 2):
                                dve.wait_ge(downed.sem, downed.at(n * E + (e - 1)))
                            nc.vector.tensor_tensor(hid[:, e % 2, f, :], vp[g % 2][:], gate[:, g % 4, :], ALU.mult).then_inc(hid_ready.sem, 1)
                            if f == 1 and e > 0:
                                add_out(n, e - 1)
                    add_out(n, E - 1)

                body(0, first=True)
                with dve.Fori(1, NQ) as n:
                    body(n)
                counts.append(chain.n)

        routed.done(1)
        step.done(counts[0])
        upped.done(2 * NQ * E * NF)
        gated.done(NQ * E * NF)
        hid_ready.done(NQ * E * NF)
        downed.done(NQ * E)
        out_used.done(NQ * E * QC)


def store_stage(k, x, out):
    nc = k.nc
    stored = k.counter("stored")
    with nc.Block() as block:

        @block.sync
        def _(sp):
            sp.dma_start(out.rearrange("o (t p) c -> p (o t) c", p=P), x[:]).then_inc(stored.sem, 16)
            sp.wait_ge(stored.sem, stored.at(16))

    stored.done(16)




def softmax_layer(k, w, h_t, wqkv, wo, parts_dram, norm, x):
    with ExitStack() as ctx:
        qkv = k.sb("qkv", [P, NT, 3 * C], F32, ctx)
        project_stage(k, [([(h_t, wqkv)], qkv, None)])
        rope_stage(k, w, qkv, norm)
        split_stage(k, w, qkv, parts_dram)
        y = k.sb("attn_out", [P, NT, C], F32, ctx)
        y_t = k.sb("attn_out_t", [P, T], F32, ctx)
        attention_stage(k, w, qkv, parts_dram, float(D) ** -0.5, y)
        transpose_stage(k, [(y, y_t)], w["ident"])
        project_stage(k, [([(y_t, wo)], x, None)], add_to=True)


def spline_layer(k, w, x):
    with ExitStack() as ctx:
        xn = k.sb("xn", [P, NT, C], F32, ctx)
        xn_t = k.sb("xn_t", [P, T], F32, ctx)
        layer_norm(k, x, xn, w["ident"], xn_t)
        spline_ffn_stage(k, w, xn_t, x)


def retention_layer(k, w, x):
    with ExitStack() as ctx:
        qkv = k.sb("ret_qkv", [P, NT, BANK], F32, ctx)
        gate = k.sb("ret_gate", [P, NT, H * VD], F32, ctx)
        q_t = k.sb("ret_q_t", [P, T], F32, ctx)
        k_t = k.sb("ret_k_t", [P, T], F32, ctx)
        part = k.sb("abs_part", [P, QC, H // QC, NT, NQ], F32, ctx)
        absum = k.sb("abs_diag", [P, NT, H], F32, ctx)
        ret = k.sb("ret_out", [P, NT, H * VD], F32, ctx)
        with ExitStack() as inner:
            xn = k.sb("xn", [P, NT, C], F32, inner)
            xn_t = k.sb("xn_t", [P, T], F32, inner)
            layer_norm(k, x, xn, w["ident"], xn_t)
            project_stage(k, [([(xn_t, w["w_qkv_r"][:])], qkv, w["b_qkv_r"][:]), ([(xn_t, w["w_g"][:])], gate, w["b_g"][:])])
        retention_decay_stage(k, w, qkv)
        transpose_stage(k, [(qkv[:, :, 0:C], q_t), (qkv[:, :, C:2 * C], k_t)], w["ident"])
        abs_sum_stage(k, w, q_t, k_t, part)
        chunk_stage(k, w, None, qkv[:, :, C:2 * C], qkv[:, :, 2 * C:], q_t, k_t, VD, w["bd16"][:], ret, absum)
        retention_norm_stage(k, w, part, absum, ret, gate)
        with ExitStack() as inner:
            g_t = [k.sb(f"gated_t{b}", [P, T], F32, inner) for b in range(2)]
            transpose_stage(k, [(gate[:, :, b * C:(b + 1) * C], g_t[b]) for b in range(2)], w["ident"])
            add_row_stage(k, x, w["b_o"])
            project_stage(k, [([(g_t[b], w["w_o_r"][:, b, :]) for b in range(2)], x, None)], add_to=True)


def linear_layer(k, w, x):
    with ExitStack() as ctx:
        qkv = k.sb("lin_qkv", [P, NT, 3 * C], F32, ctx)
        xn = k.sb("xn", [P, NT, C], F32, ctx)
        xn_t = k.sb("xn_t", [P, T], F32, ctx)
        v9 = k.sb("v9", [P, NT, H * (D + 1)], F32, ctx)
        q_t = k.sb("lin_q_t", [P, T], F32, ctx)
        k_t = k.sb("lin_k_t", [P, T], F32, ctx)
        num = k.sb("lin_out", [P, NT, H * (D + 1)], F32, ctx)
        layer_norm(k, x, xn, w["ident"], xn_t)
        project_stage(k, [([(xn_t, w["wT"][:, 4:7, :].rearrange("p b c -> p (b c)"))], qkv, None)])
        linear_features_stage(k, w, qkv, v9)
        transpose_stage(k, [(qkv[:, :, 0:C], q_t), (qkv[:, :, C:2 * C], k_t)], w["ident"])
        chunk_stage(k, w, None, qkv[:, :, C:2 * C], v9, q_t, k_t, D + 1, w["bd9"][:], num)
        linear_divide_stage(k, num, xn)
        transpose_stage(k, [(xn, xn_t)], w["ident"])
        project_stage(k, [([(xn_t, w["wT"][:, 7, :])], x, None)], add_to=True)


def rwkv_layer(k, w, x):
    with ExitStack() as ctx:
        xn = k.sb("xn", [P, NT, C], F32, ctx)
        xn_t = k.sb("xn_t", [P, T], F32, ctx)
        out_t = k.sb("rwkv_t", [P, T], F32, ctx)
        layer_norm(k, x, xn, w["ident"], xn_t)
        rwkv_stage(k, w, xn_t, out_t)
        project_stage(k, [([(out_t, w["wT"][:, 11, :])], x, None)], add_to=True)


def conv_moe_layer(k, w, x, parts_dram):
    nc = k.nc
    with ExitStack() as ctx:
        y = k.sb("moe_y", [P, NT, C], F32, ctx)
        layer_norm(k, x, y, w["ident"])
        with ExitStack() as inner:
            hc_t = k.sb("conv_t", [P, T], F32, inner)
            with ExitStack() as first:
                h = k.sb("ln1", [P, NT, C], F32, first)
                h_t = k.sb("ln1_t", [P, T], F32, first)
                layer_norm(k, y, h, w["ident"], h_t, affine=(w["ln1_w"], w["ln1_b"]))
                conv_stage(k, w, h_t, hc_t)
            softmax_layer(k, w, hc_t, w["attn_w"][:], w["proj_w"][:], parts_dram, False, y)
        with ExitStack() as inner:
            h = k.sb("ln2", [P, NT, C], F32, inner)
            h_t = k.sb("ln2_t", [P, T], F32, inner)
            layer_norm(k, y, h, w["ident"], h_t, affine=(w["ln2_w"], w["ln2_b"]))
            experts_stage(k, w, h_t, y)
        added = k.counter("moe_added")
        with nc.Block() as block:

            @block.vector
            def _(dve):
                nc.vector.tensor_tensor(x[:], x[:], y[:], ALU.add).then_inc(added.sem, 1)

        added.done(1)


def build(nc, d, out):
    ctx = ExitStack()
    with ctx:
        k = Kernel(nc, ctx)
        w = {name: k.sb(name, shape, dtype) for name, shape, dtype in [
            ("X", [P, NT, C], F32), ("wT", [P, 12, C], F32), ("ident", [P, P], F32), ("ident16", [P, P], BF16),
            ("mask_qk", [P, P], BF16), ("mask_kq", [P, P], BF16), ("keep_kq", [P, P], F32), ("ones", [P, 1], F32),
            ("cos", [P, NT, D], F32), ("sin", [P, NT, D], F32), ("headmask", [P, QC], F32),
            ("bd16", [P, H * VD], F32), ("bd9", [P, H * (D + 1)], F32),
            ("qdecay", [P, NT, H], F32), ("kdecay", [P, NT, H], F32), ("qn", [P, D], F32), ("kn", [P, D], F32),
            ("w_qkv_r", [P, BANK], F32), ("b_qkv_r", [P, BANK], F32), ("w_g", [P, H * VD], F32), ("b_g", [P, H * VD], F32),
            ("w_o_r", [P, 2, C], F32), ("b_o", [P, C], F32),
            ("Win", [P, M0], F32), ("bin", [P, 1], F32), ("W1", [P, INNER], F32), ("b1", [P, INNER], F32),
            ("W2", [P, INNER], F32), ("b2", [P, 1], F32), ("Wout", [P, C], F32), ("bout", [P, C], F32),
            ("mix", [P, 3], F32), ("decay", [P, 1], F32), ("first", [P, 1], F32),
            ("ln1_w", [P, C], F32), ("ln1_b", [P, C], F32), ("ln2_w", [P, C], F32), ("ln2_b", [P, C], F32),
            ("conv_w", [P, 3], F32), ("attn_w", [P, 3 * C], F32), ("proj_w", [P, C], F32), ("router", [P, E], F32),
            ("expert_wv", [P, E, 2 * DFF], F32), ("expert_proj", [P, E, DFF // P, C], F32)]}
        parts_dram = [nc.dram_tensor(f"{n}_parts", (PARTS, C, T), BF16, kind="Internal").ap() for n in "qk"]
        x = w["X"]
        load_stage(k, d, w)
        STAGES = d["stages"]
        if 1 in STAGES:
            with ExitStack() as inner:
                xn = k.sb("xn", [P, NT, C], F32, inner)
                xn_t = k.sb("xn_t", [P, T], F32, inner)
                layer_norm(k, x, xn, w["ident"], xn_t)
                softmax_layer(k, w, xn_t, w["wT"][:, 0:3, :].rearrange("p b c -> p (b c)"), w["wT"][:, 3, :], parts_dram, True, x)
        if 2 in STAGES:
            spline_layer(k, w, x)
        if 3 in STAGES:
            retention_layer(k, w, x)
        if 4 in STAGES:
            spline_layer(k, w, x)
        if 5 in STAGES:
            linear_layer(k, w, x)
        if 6 in STAGES:
            conv_moe_layer(k, w, x, parts_dram)
        if 7 in STAGES:
            rwkv_layer(k, w, x)
        if 8 in STAGES:
            conv_moe_layer(k, w, x, parts_dram)
        store_stage(k, x, out)


def shape_constants():
    t = np.arange(T, dtype=np.float32)
    freq = (1.0 / np.float32(10000.0) ** (np.arange(0, D // 2, dtype=np.float32) * np.float32(2.0) / np.float32(D))).astype(np.float32)
    ang = (t[:, None] * freq[None, :]).astype(np.float32)
    cos, sin = np.cos(ang), np.sin(ang)

    def tiles(a):
        return np.ascontiguousarray(a.reshape(NT, P, -1).transpose(1, 0, 2)).astype(np.float32)

    n = np.arange(P)
    head = np.arange(H, dtype=np.float64)
    gamma = np.log1p(-2.0 ** (-5.0 - head))
    pos = np.arange(T, dtype=np.float64)[:, None]
    decay_sum = -np.expm1(gamma * (pos + 1)) / -np.expm1(gamma)
    row = n // D
    return {
        "c_mask_qk": np.where(n[None, :] > n[:, None], NEG, 0.0).astype(np.float32),
        "c_mask_kq": np.where(n[:, None] > n[None, :], NEG, 0.0).astype(np.float32),
        "c_keep_kq": (n[:, None] <= n[None, :]).astype(np.float32),
        "c_ident": np.eye(P, dtype=np.float32),
        "c_cos": tiles(np.concatenate([cos, cos], 1)),
        "c_sin": tiles(np.concatenate([-sin, sin], 1)),
        "c_headmask": (row[:, None] % QC == np.arange(QC)[None, :]).astype(np.float32),
        "c_bd16": (row[:, None] == np.arange(H * VD)[None, :] // VD).astype(np.float32),
        "c_bd9": (row[:, None] == np.arange(H * (D + 1))[None, :] // (D + 1)).astype(np.float32),
        "c_qdecay": tiles(np.exp(gamma * (pos - T // 2)) / np.sqrt(decay_sum)),
        "c_kdecay": tiles(np.exp(gamma * (T // 2 - pos))),
    }


def kernel(**inputs):
    import numpy as _np
    import concourse.bacc as _bacc
    from concourse import mybir as _mybir
    from concourse.bass_utils import run_bass_kernel_spmd as _run

    nc = _bacc.Bacc("TRN2", target_bir_lowering=False, num_devices=1)
    arrays, d = {}, {}
    for name, value in list(inputs.items()) + list(shape_constants().items()):
        a = _np.ascontiguousarray(value)
        arrays[f"in_{name}"] = a
        key = "x" if name == "L0_attn_a_x" else name
        d[key] = nc.dram_tensor(f"in_{name}", a.shape, _mybir.dt.from_np(a.dtype), kind="ExternalInput").ap()
    d["stages"] = (1, 2, 3, 4, 5, 6, 7, 8)
    out = nc.dram_tensor("out_0", (1, T, C), F32, kind="ExternalOutput").ap()
    build(nc, d, out)
    r = _run(nc, [arrays], core_ids=[0])
    return r.results[0]["out_0"]
```

```python
import numpy as np
import concourse.bass as bass
from concourse import mybir
from contextlib import ExitStack

F32 = mybir.dt.float32
BF16 = mybir.dt.bfloat16
ACT = mybir.ActivationFunctionType
ALU = mybir.AluOpType
AX = mybir.AxisListType

T, C, H = 2048, 128, 16
P = 128
NT = T // P
D = C // H
BANK = 512
QC = BANK // P
NQ = T // BANK
NEG = -1e30
PARTS = 3
KROWS = PARTS * PARTS * D
SHIFT = 2
VD = 16
M0, INNER = 64, 16
E, DFF = 4, 512


class Counter:

    def __init__(self, sem):
        self.sem, self.sent = sem, 0

    def at(self, n):
        return n + self.sent if self.sent else n

    def done(self, n):
        self.sent += n


class Kernel:

    def __init__(self, nc, ctx):
        self.nc, self.ctx, self.counters, self.count = nc, ctx, {}, 0

    def counter(self, name):
        if name not in self.counters:
            self.counters[name] = Counter(self.ctx.enter_context(self.nc.semaphore(name)))
        return self.counters[name]

    def sb(self, name, shape, dtype=F32, ctx=None):
        self.count += 1
        return (ctx or self.ctx).enter_context(self.nc.sbuf_tensor(f"{name}_{self.count}", shape, dtype))

    def ps(self, name, shape, ctx, dtype=F32):
        self.count += 1
        return ctx.enter_context(self.nc.psum_tensor(f"{name}_{self.count}", shape, dtype))


class Chain:

    def __init__(self, eng, counter):
        self.eng, self.counter, self.n = eng, counter, 0

    def __call__(self, ins):
        self.n += 1
        ins.then_inc(self.counter.sem, 1)
        self.eng.wait_ge(self.counter.sem, self.counter.at(self.n))


def bcast(ap, axis, n):
    a = ap.unsqueeze(axis)
    shape = list(a.shape)
    shape[axis] = n
    return a.broadcast_to(shape)




def load_stage(k, d, w):
    nc = k.nc
    with ExitStack() as ctx:
        raw = k.sb("raw_w", [P, 12, C], F32, ctx)
        maskf = k.sb("mask_f32", [P, 3, P], F32, ctx)
        tp = k.ps("weight_t", [P, 3, BANK], ctx)
        padded = k.counter("rows_padded")
        loaded, turned, kept = k.counter("loaded"), k.counter("weights_turned"), k.counter("weights_kept")
        plain = [
            (w["X"][:], d["x"].rearrange("o (t p) c -> p (o t) c", p=P)),
            (raw[:, 0:3, :], d["L0_attn_a_w_qkv"].rearrange("(b p) c -> p b c", p=P)),
            (raw[:, 3, :], d["L0_attn_a_w_out"]),
            (raw[:, 4:7, :], d["L1_attn_a_W_qkv"].rearrange("(b p) c -> p b c", p=P)),
            (raw[:, 7, :], d["L1_attn_a_W_out"]),
            (raw[:, 8, :], d["L1_attn_b_Wk"]),
            (raw[:, 9, :], d["L1_attn_b_Wv"]),
            (raw[:, 10, :], d["L1_attn_b_Wr"]),
            (raw[:, 11, :], d["L1_attn_b_Wo"]),
            (maskf[:, 0, :], d["c_mask_qk"]),
            (maskf[:, 1, :], d["c_mask_kq"]),
            (maskf[:, 2, :], d["c_ident"]),
            (w["ident"][:], d["c_ident"]),
            (w["keep_kq"][:], d["c_keep_kq"]),
            (w["cos"][:], d["c_cos"]),
            (w["sin"][:], d["c_sin"]),
            (w["headmask"][:], d["c_headmask"]),
            (w["bd16"][:], d["c_bd16"]),
            (w["bd9"][:], d["c_bd9"]),
            (w["qdecay"][:], d["c_qdecay"]),
            (w["kdecay"][:], d["c_kdecay"]),
            (w["qn"][:], d["L0_attn_a_q_norm_w"].partition_broadcast(P)),
            (w["kn"][:], d["L0_attn_a_k_norm_w"].partition_broadcast(P)),
            (w["w_qkv_r"][:, 0:2 * C], d["L0_attn_b_W_qk"]),
            (w["w_qkv_r"][:, 2 * C:], d["L0_attn_b_W_v"]),
            (w["b_qkv_r"][:, 0:2 * C], d["L0_attn_b_b_qk"].partition_broadcast(P)),
            (w["b_qkv_r"][:, 2 * C:], d["L0_attn_b_b_v"].partition_broadcast(P)),
            (w["w_g"][:], d["L0_attn_b_W_g"]),
            (w["b_g"][:], d["L0_attn_b_b_g"].partition_broadcast(P)),
            (w["w_o_r"][:], d["L0_attn_b_W_o"].rearrange("(b p) c -> p b c", p=P)),
            (w["b_o"][:], d["L0_attn_b_b_o"].partition_broadcast(P)),
            (w["Win"][:], d["L0_ffn_Win"]),
            (w["bout"][:], d["L0_ffn_bout"].partition_broadcast(P)),
            (w["mix"][:, 0:1], d["L1_attn_b_time_mix_k"].rearrange("a b c -> c (a b)")),
            (w["mix"][:, 1:2], d["L1_attn_b_time_mix_v"].rearrange("a b c -> c (a b)")),
            (w["mix"][:, 2:3], d["L1_attn_b_time_mix_r"].rearrange("a b c -> c (a b)")),
            (w["decay"][:], d["L1_attn_b_time_decay"].rearrange("(c o) -> c o", o=1)),
            (w["first"][:], d["L1_attn_b_time_first"].rearrange("(c o) -> c o", o=1)),
            (w["ln1_w"][:], d["L1_ffn_ln1_w"].partition_broadcast(P)),
            (w["ln1_b"][:], d["L1_ffn_ln1_b"].partition_broadcast(P)),
            (w["ln2_w"][:], d["L1_ffn_ln2_w"].partition_broadcast(P)),
            (w["ln2_b"][:], d["L1_ffn_ln2_b"].partition_broadcast(P)),
            (w["conv_w"][:], d["L1_ffn_conv_w"].rearrange("c o j -> c (o j)")),
            (w["attn_w"][:], d["L1_ffn_attn_w"]),
            (w["proj_w"][:], d["L1_ffn_proj_w"]),
            (w["router"][:], d["L1_ffn_router_w"]),
            (w["expert_wv"][:], d["L1_ffn_expert_wv"].rearrange("e c f -> c e f")),
            (w["expert_proj"][:], d["L1_ffn_expert_proj"].rearrange("e (b p) c -> p e b c", p=P)),
        ]
        for half in range(2):
            at = slice(half * M0, half * M0 + M0)
            plain += [
                (w["bin"][at, :], d["L0_ffn_bin_"].rearrange("(m o) -> m o", o=1)),
                (w["W1"][at, :], d["L0_ffn_W1"]),
                (w["b1"][at, :], d["L0_ffn_b1"]),
                (w["W2"][at, :], d["L0_ffn_W2"]),
                (w["b2"][at, :], d["L0_ffn_b2"].rearrange("(m o) -> m o", o=1)),
                (w["Wout"][at, :], d["L0_ffn_Wout"]),
            ]
        with nc.Block() as block:

            @block.sync
            def _(sp):
                with nc.allow_non_contiguous_dma(reason="per-channel vectors"):
                    for dst, src in plain:
                        sp.dma_start(dst, src).then_inc(loaded.sem, 16)
                sp.wait_ge(loaded.sem, loaded.at(16 * len(plain)))

            @block.tensor
            def _(pe):
                pe.wait_ge(loaded.sem, loaded.at(16 * len(plain)))
                for b in range(12):
                    ins = nc.tensor.transpose(tp[:, b // 4, (b % 4) * P:(b % 4 + 1) * P], raw[:, b, :], w["ident"][:])
                    if b % 4 == 3:
                        ins.then_inc(turned.sem, 1)

            @block.scalar
            def _(act):
                for n in range(3):
                    act.wait_ge(turned.sem, turned.at(n + 1))
                    nc.scalar.copy(w["wT"][:, 4 * n:4 * n + 4, :].rearrange("p a b -> p (a b)"), tp[:, n, :]).then_inc(kept.sem, 1)

            @block.vector
            def _(dve):
                dve.wait_ge(loaded.sem, loaded.at(16 * len(plain)))
                nc.vector.tensor_copy(w["mask_qk"][:], maskf[:, 0, :]).then_inc(kept.sem, 1)
                nc.vector.tensor_copy(w["mask_kq"][:], maskf[:, 1, :]).then_inc(kept.sem, 1)
                nc.vector.tensor_copy(w["ident16"][:], maskf[:, 2, :]).then_inc(kept.sem, 1)
                nc.vector.memset(w["ones"][:], 1.0).then_inc(kept.sem, 1)

            @block.gpsimd
            def _(pool):
                for n, (name, value) in enumerate((("q_max", 0.0), ("q_exp", 0.0), ("k_max", -1.0), ("k_exp", -1.0))):
                    nc.gpsimd.memset(w[name][64:P, :, :], value).then_inc(padded.sem, 1)
                    pool.wait_ge(padded.sem, padded.at(n + 1))

        loaded.done(16 * len(plain))
        padded.done(4)
        turned.done(3)
        kept.done(7)




def layer_norm(k, src, dst, ident, dst_t=None, affine=None, eps=1e-5):
    nc = k.nc
    with ExitStack() as ctx:
        stats = k.sb("ln_stats", [P, NT, 6], F32, ctx)
        mv = k.sb("ln_mean_var", [P, NT, 2], F32, ctx)
        std = k.sb("ln_std", [P, NT], F32, ctx)
        rstd = k.sb("ln_rstd", [P, NT], F32, ctx)
        tp = k.ps("ln_t", [P, NQ, BANK], ctx)
        step, var_ready, std_ready = k.counter("ln_step"), k.counter("ln_var"), k.counter("ln_std")
        rows, turned, kept = k.counter("ln_rows"), k.counter("ln_turned"), k.counter("ln_kept")
        with nc.Block() as block:

            @block.vector
            def _(dve):
                chain = Chain(dve, step)
                for i in range(NT):
                    ins = nc.vector.bn_stats(stats[:, i, :], src[:, i, :])
                chain(ins)
                for i in range(NT):
                    ins = nc.vector.bn_aggr(mv[:, i, :], stats[:, i, :])
                chain(ins)
                nc.vector.tensor_scalar(std[:], mv[:, :, 1], eps, None, ALU.add).then_inc(var_ready.sem, 1)
                dve.wait_ge(std_ready.sem, std_ready.at(1))
                chain(nc.vector.reciprocal(rstd[:], std[:]))
                for q in range(NQ):
                    for i in range(QC * q, QC * q + QC):
                        ins = nc.vector.tensor_scalar(dst[:, i, :], src[:, i, :], mv[:, i, 0:1], rstd[:, i:i + 1],
                                                      ALU.subtract, ALU.mult)
                    if affine is None:
                        ins.then_inc(rows.sem, 1)
                    else:
                        chain(ins)
                        part = dst[:, QC * q:QC * q + QC, :]
                        chain(nc.vector.tensor_tensor(part, part, bcast(affine[0][:], 1, QC), ALU.mult))
                        nc.vector.tensor_tensor(part, part, bcast(affine[1][:], 1, QC), ALU.add).then_inc(rows.sem, 1)

            @block.scalar
            def _(act):
                act.wait_ge(var_ready.sem, var_ready.at(1))
                nc.scalar.sqrt(std[:], std[:]).then_inc(std_ready.sem, 1)
                if dst_t is not None:
                    for q in range(NQ):
                        act.wait_ge(turned.sem, turned.at(q + 1))
                        nc.scalar.copy(dst_t[:, q * BANK:(q + 1) * BANK], tp[:, q, :]).then_inc(kept.sem, 1)

            @block.tensor
            def _(pe):
                if dst_t is not None:
                    for q in range(NQ):
                        pe.wait_ge(rows.sem, rows.at(q + 1))
                        for i in range(QC):
                            ins = nc.tensor.transpose(tp[:, q, i * P:(i + 1) * P], dst[:, QC * q + i, :], ident[:])
                        ins.then_inc(turned.sem, 1)

        step.done(2 + 1 + (0 if affine is None else 2 * NQ))
        var_ready.done(1)
        std_ready.done(1)
        rows.done(NQ)
        if dst_t is not None:
            turned.done(NQ)
            kept.done(NQ)


def transpose_stage(k, jobs, ident):
    nc = k.nc
    with ExitStack() as ctx:
        tp = k.ps("turn", [P, 4, BANK], ctx)
        turned, kept = k.counter("turned"), k.counter("turn_kept")
        units = [(src, dst, q) for src, dst in jobs for q in range(NQ)]
        with nc.Block() as block:

            @block.tensor
            def _(pe):
                for n, (src, dst, q) in enumerate(units):
                    if n >= 4:
                        pe.wait_ge(kept.sem, kept.at(n - 3))
                    for i in range(QC):
                        ins = nc.tensor.transpose(tp[:, n % 4, i * P:(i + 1) * P], src[:, QC * q + i, :], ident[:])
                    ins.then_inc(turned.sem, 1)

            @block.scalar
            def _(act):
                for n, (src, dst, q) in enumerate(units):
                    act.wait_ge(turned.sem, turned.at(n + 1))
                    nc.scalar.copy(dst[:, q * BANK:(q + 1) * BANK], tp[:, n % 4, :]).then_inc(kept.sem, 1)

        turned.done(len(units))
        kept.done(len(units))


def project_stage(k, jobs, add_to=False):
    nc = k.nc
    with ExitStack() as ctx:
        out = k.ps("project", [P, 8, BANK], ctx)
        ready, kept = k.counter("projected"), k.counter("project_kept")
        units = [(job, i) for i in range(NT) for job in jobs]
        with nc.Block() as block:

            @block.tensor
            def _(pe):
                for n, ((chunks, dst, bias), i) in enumerate(units):
                    if n >= 8:
                        pe.wait_ge(kept.sem, kept.at(n - 7))
                    width = chunks[0][1].shape[-1]
                    for c, (x_t, wgt) in enumerate(chunks):
                        ins = nc.tensor.matmul(out[:, n % 8, 0:width], x_t[:, i * P:(i + 1) * P], wgt,
                                               start=(c == 0), stop=(c == len(chunks) - 1))
                    ins.then_inc(ready.sem, 1)

            @block.vector
            def _(dve):
                for n, ((chunks, dst, bias), i) in enumerate(units):
                    width = chunks[0][1].shape[-1]
                    dve.wait_ge(ready.sem, ready.at(n + 1))
                    o = out[:, n % 8, 0:width]
                    if add_to:
                        ins = nc.vector.tensor_tensor(dst[:, i, :], o, dst[:, i, :], ALU.add)
                    elif bias is not None:
                        ins = nc.vector.tensor_tensor(dst[:, i, :], o, bias, ALU.add)
                    else:
                        ins = nc.vector.tensor_copy(dst[:, i, :], o)
                    ins.then_inc(kept.sem, 1)

        ready.done(len(units))
        kept.done(len(units))


def rope_stage(k, w, qkv, norm):
    nc = k.nc
    half = D // 2
    with ExitStack() as ctx:
        names = ("q", "k")
        work = [k.sb(f"rope_{n}", [P, NT, C], F32, ctx) for n in names]
        ms = [k.sb(f"rms_{n}", [P, NT * H], F32, ctx) for n in names]
        done = [k.counter(f"rope_{n}_step") for n in names]
        ms_ready, std_ready = k.counter("rms_ready"), k.counter("rms_std")
        counts = [0, 0]

        def rotate(eng, s):
            chain = Chain(eng, done[s])
            x = qkv[:, :, s * C:(s + 1) * C]
            xs = x.rearrange("p t (h d) -> p t h d", d=D)
            ws = work[s][:].rearrange("p t (h d) -> p t h d", d=D)
            eng.tensor_tensor(ws[:, :, :, 0:half], xs[:, :, :, half:], bcast(w["sin"][:, :, 0:half], 2, H), ALU.mult)
            chain(eng.tensor_tensor(ws[:, :, :, half:], xs[:, :, :, 0:half], bcast(w["sin"][:, :, half:], 2, H), ALU.mult))
            chain(eng.tensor_tensor(xs, xs, bcast(w["cos"][:], 2, H), ALU.mult))
            chain(eng.tensor_tensor(x, x, work[s][:], ALU.add))
            return chain

        with nc.Block() as block:

            @block.vector
            def _(dve):
                chain = rotate(nc.vector, 0)
                if norm:
                    for s in range(2):
                        if s == 1:
                            dve.wait_ge(done[1].sem, done[1].at(4))
                        else:
                            chain(nc.vector.tensor_tensor(work[0][:], qkv[:, :, 0:C], qkv[:, :, 0:C], ALU.mult))
                        chain(nc.vector.tensor_reduce(ms[s][:], work[s][:].rearrange("p t (h d) -> p (t h) d", d=D), AX.X, ALU.add))
                        nc.vector.tensor_scalar(ms[s][:], ms[s][:], 1.0 / D, 1e-6, ALU.mult, ALU.add).then_inc(ms_ready.sem, 1)
                    for s in range(2):
                        dve.wait_ge(std_ready.sem, std_ready.at(s + 1))
                        chain(nc.vector.reciprocal(ms[s][:], ms[s][:]))
                        xs = qkv[:, :, s * C:(s + 1) * C].rearrange("p t (h d) -> p t h d", d=D)
                        r = bcast(ms[s][:].rearrange("p (t h) -> p t h", h=H), 3, D)
                        chain(nc.vector.tensor_tensor(xs, xs, r, ALU.mult))
                        xt = qkv[:, :, s * C:(s + 1) * C].rearrange("p t (h d) -> p t h d", d=D)
                        for i in range(NT):
                            ins = nc.vector.tensor_tensor(xt[:, i], xt[:, i], bcast(w["qn" if s == 0 else "kn"][:], 1, H), ALU.mult)
                        chain(ins)
                counts[0] = chain.n

            @block.gpsimd
            def _(pool):
                chain = rotate(nc.gpsimd, 1)
                if norm:
                    chain(nc.gpsimd.tensor_tensor(work[1][:], qkv[:, :, C:2 * C], qkv[:, :, C:2 * C], ALU.mult))
                counts[1] = chain.n

            if norm:
                @block.scalar
                def _(act):
                    for s in range(2):
                        act.wait_ge(ms_ready.sem, ms_ready.at(s + 1))
                        nc.scalar.sqrt(ms[s][:], ms[s][:]).then_inc(std_ready.sem, 1)

        done[0].done(counts[0])
        done[1].done(counts[1])
        if norm:
            ms_ready.done(2)
            std_ready.done(2)




def split_stage(k, w, qkv, parts_dram):
    nc = k.nc
    with ExitStack() as ctx:
        parts = [k.sb(f"parts_{n}", [P, PARTS, NT, C], BF16, ctx) for n in "qk"]
        rest = [k.sb(f"rest_{n}", [P, NT, C], F32, ctx) for n in "qk"]
        turned_sb = [k.sb(f"parts_t_{n}", [P, PARTS, T], BF16, ctx) for n in "qk"]
        tp = k.ps("parts_turn", [P, 4, 2 * BANK], ctx, BF16)
        rounded = [k.counter(f"part_rounded_{n}") for n in "qk"]
        subbed = [k.counter(f"part_rest_{n}") for n in "qk"]
        turned, kept, stored = k.counter("parts_turned"), k.counter("parts_kept"), k.counter("parts_stored")
        half = 2 * QC
        units = [(s, a, u) for a in range(PARTS) for s in range(2) for u in range(NT // half)]
        with nc.Block() as block:

            def subtract(eng, s):
                x = qkv[:, :, s * C:(s + 1) * C]
                eng.wait_ge(rounded[s].sem, rounded[s].at(1))
                eng.tensor_tensor(rest[s][:], x, parts[s][:, 0], ALU.subtract).then_inc(subbed[s].sem, 1)
                eng.wait_ge(rounded[s].sem, rounded[s].at(2))
                eng.tensor_tensor(parts[s][:, 2], rest[s][:], parts[s][:, 1], ALU.subtract).then_inc(subbed[s].sem, 1)

            @block.vector
            def _(dve):
                subtract(nc.vector, 0)

            @block.gpsimd
            def _(pool):
                subtract(nc.gpsimd, 1)

            @block.scalar
            def _(act):
                for s in range(2):
                    nc.scalar.copy(parts[s][:, 0], qkv[:, :, s * C:(s + 1) * C]).then_inc(rounded[s].sem, 1)
                for s in range(2):
                    act.wait_ge(subbed[s].sem, subbed[s].at(1))
                    nc.scalar.copy(parts[s][:, 1], rest[s][:]).then_inc(rounded[s].sem, 1)
                for n, (s, a, u) in enumerate(units):
                    act.wait_ge(turned.sem, turned.at(n + 1))
                    nc.scalar.copy(turned_sb[s][:, a, u * 2 * BANK:(u + 1) * 2 * BANK], tp[:, n % 4, :]).then_inc(kept.sem, 1)

            @block.tensor
            def _(pe):
                for n, (s, a, u) in enumerate(units):
                    if a < 2:
                        pe.wait_ge(rounded[s].sem, rounded[s].at(a + 1))
                    else:
                        pe.wait_ge(subbed[s].sem, subbed[s].at(2))
                    if n >= 4:
                        pe.wait_ge(kept.sem, kept.at(n - 3))
                    for i in range(half):
                        ins = nc.tensor.transpose(tp[:, n % 4, i * P:(i + 1) * P], parts[s][:, a, u * half + i, :], w["ident16"][:])
                    ins.then_inc(turned.sem, 1)

            @block.sync
            def _(sp):
                for n, (s, a, u) in enumerate(units):
                    if u == NT // half - 1:
                        sp.wait_ge(kept.sem, kept.at(n + 1))
                        sp.dma_start(parts_dram[s][a], turned_sb[s][:, a, :]).then_inc(stored.sem, 16)
                sp.wait_ge(stored.sem, stored.at(16 * 2 * PARTS))

        for s in range(2):
            rounded[s].done(2)
            subbed[s].done(2)
        turned.done(len(units))
        kept.done(len(units))
        stored.done(16 * 2 * PARTS)


def attention_stage(k, w, v, parts_dram, scale, y):
    nc = k.nc
    MAXU = [(i, c) for i in range(NT) for c in range(i // QC + 1)]
    EXPU = []
    for j in range(NQ):
        for u in range(2 * j):
            EXPU.append((j, [(2 * u, 0), (2 * u + 1, 0)]))
        EXPU.append((j, [(QC * j, 0), (QC * j + 1, 1)]))
        EXPU.append((j, [(QC * j + 2, 2), (QC * j + 3, 3)]))
    NM, NE = len(MAXU), len(EXPU)
    STATU = NM + 2
    PRE = 2 * NM + 1
    RING, PSLOTS = 3, 4
    assert STATU % RING == 0 and NE % PSLOTS == 0 and NE % 2 == 0
    M_AT = {e: (2 * e, 2 * e + 2) for e in range(NE)}
    SHIFT_AT = 2
    LOOPED = H - 2
    TAIL = PRE + LOOPED * STATU
    counts = []
    with ExitStack() as ctx:
        qm, km, qe, ke = w["q_max"], w["k_max"], w["q_exp"], w["k_exp"]
        probs = k.sb("probs", [P, PSLOTS, 2 * BANK], F32, ctx)
        vh = k.sb("v_head", [P, 2, NT, 32], F32, ctx)
        mpart = k.sb("max_part", [P, 2, NT, NQ], F32, ctx)
        mx = k.sb("row_max", [P, 2, NT], F32, ctx)
        mxb = k.sb("row_max_parts", [P, 2, SHIFT * NT], BF16, ctx)
        mxt = k.sb("row_max_turned", [SHIFT * NT, 2, P], BF16, ctx)
        ot = k.sb("out_turned", [P, 2, BANK], F32, ctx)
        rden = k.sb("inv_denominator", [P, 2, NT], F32, ctx)
        ring = [k.ps(f"stat{n}", [P, BANK], ctx) for n in range(RING)]
        sc = [k.ps(f"score{n}", [P, 2 * BANK], ctx) for n in range(2)]
        acc = k.ps("pv", [P, BANK], ctx)

        m_loaded = [k.counter(f"max_rows_loaded{n}") for n in range(2)]
        e_loaded = [k.counter(f"exp_rows_loaded{n}") for n in range(2)]
        shift_in = [k.counter(f"shift_rows_loaded{n}") for n in range(2)]
        stat_full, stat_used = k.counter("stat_bank_full"), k.counter("stat_bank_used")
        max_step, max_ready = k.counter("max_step"), k.counter("row_max_ready")
        scored, expd, pv_done = k.counter("scores_ready"), k.counter("probs_ready"), k.counter("pv_done")
        out_copied, v_ready = k.counter("pv_copied_out"), k.counter("v_head_ready")
        q_rows, k_rows = (parts_dram[s].rearrange("a (h d) t -> h a d t", d=D) for s in range(2))

        def load_rows(sp, qt, kt, par, h, loaded):
            for a in range(PARTS):
                at = slice(a * PARTS * D, (a + 1) * PARTS * D)
                for b in range(PARTS):
                    r = a * PARTS * D + b * D
                    sp.dma_start(qt[r:r + D, par, :], q_rows[h, a]).then_inc(loaded.sem, 16)
                sp.dma_start(kt[at, par, :], k_rows[h]).then_inc(loaded.sem, 16)

        NL = (PARTS + 1) * PARTS * 16

        with nc.Block() as block:

            @block.sync
            def _(sp):
                def load_max(h, par):
                    load_rows(sp, qm, km, par, h, m_loaded[par])

                def load_exp(h, par, prev):
                    if prev is not None:
                        sp.wait_ge(scored.sem, scored.at(NE * prev + NE))
                    load_rows(sp, qe, ke, par, h, e_loaded[par])

                def load_shift(h, par, unit):
                    sp.wait_ge(stat_used.sem, stat_used.at(unit))
                    for n in range(SHIFT):
                        r = KROWS + n
                        sp.dma_start(qe[r:r + 1, par, :].rearrange("o (i q) -> o i q", q=P),
                                     mxt[n * NT:(n + 1) * NT, par, :]).then_inc(shift_in[par].sem, 16)

                load_max(0, 0)
                load_max(1, 1)
                load_exp(0, 0, None)
                sp.wait_ge(stat_full.sem, stat_full.at(NM))
                load_max(2, 0)
                load_shift(0, 0, NM + 1)

                def body(h, par, max_load=True, prev=True, shift_at=2 * SHIFT_AT):
                    nxt = 1 - par
                    if max_load:
                        if isinstance(h, int) and h == 0:
                            sp.wait_ge(stat_full.sem, stat_full.at(PRE))
                        else:
                            sp.wait_ge(stat_full.sem, stat_full.at(h * STATU + (PRE + NM + 1 - STATU)))
                        load_max(h + 3, nxt)
                    load_exp(h + 1, nxt, h - 1 if prev else None)
                    load_shift(h + 1, nxt, h * STATU + (PRE + shift_at + 1))

                body(0, 0, prev=False)
                body(1, 1)
                with sp.Fori(1, 6) as i:
                    for par in range(2):
                        body(2 * i + par, par)
                body(12, 0)
                body(13, 1, max_load=False)
                body(14, 0, max_load=False, shift_at=0)

            @block.gpsimd
            def _(pool):
                nc.gpsimd.memset(vh[:], 0.0).then_inc(v_ready.sem, 1)
                pool.wait_ge(v_ready.sem, v_ready.at(1))
                nc.gpsimd.memset(vh[:, :, :, D:D + 1], 1.0).then_inc(v_ready.sem, 1)
                pool.wait_ge(v_ready.sem, v_ready.at(2))

                def gather(h, par):
                    nc.gpsimd.tensor_copy(vh[:, par, :, 0:D], v[:, :, bass.ds(2 * C + h * D, D)]).then_inc(v_ready.sem, 1)

                gather(0, 0)
                gather(1, 1)
                with pool.Fori(1, H // 2) as i:
                    for par in range(2):
                        h = 2 * i + par
                        pool.wait_ge(pv_done.sem, pv_done.at(NE * h - NE))
                        gather(h, par)

            @block.scalar
            def _(act):
                def body(h, par, first=False, first_two=False):
                    for e, (j, tiles) in enumerate(EXPU):
                        n = NE * h + e
                        act.wait_ge(scored.sem, scored.at(n + 1))
                        if not first or e >= PSLOTS:
                            act.wait_ge(pv_done.sem, pv_done.at(n + 1 - PSLOTS))
                        width = sum(BANK - f * P for _, f in tiles)
                        nc.scalar.activation(probs[:, e % PSLOTS, 0:width], sc[e % 2][:, 0:width], ACT.Exp,
                                             scale=scale).then_inc(expd.sem, 1)
                    act.wait_ge(pv_done.sem, pv_done.at(NE * h + NE))
                    if not first_two:
                        act.wait_ge(stat_full.sem, stat_full.at(h * STATU + (PRE - STATU)))
                    nc.scalar.copy(ot[:, par, :], acc[:]).then_inc(out_copied.sem, 1)

                body(0, 0, first=True, first_two=True)
                body(1, 1, first_two=True)
                with act.Fori(1, H // 2) as i:
                    for par in range(2):
                        body(2 * i + par, par)

            @block.tensor
            def _(pe):
                def max_unit(n, unit, par):
                    i, c = MAXU[unit]
                    width = BANK if c < i // QC else (i % QC + 1) * P
                    out = ring[n % RING]
                    last = nc.tensor.matmul(out[:, 0:width], qm[:, par, i * P:(i + 1) * P],
                                            km[:, par, c * BANK:c * BANK + width], start=True, stop=c < i // QC)
                    if c == i // QC:
                        last = nc.tensor.matmul(out[:, width - P:width], w["ident16"][:], w["mask_qk"][:], start=False, stop=True)
                    last.then_inc(stat_full.sem, 1)

                def shift_unit(n, par):
                    out = ring[n % RING]
                    nc.tensor.transpose(out[0:SHIFT * NT, 0:P // 2].bitcast(BF16), mxb[:, par, :], w["ident16"][:]).then_inc(stat_full.sem, 1)

                def out_unit(n, par):
                    for j in range(NQ):
                        last = nc.tensor.transpose(ring[n % RING][:, j * P:(j + 1) * P], ot[:, par, j * P:(j + 1) * P], w["ident"][:])
                    last.then_inc(stat_full.sem, 1)

                def scores(e, par):
                    j, tiles = EXPU[e]
                    at = 0
                    for kt, f in tiles:
                        width = BANK - f * P
                        out = sc[e % 2][:, at:at + width]
                        diag = kt >= QC * j
                        last = nc.tensor.matmul(out, ke[:, par, kt * P:(kt + 1) * P],
                                                qe[:, par, j * BANK + f * P:(j + 1) * BANK],
                                                start=True, stop=not diag)
                        if diag:
                            last = nc.tensor.matmul(out[:, 0:P], w["ident16"][:], w["mask_kq"][:], start=False, stop=True)
                        at += width
                    last.then_inc(scored.sem, 1)

                def pv(e, par):
                    j, tiles = EXPU[e]
                    at = 0
                    for kt, f in tiles:
                        for c in range(f, QC):
                            last = nc.tensor.matmul(acc[32 * c:32 * c + 32, j * P:(j + 1) * P], vh[:, par, kt, :],
                                                    probs[:, e % PSLOTS, at:at + P], start=kt == 0, stop=kt == QC * j + c,
                                                    tile_position=(0, 32 * c))
                            at += P
                    last.then_inc(pv_done.sem, 1)

                pe.wait_ge(m_loaded[0].sem, m_loaded[0].at(NL))
                n = 0
                for u in range(NM):
                    if n >= RING:
                        pe.wait_ge(stat_used.sem, stat_used.at(n + 1 - RING))
                    max_unit(n, u, 0)
                    n += 1
                pe.wait_ge(max_ready.sem, max_ready.at(1))
                pe.wait_ge(stat_used.sem, stat_used.at(n + 1 - RING))
                shift_unit(n, 0)
                n += 1
                pe.wait_ge(m_loaded[1].sem, m_loaded[1].at(NL))
                for u in range(NM):
                    pe.wait_ge(stat_used.sem, stat_used.at(n + 1 - RING))
                    max_unit(n, u, 1)
                    n += 1
                assert n == PRE
                pe.wait_ge(e_loaded[0].sem, e_loaded[0].at(NL))
                pe.wait_ge(shift_in[0].sem, shift_in[0].at(SHIFT * 16))
                scores(0, 0)
                scores(1, 0)

                def body(h, turn, par, base, ring_at, maxes=True, more=True):
                    nxt = 1 - par
                    n = 0

                    def free_bank():
                        pe.wait_ge(stat_used.sem, stat_used.at(base + (n + 1 - RING)))

                    pe.wait_ge(v_ready.sem, v_ready.at(h + 3))
                    if maxes:
                        pe.wait_ge(m_loaded[par].sem, m_loaded[par].at(turn * NL + 2 * NL))
                    for e in range(NE):
                        pe.wait_ge(expd.sem, expd.at(h * NE + (e + 1)))
                        if e + 2 < NE:
                            scores(e + 2, par)
                        elif more:
                            if e + 2 == NE:
                                pe.wait_ge(e_loaded[nxt].sem, e_loaded[nxt].at(turn * NL + (1 + par) * NL))
                                pe.wait_ge(shift_in[nxt].sem, shift_in[nxt].at(turn * (SHIFT * 16) + (1 + par) * SHIFT * 16))
                            scores(e + 2 - NE, nxt)
                        pv(e, par)
                        if e == SHIFT_AT and more:
                            pe.wait_ge(max_ready.sem, max_ready.at(h + 2))
                            free_bank()
                            shift_unit(ring_at + n, nxt)
                            n += 1
                        if maxes:
                            for u in range(*M_AT[e]):
                                free_bank()
                                max_unit(ring_at + n, u, par)
                                n += 1
                    pe.wait_ge(out_copied.sem, out_copied.at(h + 1))
                    free_bank()
                    out_unit(ring_at + n, par)

                with pe.Fori(0, LOOPED // 2) as i:
                    for par in range(2):
                        body(2 * i + par, i, par, i * (2 * STATU) + (PRE + par * STATU), PRE)
                body(H - 2, H // 2 - 1, 0, TAIL, TAIL, maxes=False)
                body(H - 1, H // 2 - 1, 1, TAIL + 2, TAIL + 2, maxes=False, more=False)

            @block.vector
            def _(dve):
                chain = Chain(dve, max_step)

                def max_unit(n, at, unit, par):
                    i, c = MAXU[unit]
                    width = BANK if c < i // QC else (i % QC + 1) * P
                    dve.wait_ge(stat_full.sem, stat_full.at(n + 1))
                    nc.vector.reduce_max(mpart[:, par, i, c:c + 1], ring[at % RING][:, 0:width], AX.X).then_inc(stat_used.sem, 1)

                def row_max(n, par, turn):
                    dve.wait_ge(stat_used.sem, stat_used.at(n))
                    step(nc.vector.tensor_reduce(mx[:, par, :], mpart[:, par], AX.X, ALU.max))
                    step(nc.vector.tensor_copy(mxb[:, par, 0:NT], mx[:, par, :]))
                    nc.vector.tensor_tensor(mxb[:, par, NT:], mx[:, par, :], mxb[:, par, 0:NT], ALU.subtract).then_inc(max_ready.sem, 1)

                steps = [0, 0]

                def step(ins):
                    steps[1] += 1
                    ins.then_inc(max_step.sem, 1)
                    dve.wait_ge(max_step.sem, max_step.at(steps[0] + steps[1]))

                def shift_unit(n, at, par, earlier):
                    if earlier is not None:
                        dve.wait_ge(shift_in[par].sem, shift_in[par].at(earlier))
                    dve.wait_ge(stat_full.sem, stat_full.at(n + 1))
                    nc.vector.tensor_copy(mxt[:, par, :], ring[at % RING][0:SHIFT * NT, 0:P // 2].bitcast(BF16)).then_inc(stat_used.sem, 1)

                def out_unit(n, at, h, par):
                    dve.wait_ge(stat_full.sem, stat_full.at(n + 1))
                    o = ring[at % RING][:].rearrange("p (t x) -> p t x", x=32)
                    step(nc.vector.reciprocal(rden[:, par, :], o[:, :, D]))
                    nc.vector.tensor_tensor(y[:, :, bass.ds(h * D, D)], o[:, :, 0:D], bcast(rden[:, par, :], 2, D),
                                            ALU.mult).then_inc(stat_used.sem, 1)

                nc.vector.memset(mpart[:], -3e38).then_inc(max_step.sem, 1)
                steps[1] = 1
                dve.wait_ge(max_step.sem, max_step.at(1))
                n = 0
                for u in range(NM):
                    max_unit(n, n, u, 0)
                    n += 1
                row_max(n, 0, 0)
                shift_unit(n, n, 0, None)
                n += 1
                for u in range(NM):
                    max_unit(n, n, u, 1)
                    n += 1
                row_max(n, 1, 0)

                def body(h, par, base, ring_at, earlier, maxes=True, more=True):
                    n = 0
                    for e in range(NE):
                        if e == SHIFT_AT and more:
                            shift_unit(base + n, ring_at + n, 1 - par, earlier)
                            n += 1
                        if maxes:
                            for u in range(*M_AT[e]):
                                max_unit(base + n, ring_at + n, u, par)
                                n += 1
                    if maxes:
                        row_max(base + n, par, None)
                    out_unit(base + n, ring_at + n, h, par)

                first_steps = steps[1]
                with dve.Fori(0, LOOPED // 2) as i:
                    for par in range(2):
                        steps[0], steps[1] = i * (2 * 3) + first_steps, par * 3
                        body(2 * i + par, par, i * (2 * STATU) + (PRE + par * STATU), PRE,
                             i * (SHIFT * 16) + par * SHIFT * 16)
                steps[0], steps[1] = first_steps + LOOPED * 3, 0
                body(H - 2, 0, TAIL, TAIL, (H // 2 - 1) * SHIFT * 16, maxes=False)
                body(H - 1, 1, TAIL + 2, TAIL + 2, None, maxes=False, more=False)
                counts.append(steps[0] + steps[1])

        for par in range(2):
            m_loaded[par].done(NL * H // 2)
            e_loaded[par].done(NL * H // 2)
            shift_in[par].done(SHIFT * 16 * H // 2)
        stat_full.done(TAIL + 3)
        stat_used.done(TAIL + 3)
        max_step.done(counts[0])
        max_ready.done(H)
        scored.done(NE * H)
        expd.done(NE * H)
        pv_done.done(NE * H)
        out_copied.done(H)
        v_ready.done(2 + H)




def spline_ffn_stage(k, w, xn_t, x):
    nc = k.nc
    HALF = T // 2
    with ExitStack() as ctx:
        s2 = k.sb("spline_in", [P, HALF], F32, ctx)
        knot = k.sb("spline_knot", [P, 4, HALF], F32, ctx)
        g = k.sb("spline_sum", [P, 2, HALF], F32, ctx)
        sp_in = k.ps("spline_in_ps", [P, 2, BANK], ctx)
        out = k.ps("spline_out_ps", [P, 4, BANK], ctx)
        fed, s_ready, knots, summed = k.counter("spline_fed"), k.counter("spline_s"), k.counter("spline_knots"), k.counter("spline_summed")
        out_ready, biased, out_used = k.counter("spline_out"), k.counter("spline_biased"), k.counter("spline_out_used")
        with nc.Block() as block:

            @block.tensor
            def _(pe):
                for c in range(2):
                    for half in range(2):
                        ins = nc.tensor.matmul(sp_in[half * M0:half * M0 + M0, c, :], w["Win"][:],
                                               xn_t[:, half * HALF + c * BANK:half * HALF + (c + 1) * BANK], start=True, stop=True,
                                               tile_position=(0, half * M0))
                    ins.then_inc(fed.sem, 1)
                pe.wait_ge(summed.sem, summed.at(INNER))
                for q in range(NQ):
                    half = q // 2
                    at = slice(half * M0, half * M0 + M0)
                    for i in range(QC):
                        t0 = (q % 2) * BANK + i * P
                        ins = nc.tensor.matmul(out[:, q, i * P:(i + 1) * P], g[at, (INNER - 1) % 2, t0:t0 + P], w["Wout"][at, :],
                                               start=True, stop=True)
                    ins.then_inc(out_ready.sem, 1)

            @block.scalar
            def _(act):
                for c in range(2):
                    act.wait_ge(fed.sem, fed.at(c + 1))
                    nc.scalar.activation(s2[:, c * BANK:(c + 1) * BANK], sp_in[:, c, :], ACT.Identity,
                                         bias=w["bin"][:, 0:1]).then_inc(s_ready.sem, 1)
                act.wait_ge(s_ready.sem, s_ready.at(2))
                for h in range(INNER):
                    if h >= 4:
                        act.wait_ge(summed.sem, summed.at(h - 3))
                    nc.scalar.activation(knot[:, h % 4, :], s2[:], ACT.Relu, bias=w["b1"][:, h:h + 1],
                                         scale=w["W1"][:, h:h + 1]).then_inc(knots.sem, 1)

            @block.gpsimd
            def _(pool):
                nc.gpsimd.tensor_tensor(x[:], x[:], bcast(w["bout"][:], 1, NT), ALU.add).then_inc(biased.sem, 1)

            @block.vector
            def _(dve):
                for h in range(INNER):
                    dve.wait_ge(knots.sem, knots.at(h + 1))
                    if h == 0:
                        ins = nc.vector.tensor_scalar(g[:, 0, :], knot[:, 0, :], w["W2"][:, 0:1], w["b2"][:, 0:1], ALU.mult, ALU.add)
                    else:
                        dve.wait_ge(summed.sem, summed.at(h))
                        ins = nc.vector.scalar_tensor_tensor(g[:, h % 2, :], knot[:, h % 4, :], w["W2"][:, h:h + 1],
                                                             g[:, (h - 1) % 2, :], ALU.mult, ALU.add)
                    ins.then_inc(summed.sem, 1)
                dve.wait_ge(biased.sem, biased.at(1))
                for q in range(NQ):
                    dve.wait_ge(out_ready.sem, out_ready.at(q + 1))
                    part = x[:, QC * q:QC * q + QC, :]
                    nc.vector.tensor_tensor(part, out[:, q, :].rearrange("p (i c) -> p i c", c=C), part, ALU.add).then_inc(out_used.sem, 1)

        fed.done(2)
        s_ready.done(2)
        knots.done(INNER)
        summed.done(INNER)
        out_ready.done(NQ)
        biased.done(1)
        out_used.done(NQ)




def chunk_stage(k, w, kk, v, q_t, k_t, width, keep, out, inner=True):
    nc = k.nc
    VW = H * width
    NB = H * P // BANK
    HP = H // 2
    SLOTS = 4
    with ExitStack() as ctx:
        qts = k.sb("tile_q_t", [P, SLOTS, P], F32, ctx)
        ks = k.sb("tile_k", [P, SLOTS, P], F32, ctx)
        vs = k.sb("tile_v", [P, SLOTS, H, 32 if inner else width], F32, ctx)
        state = k.sb("state", [P, SLOTS, VW], F32, ctx)
        o_ps = [k.ps(f"tile_out_ps{n}", [P, BANK], ctx) for n in range(2)]
        u_ps = k.ps("state_ps", [P, BANK], ctx)
        if inner:
            kts = k.sb("tile_k_t", [P, SLOTS, P], F32, ctx)
            qx = k.sb("tile_q_heads", [P, SLOTS, H, P], F32, ctx)
            sm = k.sb("tile_scores", [P, 2, NB, BANK], F32, ctx)
            ot = k.sb("tile_out_turned", [P, BANK], F32, ctx)
            pv_ps = k.ps("tile_pv_ps", [P, BANK], ctx)
            st_ps = [k.ps(f"tile_scores_ps{n}", [P, BANK], ctx) for n in range(NB)]
        staged, masked, s_full = k.counter("tile_staged"), k.counter("tile_masked"), k.counter("tile_scored")
        o_ready, o_used, u_ready, u_kept = k.counter("tile_out"), k.counter("tile_out_used"), k.counter("state_grown"), k.counter("state_kept")
        spread_act, cleared = k.counter("tile_spread_act"), k.counter("tile_v_cleared")
        pv_ready, pv_copied = k.counter("tile_pv"), k.counter("tile_pv_copied")
        NS = 5 if inner else 3
        with nc.Block() as block:

            @block.gpsimd
            def _(pool):
                def body(i, slot, first=False):
                    if not first:
                        pool.wait_ge(o_ready.sem, o_ready.at(i - (SLOTS - 1)))
                    nc.gpsimd.tensor_copy(qts[:, slot, :], q_t[:, bass.ds(i * P, P)]).then_inc(staged.sem, 1)
                    if inner:
                        nc.gpsimd.tensor_copy(kts[:, slot, :], k_t[:, bass.ds(i * P, P)]).then_inc(staged.sem, 1)
                        pool.wait_ge(staged.sem, staged.at(i * NS + 1))
                        nc.gpsimd.tensor_tensor(qx[:, slot, 0:HP, :], bcast(qts[:, slot, :], 1, HP), bcast(w["headmask"][:, 0:HP], 2, P), ALU.mult).then_inc(staged.sem, 1)
                    nc.gpsimd.tensor_copy(ks[:, slot, :], kk[:, bass.ds(i, 1), :]).then_inc(staged.sem, 1)
                    nc.gpsimd.tensor_copy(vs[:, slot, :, 0:width], v[:, bass.ds(i, 1), :].rearrange("p o (h e) -> p (o h) e", e=width)).then_inc(staged.sem, 1)

                if inner:
                    nc.gpsimd.memset(vs[:], 0.0).then_inc(cleared.sem, 1)
                    pool.wait_ge(cleared.sem, cleared.at(1))
                for slot in range(SLOTS):
                    body(slot, slot, first=True)
                with pool.Fori(1, NT // SLOTS) as n:
                    for slot in range(SLOTS):
                        body(SLOTS * n + slot, slot)

            @block.tensor
            def _(pe):
                def scores(i, slot, first=False):
                    pe.wait_ge(staged.sem, staged.at(i * NS + NS))
                    if inner:
                        if not first:
                            pe.wait_ge(masked.sem, masked.at(i * NB))
                        pe.wait_ge(spread_act.sem, spread_act.at(i + 1))
                        for b in range(NB):
                            nc.tensor.matmul(st_ps[b][:], kts[:, slot, :], qx[:, slot, b * QC:(b + 1) * QC, :].rearrange("p j t -> p (j t)"),
                                             start=True, stop=True).then_inc(s_full.sem, 1)
                    pe.wait_ge(u_kept.sem, u_kept.at(i + 1))
                    nc.tensor.matmul(u_ps[:, 0:VW].rearrange("p (h e) -> p h e", e=width), ks[:, slot, :], vs[:, slot, :, 0:width], start=first, stop=True, skip_group_check=True).then_inc(u_ready.sem, 1)

                def within(i, slot, first=False):
                    pe.wait_ge(masked.sem, masked.at(i * NB + NB))
                    if not first:
                        pe.wait_ge(pv_copied.sem, pv_copied.at(i))
                    for h in range(H):
                        g, j = h % QC, h // QC
                        ins = nc.tensor.matmul(pv_ps[32 * g:32 * g + 32, j * P:(j + 1) * P], vs[:, slot, h, :], sm[:, slot % 2, j, g * P:(g + 1) * P],
                                               start=True, stop=True, tile_position=(0, 32 * g))
                    ins.then_inc(pv_ready.sem, 1)

                def finish(i, slot, first_two=False):
                    if not first_two:
                        pe.wait_ge(o_used.sem, o_used.at(i - 1))
                    o = o_ps[slot % 2]
                    ins = nc.tensor.matmul(o[:, 0:VW], qts[:, slot, :], state[:, slot, :], start=True, stop=not inner)
                    if inner:
                        pe.wait_ge(pv_copied.sem, pv_copied.at(i + 1))
                        rows = w["ident"][:].rearrange("p (g e) -> p g e", e=32)[:, :, 0:width]
                        for j in range(H // QC):
                            ins = nc.tensor.matmul(o[:, j * QC * width:(j + 1) * QC * width].rearrange("p (g e) -> p g e", e=width),
                                                   ot[:, j * P:(j + 1) * P], rows, start=False, stop=j == H // QC - 1)
                    ins.then_inc(o_ready.sem, 1)

                def body(i, slot, step=None):
                    scores(i, slot, first=step == 0)
                    if step is None or step >= 2:
                        finish(i - 2, (slot - 2) % SLOTS, first_two=step in (2, 3))
                    if inner and step != 0:
                        within(i - 1, (slot - 1) % SLOTS, first=step == 1)

                for i in range(SLOTS):
                    body(i, i, step=i)
                with pe.Fori(1, NT // SLOTS) as n:
                    for slot in range(SLOTS):
                        body(SLOTS * n + slot, slot)
                finish(NT - 2, SLOTS - 2)
                if inner:
                    within(NT - 1, SLOTS - 1)
                finish(NT - 1, SLOTS - 1)

            @block.vector
            def _(dve):
                nc.vector.memset(state[:, 0, :], 0.0).then_inc(u_kept.sem, 1)

                def body(i, slot, first_two=False, early=False, last=False):
                    par = slot % 2
                    if inner:
                        for b in range(NB):
                            dve.wait_ge(s_full.sem, s_full.at(i * NB + (b + 1)))
                            if b == 0 and not first_two:
                                dve.wait_ge(pv_ready.sem, pv_ready.at(i - 1))
                            nc.vector.tensor_tensor(sm[:, par, b, :].rearrange("p (j t) -> p j t", t=P), st_ps[b][:].rearrange("p (j t) -> p j t", t=P),
                                                    bcast(w["keep_kq"][:], 1, QC), ALU.mult).then_inc(masked.sem, 1)
                    if not last:
                        dve.wait_ge(u_ready.sem, u_ready.at(i + 1))
                        if not early:
                            dve.wait_ge(o_ready.sem, o_ready.at(i - 2))
                        nc.vector.tensor_tensor(state[:, (slot + 1) % SLOTS, :], u_ps[:, 0:VW], keep, ALU.mult).then_inc(u_kept.sem, 1)

                for i in range(SLOTS):
                    body(i, i, first_two=i < 2, early=i < 3)
                with dve.Fori(1, NT // SLOTS - 1) as n:
                    for slot in range(SLOTS):
                        body(SLOTS * n + slot, slot)
                for slot in range(SLOTS):
                    body(NT - SLOTS + slot, slot, last=slot == SLOTS - 1)

            @block.scalar
            def _(act):
                def spread_heads(i, slot):
                    act.wait_ge(staged.sem, staged.at(i * NS + 1))
                    for h in range(HP, H):
                        ins = nc.scalar.activation(qx[:, slot, h, :], qts[:, slot, :], ACT.Copy, scale=w["headmask"][:, h:h + 1])
                    ins.then_inc(spread_act.sem, 1)

                def copy_pv(i, first=False):
                    act.wait_ge(pv_ready.sem, pv_ready.at(i + 1))
                    if not first:
                        act.wait_ge(o_ready.sem, o_ready.at(i))
                    nc.scalar.copy(ot[:], pv_ps[:]).then_inc(pv_copied.sem, 1)

                def take_out(i, par):
                    act.wait_ge(o_ready.sem, o_ready.at(i + 1))
                    nc.scalar.copy(out[:, bass.ds(i, 1), :], o_ps[par][:, 0:VW]).then_inc(o_used.sem, 1)

                if inner:
                    for slot in range(SLOTS):
                        spread_heads(slot, slot)
                def body(i, slot, first=False, more=True):
                    if inner:
                        copy_pv(i, first=first)
                        if more:
                            spread_heads(i + SLOTS, slot)
                    take_out(i, slot % 2)

                body(0, 0, first=True)
                for slot in range(1, SLOTS):
                    body(slot, slot)
                with act.Fori(1, NT // SLOTS - 1) as n:
                    for slot in range(SLOTS):
                        body(SLOTS * n + slot, slot)
                for slot in range(SLOTS):
                    body(NT - SLOTS + slot, slot, more=False)

        staged.done(NS * NT)
        if inner:
            spread_act.done(NT)
            cleared.done(1)
            pv_ready.done(NT)
            pv_copied.done(NT)
            s_full.done(NB * NT)
            masked.done(NB * NT)
        o_ready.done(NT)
        o_used.done(NT)
        u_ready.done(NT)
        u_kept.done(NT)


def linear_features_stage(k, w, qkv, v9):
    nc = k.nc
    with ExitStack() as ctx:
        low = k.sb("elu_exp", [P, NT, 2 * C], F32, ctx)
        clipped, exped, step, v_step = k.counter("elu_clipped"), k.counter("elu_exp"), k.counter("elu_step"), k.counter("v9_step")
        counts = []
        with nc.Block() as block:

            @block.vector
            def _(dve):
                chain = Chain(dve, step)
                nc.vector.tensor_scalar(low[:], qkv[:, :, 0:2 * C], 0.0, None, ALU.min).then_inc(clipped.sem, 1)
                dve.wait_ge(exped.sem, exped.at(1))
                chain(nc.vector.scalar_tensor_tensor(qkv[:, :, 0:2 * C], qkv[:, :, 0:2 * C], 0.0, low[:], ALU.max, ALU.add))
                chain(nc.vector.tensor_scalar(qkv[:, :, 0:C], qkv[:, :, 0:C], float(D) ** -0.5, None, ALU.mult))
                counts.append(chain.n)

            @block.scalar
            def _(act):
                act.wait_ge(clipped.sem, clipped.at(1))
                nc.scalar.activation(low[:], low[:], ACT.Exp).then_inc(exped.sem, 1)

            @block.gpsimd
            def _(pool):
                nc.gpsimd.memset(v9[:], 1.0).then_inc(v_step.sem, 1)
                pool.wait_ge(v_step.sem, v_step.at(1))
                for i in range(NT):
                    ins = nc.gpsimd.tensor_copy(v9[:, i, :].rearrange("p (h e) -> p h e", e=D + 1)[:, :, 0:D],
                                                qkv[:, i, 2 * C:3 * C].rearrange("p (h d) -> p h d", d=D))
                ins.then_inc(v_step.sem, 1)

        clipped.done(1)
        exped.done(1)
        step.done(counts[0])
        v_step.done(2)


def linear_divide_stage(k, num, y):
    nc = k.nc
    with ExitStack() as ctx:
        den = k.sb("linear_den", [P, NT, H], F32, ctx)
        step = k.counter("linear_divide")
        counts = []
        with nc.Block() as block:

            @block.vector
            def _(dve):
                chain = Chain(dve, step)
                n = num[:].rearrange("p t (h e) -> p t h e", e=D + 1)
                chain(nc.vector.tensor_scalar(den[:], n[:, :, :, D], 1e-6, None, ALU.max))
                chain(nc.vector.reciprocal(den[:], den[:]))
                chain(nc.vector.tensor_tensor(y.rearrange("p t (h d) -> p t h d", d=D), n[:, :, :, 0:D], bcast(den[:], 3, D), ALU.mult))
                counts.append(chain.n)

        step.done(counts[0])




def retention_decay_stage(k, w, qkv):
    nc = k.nc
    done = k.counter("decayed")
    with nc.Block() as block:

        def scale(eng, s, table):
            x = qkv[:, :, s * C:(s + 1) * C].rearrange("p t (h d) -> p t h d", d=D)
            eng.tensor_tensor(x, x, bcast(table[:], 3, D), ALU.mult).then_inc(done.sem, 1)

        @block.vector
        def _(dve):
            scale(nc.vector, 0, w["qdecay"])

        @block.gpsimd
        def _(pool):
            scale(nc.gpsimd, 1, w["kdecay"])

    done.done(2)


def retention_heads_stage(k, w, v, parts_dram, part, diag, ret):
    nc = k.nc
    LONG = 2 * BANK
    ACTU = [(i, 0, min(i * P, LONG)) for i in range(5, NT)]
    DVEU = []
    for i in range(1, NT):
        at = 0 if i < 5 else LONG
        while at < i * P:
            DVEU.append((i, at, min(BANK, i * P - at)))
            at += BANK
    ND = NT // QC
    NA, NV = len(ACTU), ND + len(DVEU)
    DRING = 3
    assert NV % DRING == 0
    OW = 32
    with ExitStack() as ctx:
        qm, km = w["q_max"], w["k_max"]
        sm = k.sb("own_scores", [P, 2, T], F32, ctx)
        sa = k.sb("own_positive", [P, 2, T], F32, ctx)
        vh = k.sb("ret_v_head", [P, 2, NT, OW], F32, ctx)
        twice = k.sb("twice_sum", [P, OW], F32, ctx)
        ot = k.sb("own_out_turned", [P, BANK], F32, ctx)
        a_ps = [k.ps(f"abs_act_ps{n}", [P, LONG], ctx) for n in range(2)]
        d_ps = [k.ps(f"abs_dve_ps{n}", [P, BANK], ctx) for n in range(DRING)]
        o_ps = k.ps("own_out_ps", [P, BANK], ctx)
        loaded = [k.counter(f"ret_rows_loaded{n}") for n in range(2)]
        a_full, a_used, d_full, d_used = (k.counter("abs_" + n) for n in ("act_full", "act_used", "dve_full", "dve_used"))
        v_ready, abs_ready = k.counter("ret_v_ready"), k.counter("own_abs_ready")
        o_ready, o_used, cleared = k.counter("own_out_ready"), k.counter("own_out_used"), k.counter("abs_cleared")
        o_copied, o_turned = k.counter("own_out_copied"), k.counter("own_out_turned")
        NL = (PARTS + 1) * PARTS * 16
        q_rows, k_rows = (parts_dram[s].rearrange("a (h d) t -> h a d t", d=D) for s in range(2))
        order = []
        for n in range(NV):
            order += [("a", m) for m in range(n * NA // NV, (n + 1) * NA // NV)]
            order.append(("d", n))
        PV_AT, TURN_AT, READ_AT = 8, 14, 16
        COPY_AT = (PV_AT + 1) * NA // NV
        with nc.Block() as block:

            @block.sync
            def _(sp):
                def body(h, par, first=False):
                    if not first:
                        sp.wait_ge(a_full.sem, a_full.at(h * NA - NA))
                        sp.wait_ge(d_full.sem, d_full.at(h * NV - NV))
                    for a in range(PARTS):
                        at = slice(a * PARTS * D, (a + 1) * PARTS * D)
                        for b in range(PARTS):
                            r = a * PARTS * D + b * D
                            sp.dma_start(qm[r:r + D, par, :], q_rows[h, a]).then_inc(loaded[par].sem, 16)
                        sp.dma_start(km[at, par, :], k_rows[h]).then_inc(loaded[par].sem, 16)

                body(0, 0, first=True)
                body(1, 1, first=True)
                with sp.Fori(1, H // 2) as n:
                    for par in range(2):
                        body(2 * n + par, par)

            @block.gpsimd
            def _(pool):
                nc.gpsimd.memset(part[:], 0.0).then_inc(cleared.sem, 1)
                pool.wait_ge(cleared.sem, cleared.at(1))
                nc.gpsimd.memset(twice[:], 0.0).then_inc(cleared.sem, 1)
                pool.wait_ge(cleared.sem, cleared.at(2))
                nc.gpsimd.memset(twice[:, VD:VD + 1], 2.0).then_inc(cleared.sem, 1)
                pool.wait_ge(cleared.sem, cleared.at(3))
                nc.gpsimd.memset(vh[:], 0.0).then_inc(cleared.sem, 1)
                pool.wait_ge(cleared.sem, cleared.at(4))
                nc.gpsimd.memset(vh[:, :, :, VD:VD + 1], -1.0).then_inc(cleared.sem, 1)
                pool.wait_ge(cleared.sem, cleared.at(5))

                def body(h, par, first=False):
                    if not first:
                        pool.wait_ge(o_ready.sem, o_ready.at(h - 1))
                    pool.wait_ge(d_used.sem, d_used.at(h * NV + ND))
                    nc.gpsimd.tensor_copy(vh[:, par, :, 0:VD], v[:, :, bass.ds(h * VD, VD)]).then_inc(v_ready.sem, 1)
                    nc.gpsimd.tensor_scalar(sa[:, par, :], sm[:, par, :], 0.0, None, ALU.max).then_inc(abs_ready.sem, 1)
                    pool.wait_ge(abs_ready.sem, abs_ready.at(h + 1))

                body(0, 0, first=True)
                body(1, 1, first=True)
                with pool.Fori(1, H // 2) as n:
                    for par in range(2):
                        body(2 * n + par, par)

            @block.tensor
            def _(pe):
                def own_out(h, par, first=False):
                    pe.wait_ge(v_ready.sem, v_ready.at(h + 1))
                    pe.wait_ge(abs_ready.sem, abs_ready.at(h + 1))
                    if not first:
                        pe.wait_ge(o_used.sem, o_used.at(2 * h))
                    for i in range(NT):
                        j, g, at = i // QC, i % QC, slice(i * P, (i + 1) * P)
                        o = o_ps[g * OW:(g + 1) * OW, j * P:(j + 1) * P]
                        nc.tensor.matmul(o, vh[:, par, i, :], sm[:, par, at], start=True, stop=False, tile_position=(0, g * OW))
                        ins = nc.tensor.matmul(o, twice[:], sa[:, par, at], start=False, stop=True, tile_position=(0, g * OW))
                    ins.then_inc(o_ready.sem, 1)

                def turn_out(h):
                    pe.wait_ge(o_copied.sem, o_copied.at(h + 1))
                    for j in range(NQ):
                        ins = nc.tensor.transpose(o_ps[:, j * P:(j + 1) * P], ot[:, j * P:(j + 1) * P], w["ident"][:])
                    ins.then_inc(o_turned.sem, 1)

                def body(h, turn, par, first=False, second=False):
                    pe.wait_ge(loaded[par].sem, loaded[par].at(turn * NL + NL))
                    for kind, n in order:
                        if kind == "a":
                            slot = (par * NA + n) % 2
                            if not first or n >= 2:
                                pe.wait_ge(a_used.sem, a_used.at(h * NA + (n - 1)))
                            i, at, width = ACTU[n]
                            for b in range(0, width, BANK):
                                ins = nc.tensor.matmul(a_ps[slot][:, b:min(b + BANK, width)], qm[:, par, i * P:(i + 1) * P],
                                                       km[:, par, at + b:at + min(b + BANK, width)], start=True, stop=True)
                            ins.then_inc(a_full.sem, 1)
                            continue
                        if not first or n >= DRING:
                            pe.wait_ge(d_used.sem, d_used.at(h * NV + (n + 1 - DRING)))
                        out = d_ps[n % DRING]
                        if n < ND:
                            for s in range(QC):
                                i = n * QC + s
                                ins = nc.tensor.matmul(out[:, s * P:(s + 1) * P], km[:, par, i * P:(i + 1) * P],
                                                       qm[:, par, i * P:(i + 1) * P], start=True, stop=True)
                        else:
                            i, at, width = DVEU[n - ND]
                            ins = nc.tensor.matmul(out[:, 0:width], qm[:, par, i * P:(i + 1) * P], km[:, par, at:at + width], start=True, stop=True)
                        ins.then_inc(d_full.sem, 1)
                        if n == PV_AT and not first:
                            own_out(h - 1, 1 - par, first=second)
                        if n == TURN_AT and not first:
                            turn_out(h - 1)

                body(0, 0, 0, first=True)
                body(1, 0, 1, second=True)
                with pe.Fori(1, H // 2) as n:
                    for par in range(2):
                        body(2 * n + par, n, par)
                own_out(H - 1, 1)
                turn_out(H - 1)

            @block.scalar
            def _(act):
                act.wait_ge(cleared.sem, cleared.at(1))
                def copy_out(h):
                    act.wait_ge(o_ready.sem, o_ready.at(h + 1))
                    if not isinstance(h, int) or h > 0:
                        act.wait_ge(o_turned.sem, o_turned.at(h))
                    nc.scalar.copy(ot[:], o_ps[:]).then_inc(o_copied.sem, 1)

                def body(h, par, first=False):
                    for n, (i, at, width) in enumerate(ACTU):
                        if n == COPY_AT and not first:
                            copy_out(h - 1)
                        act.wait_ge(a_full.sem, a_full.at(h * NA + (n + 1)))
                        ps = a_ps[(par * NA + n) % 2][:, 0:width]
                        nc.scalar.activation(ps, ps, ACT.Abs, accum_out=part[:, bass.ds(h, 1), i, 0:1]).then_inc(a_used.sem, 1)

                body(0, 0, first=True)
                body(1, 1)
                with act.Fori(1, H // 2) as m:
                    for par in range(2):
                        body(2 * m + par, par)
                copy_out(H - 1)

            @block.vector
            def _(dve):
                dve.wait_ge(cleared.sem, cleared.at(1))

                def take_out(h):
                    dve.wait_ge(o_turned.sem, o_turned.at(h + 1))
                    o = o_ps[:].rearrange("p (t e) -> p t e", e=OW)
                    r = ret[:, :, bass.ds(h * VD, VD)]
                    nc.vector.tensor_tensor(r, o[:, :, 0:VD], r, ALU.add).then_inc(o_used.sem, 1)
                    nc.vector.tensor_copy(diag[:, bass.ds(h, 1), :], o[:, :, VD]).then_inc(o_used.sem, 1)

                def body(h, par, first=False, first_two=False):
                    for n in range(NV):
                        dve.wait_ge(d_full.sem, d_full.at(h * NV + (n + 1)))
                        if n < ND:
                            if n == 0 and not first_two:
                                dve.wait_ge(o_ready.sem, o_ready.at(h - 1))
                            nc.vector.tensor_tensor(sm[:, par, n * BANK:(n + 1) * BANK].rearrange("p (s t) -> p s t", t=P),
                                                    d_ps[n % DRING][:].rearrange("p (s t) -> p s t", t=P), bcast(w["keep_kq"][:], 1, QC),
                                                    ALU.mult).then_inc(d_used.sem, 1)
                        else:
                            i, at, width = DVEU[n - ND]
                            slot = 1 + (at // BANK) % 2
                            nc.vector.tensor_reduce(part[:, bass.ds(h, 1), i, slot:slot + 1], d_ps[n % DRING][:, 0:width], AX.X, ALU.add,
                                                    apply_absolute_value=True).then_inc(d_used.sem, 1)
                        if n == READ_AT and not first:
                            take_out(h - 1)

                body(0, 0, first=True, first_two=True)
                body(1, 1, first_two=True)
                with dve.Fori(1, H // 2) as n:
                    for par in range(2):
                        body(2 * n + par, par)
                take_out(H - 1)

        for par in range(2):
            loaded[par].done(NL * H // 2)
        cleared.done(5)
        a_full.done(NA * H)
        a_used.done(NA * H)
        d_full.done(NV * H)
        d_used.done(NV * H)
        v_ready.done(H)
        abs_ready.done(H)
        o_ready.done(H)
        o_copied.done(H)
        o_turned.done(H)
        o_used.done(2 * H)


def retention_norm_stage(k, w, part, diag, ret, gate):
    nc = k.nc
    eps = float(np.finfo(np.float32).eps)
    with ExitStack() as ctx:
        den = k.sb("ret_den", [P, NT, H], F32, ctx)
        sq = k.sb("ret_sq", [P, NT, H * VD], F32, ctx)
        ms = k.sb("ret_ms", [P, NT, H], F32, ctx)
        step, squared, ms_ready, std_ready, gated = (k.counter("ret_" + n) for n in ("step", "squared", "ms", "std", "gated"))
        counts = []
        with nc.Block() as block:

            @block.scalar
            def _(act):
                nc.scalar.activation(sq[:], ret[:], ACT.Square).then_inc(squared.sem, 1)
                act.wait_ge(ms_ready.sem, ms_ready.at(1))
                nc.scalar.sqrt(ms[:], ms[:]).then_inc(std_ready.sem, 1)

            @block.gpsimd
            def _(pool):
                nc.gpsimd.tensor_tensor(gate[:], gate[:], ret[:], ALU.mult).then_inc(gated.sem, 1)

            @block.vector
            def _(dve):
                chain = Chain(dve, step)
                by_head = den[:].rearrange("p t h -> p h t")
                chain(nc.vector.tensor_reduce(by_head, part[:], AX.X, ALU.add))
                chain(nc.vector.tensor_tensor(by_head, by_head, diag[:], ALU.add))
                chain(nc.vector.tensor_scalar(den[:], den[:], 1.0, 50000.0, ALU.max, ALU.min))
                chain(nc.vector.reciprocal(den[:], den[:]))
                dve.wait_ge(squared.sem, squared.at(1))
                chain(nc.vector.tensor_reduce(ms[:], sq[:].rearrange("p t (h v) -> p t h v", v=VD), AX.X, ALU.add))
                chain(nc.vector.scalar_tensor_tensor(ms[:], ms[:], 1.0 / VD, den[:], ALU.mult, ALU.mult))
                chain(nc.vector.tensor_tensor(ms[:], ms[:], den[:], ALU.mult))
                nc.vector.tensor_scalar(ms[:], ms[:], eps, None, ALU.add).then_inc(ms_ready.sem, 1)
                dve.wait_ge(std_ready.sem, std_ready.at(1))
                chain(nc.vector.reciprocal(ms[:], ms[:]))
                chain(nc.vector.tensor_tensor(ms[:], ms[:], den[:], ALU.mult))
                dve.wait_ge(gated.sem, gated.at(1))
                gv = gate[:].rearrange("p t (h v) -> p t h v", v=VD)
                chain(nc.vector.tensor_tensor(gv, gv, bcast(ms[:], 3, VD), ALU.mult))
                counts.append(chain.n)

        step.done(counts[0])
        for s in (squared, ms_ready, std_ready, gated):
            s.done(1)


def add_row_stage(k, x, row):
    nc = k.nc
    done = k.counter("row_added")
    with nc.Block() as block:

        @block.gpsimd
        def _(pool):
            nc.gpsimd.tensor_tensor(x[:], x[:], bcast(row[:], 1, NT), ALU.add).then_inc(done.sem, 1)

    done.done(1)




def rwkv_stage(k, w, xn_t, out_t):
    nc = k.nc
    with ExitStack() as ctx:
        xm = k.sb("mixed", [P, 3, T], F32, ctx)
        om = k.sb("one_minus_mix", [P, 3], F32, ctx)
        kvr = k.sb("kvr", [P, 3, T], F32, ctx)
        wneg = k.sb("neg_decay", [P, 1], F32, ctx)
        pmax = k.sb("exp_max", [P, T + 1], F32, ctx)
        num = k.sb("wkv_num", [P, T + 1], F32, ctx)
        den = k.sb("wkv_den", [P, T + 1], F32, ctx)
        grow = k.sb("carry_factor", [P, T], F32, ctx)
        add = k.sb("new_factor", [P, T], F32, ctx)
        e1, e2 = xm[:, 0, :], xm[:, 1, :]
        wt = k.sb("decay_row", [P, T], F32, ctx)
        ps = k.ps("kvr_ps", [P, 4, BANK], ctx)
        step, mixed, fed, kept, w_ready = (k.counter("rwkv_" + n) for n in ("step", "mixed", "fed", "kept", "w"))
        args, exps = k.counter("rwkv_args"), k.counter("rwkv_exps")
        counts = []
        kk, vv, rr = kvr[:, 0, :], kvr[:, 1, :], kvr[:, 2, :]
        with nc.Block() as block:

            @block.vector
            def _(dve):
                chain = Chain(dve, step)
                chain(nc.vector.tensor_scalar(om[:], w["mix"][:], -1.0, 1.0, ALU.mult, ALU.add))
                for n in range(3):
                    chain(nc.vector.tensor_scalar(xm[:, n, :], xn_t[:], w["mix"][:, n:n + 1], None, ALU.mult))
                    nc.vector.scalar_tensor_tensor(xm[:, n, 1:], xn_t[:, 0:T - 1], om[:, n:n + 1], xm[:, n, 1:],
                                                   ALU.mult, ALU.add).then_inc(mixed.sem, 1)
                nc.vector.memset(pmax[:, 0:1], -1e38)
                nc.vector.memset(num[:, 0:1], 0.0)
                nc.vector.memset(den[:, 0:1], 0.0)
                chain(nc.vector.memset(wt[:], 0.0))
                dve.wait_ge(w_ready.sem, w_ready.at(1))
                chain(nc.vector.tensor_scalar(wneg[:], wneg[:], -1.0, None, ALU.mult))
                chain(nc.vector.tensor_scalar(wt[:], wt[:], wneg[:, 0:1], None, ALU.add))
                dve.wait_ge(kept.sem, kept.at(4))
                chain(nc.vector.tensor_tensor_scan(pmax[:, 1:], wt[:], kk, -1e38, ALU.add, ALU.max))
                chain(nc.vector.scalar_tensor_tensor(grow[:], pmax[:, 0:T], wneg[:, 0:1], pmax[:, 1:], ALU.add, ALU.subtract))
                nc.vector.tensor_tensor(add[:], kk, pmax[:, 1:], ALU.subtract).then_inc(args.sem, 1)
                chain(nc.vector.scalar_tensor_tensor(wt[:], kk, w["first"][:, 0:1], pmax[:, 0:T], ALU.add, ALU.max))
                chain(nc.vector.tensor_tensor(e1, pmax[:, 0:T], wt[:], ALU.subtract))
                dve.wait_ge(kept.sem, kept.at(2 * NQ))
                nc.vector.scalar_tensor_tensor(e2, kk, w["first"][:, 0:1], wt[:], ALU.add, ALU.subtract).then_inc(args.sem, 1)
                dve.wait_ge(exps.sem, exps.at(2))
                chain(nc.vector.tensor_tensor_scan(den[:, 1:], grow[:], add[:], 0.0, ALU.mult, ALU.add))
                chain(nc.vector.tensor_tensor(add[:], add[:], vv, ALU.mult))
                chain(nc.vector.tensor_tensor_scan(num[:, 1:], grow[:], add[:], 0.0, ALU.mult, ALU.add))
                dve.wait_ge(exps.sem, exps.at(4))
                chain(nc.vector.tensor_tensor(grow[:], e1, den[:, 0:T], ALU.mult))
                chain(nc.vector.tensor_tensor(grow[:], grow[:], e2, ALU.add))
                chain(nc.vector.tensor_tensor(e1, e1, num[:, 0:T], ALU.mult))
                chain(nc.vector.tensor_tensor(e2, e2, vv, ALU.mult))
                chain(nc.vector.tensor_tensor(e1, e1, e2, ALU.add))
                dve.wait_ge(kept.sem, kept.at(3 * NQ))
                chain(nc.vector.scalar_tensor_tensor(grow[:], rr, 1.0, grow[:], ALU.add, ALU.mult))
                chain(nc.vector.reciprocal(grow[:], grow[:]))
                chain(nc.vector.tensor_tensor(out_t[:], e1, grow[:], ALU.mult))
                counts.append(chain.n)

            @block.tensor
            def _(pe):
                for n in range(3):
                    pe.wait_ge(mixed.sem, mixed.at(n + 1))
                    for q in range(NQ):
                        u = n * NQ + q
                        if u >= 4:
                            pe.wait_ge(kept.sem, kept.at(u - 3))
                        nc.tensor.matmul(ps[:, u % 4, :], w["wT"][:, 8 + n, :], xm[:, n, q * BANK:(q + 1) * BANK],
                                         start=True, stop=True).then_inc(fed.sem, 1)

            @block.scalar
            def _(act):
                nc.scalar.activation(wneg[:], w["decay"][:], ACT.Exp).then_inc(w_ready.sem, 1)
                for u in range(3 * NQ):
                    act.wait_ge(fed.sem, fed.at(u + 1))
                    dst = kvr[:, u // NQ, (u % NQ) * BANK:(u % NQ + 1) * BANK]
                    if u < 2 * NQ:
                        nc.scalar.copy(dst, ps[:, u % 4, :]).then_inc(kept.sem, 1)
                    else:
                        nc.scalar.activation(dst, ps[:, u % 4, :], ACT.Exp, scale=-1.0).then_inc(kept.sem, 1)
                act.wait_ge(args.sem, args.at(1))
                for a in (grow[:], add[:]):
                    nc.scalar.activation(a, a, ACT.Exp).then_inc(exps.sem, 1)
                act.wait_ge(args.sem, args.at(2))
                for a in (e1, e2):
                    nc.scalar.activation(a, a, ACT.Exp).then_inc(exps.sem, 1)

        step.done(counts[0])
        mixed.done(3)
        fed.done(3 * NQ)
        kept.done(3 * NQ)
        w_ready.done(1)
        args.done(2)
        exps.done(4)




def conv_stage(k, w, h_t, hc_t):
    nc = k.nc
    step = k.counter("conv_step")
    counts = []
    with nc.Block() as block:

        @block.vector
        def _(dve):
            chain = Chain(dve, step)
            chain(nc.vector.tensor_scalar(hc_t[:], h_t[:], w["conv_w"][:, 2:3], None, ALU.mult))
            for tap in (1, 0):
                lag = 2 - tap
                chain(nc.vector.scalar_tensor_tensor(hc_t[:, lag:], h_t[:, 0:T - lag], w["conv_w"][:, tap:tap + 1], hc_t[:, lag:], ALU.mult, ALU.add))
            counts.append(chain.n)

    step.done(counts[0])


def experts_stage(k, w, h_t, x):
    nc = k.nc
    NF = DFF // P
    with ExitStack() as ctx:
        logits = k.sb("logits", [P, NT, E], F32, ctx)
        best = k.sb("best", [P, NT], F32, ctx)
        pick = k.sb("pick", [P, NT, E], F32, ctx)
        free = k.sb("not_picked", [P, NT], F32, ctx)
        gate = k.sb("gate", [P, 4, BANK], F32, ctx)
        hid = k.sb("hidden", [P, 2, NF, BANK], F32, ctx)
        lp = k.ps("logits_ps", [P, BANK], ctx)
        gp = [k.ps(f"gate_ps{n}", [P, BANK], ctx) for n in range(2)]
        vp = [k.ps(f"value_ps{n}", [P, BANK], ctx) for n in range(2)]
        op = [k.ps(f"expert_ps{n}", [P, BANK], ctx) for n in range(2)]
        routed, step = k.counter("routed"), k.counter("route_step")
        upped, gated, hid_ready, downed, out_used = (k.counter("expert_" + n) for n in ("up", "gate", "hidden", "down", "used"))
        counts = []
        with nc.Block() as block:

            @block.tensor
            def _(pe):
                for i in range(NT):
                    ins = nc.tensor.matmul(lp[:, i * E:(i + 1) * E], h_t[:, i * P:(i + 1) * P], w["router"][:], start=True, stop=True)
                ins.then_inc(routed.sem, 1)

                def down(n, e):
                    u = n * E + e
                    pe.wait_ge(hid_ready.sem, hid_ready.at(n * (E * NF) + (e + 1) * NF))
                    for s in range(QC):
                        for f in range(NF):
                            ins = nc.tensor.matmul(op[e % 2][:, s * P:(s + 1) * P], hid[:, e % 2, f, s * P:(s + 1) * P],
                                                   w["expert_proj"][:, e, f, :], start=f == 0, stop=f == NF - 1)
                    ins.then_inc(downed.sem, 1)

                def body(n, first=False):
                    for e in range(E):
                        for f in range(NF):
                            g = e * NF + f
                            if not first or g >= 2:
                                pe.wait_ge(hid_ready.sem, hid_ready.at(n * (E * NF) + (g - 1)))
                            rhs = h_t[:, bass.ds(n * BANK, BANK)]
                            nc.tensor.matmul(gp[g % 2][:], w["expert_wv"][:, e, f * P:(f + 1) * P], rhs, start=True, stop=True).then_inc(upped.sem, 1)
                            nc.tensor.matmul(vp[g % 2][:], w["expert_wv"][:, e, DFF + f * P:DFF + (f + 1) * P], rhs, start=True, stop=True).then_inc(upped.sem, 1)
                        if not first or e >= 2:
                            pe.wait_ge(out_used.sem, out_used.at(n * (E * QC) + (e - 1) * QC))
                        down(n, e)

                body(0, first=True)
                with pe.Fori(1, NQ) as n:
                    body(n)

            @block.scalar
            def _(act):
                def body(n, first=False):
                    for g in range(E * NF):
                        act.wait_ge(upped.sem, upped.at(n * (2 * E * NF) + (2 * g + 1)))
                        if not first or g >= 4:
                            act.wait_ge(hid_ready.sem, hid_ready.at(n * (E * NF) + (g - 3)))
                        nc.scalar.activation(gate[:, g % 4, :], gp[g % 2][:], ACT.Silu).then_inc(gated.sem, 1)

                body(0, first=True)
                with act.Fori(1, NQ) as n:
                    body(n)

            @block.vector
            def _(dve):
                chain = Chain(dve, step)
                dve.wait_ge(routed.sem, routed.at(1))
                lv = lp[:, 0:NT * E].rearrange("p (t e) -> p t e", e=E)
                chain(nc.vector.tensor_copy(logits[:], lv))
                nc.vector.memset(free[:], 1.0)
                chain(nc.vector.tensor_reduce(best[:], logits[:], AX.X, ALU.max))
                for e in range(E):
                    chain(nc.vector.tensor_tensor(pick[:, :, e], logits[:, :, e], best[:], ALU.is_equal))
                    chain(nc.vector.tensor_tensor(pick[:, :, e], pick[:, :, e], free[:], ALU.mult))
                    chain(nc.vector.tensor_tensor(free[:], free[:], pick[:, :, e], ALU.subtract))

                def add_out(n, e):
                    dve.wait_ge(downed.sem, downed.at(n * E + (e + 1)))
                    for s in range(QC):
                        i = n * QC + s
                        if e > 0:
                            dve.wait_ge(out_used.sem, out_used.at(n * (E * QC) + ((e - 1) * QC + s + 1)))
                        xi = x[:, bass.ds(i, 1), :].rearrange("p o c -> p (o c)")
                        nc.vector.scalar_tensor_tensor(xi, op[e % 2][:, s * P:(s + 1) * P], pick[:, bass.ds(i, 1), e], xi,
                                                       ALU.mult, ALU.add).then_inc(out_used.sem, 1)

                def body(n, first=False):
                    for e in range(E):
                        for f in range(NF):
                            g = e * NF + f
                            dve.wait_ge(gated.sem, gated.at(n * (E * NF) + (g + 1)))
                            dve.wait_ge(upped.sem, upped.at(n * (2 * E * NF) + (2 * g + 2)))
                            if f == 0 and (not first or e >= 2):
                                dve.wait_ge(downed.sem, downed.at(n * E + (e - 1)))
                            nc.vector.tensor_tensor(hid[:, e % 2, f, :], vp[g % 2][:], gate[:, g % 4, :], ALU.mult).then_inc(hid_ready.sem, 1)
                            if f == 1 and e > 0:
                                add_out(n, e - 1)
                    add_out(n, E - 1)

                body(0, first=True)
                with dve.Fori(1, NQ) as n:
                    body(n)
                counts.append(chain.n)

        routed.done(1)
        step.done(counts[0])
        upped.done(2 * NQ * E * NF)
        gated.done(NQ * E * NF)
        hid_ready.done(NQ * E * NF)
        downed.done(NQ * E)
        out_used.done(NQ * E * QC)


def store_stage(k, x, out):
    nc = k.nc
    stored = k.counter("stored")
    with nc.Block() as block:

        @block.sync
        def _(sp):
            sp.dma_start(out.rearrange("o (t p) c -> p (o t) c", p=P), x[:]).then_inc(stored.sem, 16)
            sp.wait_ge(stored.sem, stored.at(16))

    stored.done(16)




def softmax_layer(k, w, h_t, wqkv, wo, parts_dram, norm, x):
    with ExitStack() as ctx:
        qkv = k.sb("qkv", [P, NT, 3 * C], F32, ctx)
        project_stage(k, [([(h_t, wqkv)], qkv, None)])
        rope_stage(k, w, qkv, norm)
        split_stage(k, w, qkv, parts_dram)
        y = k.sb("attn_out", [P, NT, C], F32, ctx)
        y_t = k.sb("attn_out_t", [P, T], F32, ctx)
        attention_stage(k, w, qkv, parts_dram, float(D) ** -0.5, y)
        transpose_stage(k, [(y, y_t)], w["ident"])
        project_stage(k, [([(y_t, wo)], x, None)], add_to=True)


def spline_layer(k, w, x):
    with ExitStack() as ctx:
        xn = k.sb("xn", [P, NT, C], F32, ctx)
        xn_t = k.sb("xn_t", [P, T], F32, ctx)
        layer_norm(k, x, xn, w["ident"], xn_t)
        spline_ffn_stage(k, w, xn_t, x)


def retention_layer(k, w, x, parts_dram):
    with ExitStack() as ctx:
        qkv = k.sb("ret_qkv", [P, NT, BANK], F32, ctx)
        gate = k.sb("ret_gate", [P, NT, H * VD], F32, ctx)
        with ExitStack() as inner:
            xn = k.sb("xn", [P, NT, C], F32, inner)
            xn_t = k.sb("xn_t", [P, T], F32, inner)
            layer_norm(k, x, xn, w["ident"], xn_t)
            project_stage(k, [([(xn_t, w["w_qkv_r"][:])], qkv, w["b_qkv_r"][:]), ([(xn_t, w["w_g"][:])], gate, w["b_g"][:])])
        retention_decay_stage(k, w, qkv)
        split_stage(k, w, qkv, parts_dram)
        part = k.sb("abs_part", [P, H, NT, 3], F32, ctx)
        diag = k.sb("abs_diag", [P, H, NT], F32, ctx)
        ret = k.sb("ret_out", [P, NT, H * VD], F32, ctx)
        with ExitStack() as inner:
            q_t = k.sb("ret_q_t", [P, T], F32, inner)
            transpose_stage(k, [(qkv[:, :, 0:C], q_t)], w["ident"])
            chunk_stage(k, w, qkv[:, :, C:2 * C], qkv[:, :, 2 * C:], q_t, None, VD, w["bd16"][:], ret, inner=False)
        retention_heads_stage(k, w, qkv[:, :, 2 * C:], parts_dram, part, diag, ret)
        retention_norm_stage(k, w, part, diag, ret, gate)
        with ExitStack() as inner:
            g_t = [k.sb(f"gated_t{b}", [P, T], F32, inner) for b in range(2)]
            transpose_stage(k, [(gate[:, :, b * C:(b + 1) * C], g_t[b]) for b in range(2)], w["ident"])
            add_row_stage(k, x, w["b_o"])
            project_stage(k, [([(g_t[b], w["w_o_r"][:, b, :]) for b in range(2)], x, None)], add_to=True)


def linear_layer(k, w, x):
    with ExitStack() as ctx:
        xn_t = k.sb("xn_t", [P, T], F32, ctx)
        with ExitStack() as inner:
            xn = k.sb("xn", [P, NT, C], F32, inner)
            layer_norm(k, x, xn, w["ident"], xn_t)
        with ExitStack() as inner:
            qkv = k.sb("lin_qkv", [P, NT, 3 * C], F32, inner)
            v9 = k.sb("v9", [P, NT, H * (D + 1)], F32, inner)
            project_stage(k, [([(xn_t, w["wT"][:, 4:7, :].rearrange("p b c -> p (b c)"))], qkv, None)])
            linear_features_stage(k, w, qkv, v9)
            q_t = xn_t
            k_t = k.sb("lin_k_t", [P, T], F32, inner)
            transpose_stage(k, [(qkv[:, :, 0:C], q_t), (qkv[:, :, C:2 * C], k_t)], w["ident"])
            chunk_stage(k, w, qkv[:, :, C:2 * C], v9, q_t, k_t, D + 1, w["bd9"][:], v9)
            linear_divide_stage(k, v9, qkv[:, :, 0:C])
            transpose_stage(k, [(qkv[:, :, 0:C], xn_t)], w["ident"])
        project_stage(k, [([(xn_t, w["wT"][:, 7, :])], x, None)], add_to=True)


def rwkv_layer(k, w, x):
    with ExitStack() as ctx:
        xn_t = k.sb("xn_t", [P, T], F32, ctx)
        out_t = k.sb("rwkv_t", [P, T], F32, ctx)
        with ExitStack() as inner:
            xn = k.sb("xn", [P, NT, C], F32, inner)
            layer_norm(k, x, xn, w["ident"], xn_t)
        rwkv_stage(k, w, xn_t, out_t)
        project_stage(k, [([(out_t, w["wT"][:, 11, :])], x, None)], add_to=True)


def conv_moe_layer(k, w, x, parts_dram):
    nc = k.nc
    with ExitStack() as ctx:
        y = k.sb("moe_y", [P, NT, C], F32, ctx)
        layer_norm(k, x, y, w["ident"])
        with ExitStack() as inner:
            hc_t = k.sb("conv_t", [P, T], F32, inner)
            with ExitStack() as first:
                h = k.sb("ln1", [P, NT, C], F32, first)
                h_t = k.sb("ln1_t", [P, T], F32, first)
                layer_norm(k, y, h, w["ident"], h_t, affine=(w["ln1_w"], w["ln1_b"]))
                conv_stage(k, w, h_t, hc_t)
            softmax_layer(k, w, hc_t, w["attn_w"][:], w["proj_w"][:], parts_dram, False, y)
        with ExitStack() as inner:
            h = k.sb("ln2", [P, NT, C], F32, inner)
            h_t = k.sb("ln2_t", [P, T], F32, inner)
            layer_norm(k, y, h, w["ident"], h_t, affine=(w["ln2_w"], w["ln2_b"]))
            experts_stage(k, w, h_t, y)
        added = k.counter("moe_added")
        with nc.Block() as block:

            @block.vector
            def _(dve):
                nc.vector.tensor_tensor(x[:], x[:], y[:], ALU.add).then_inc(added.sem, 1)

        added.done(1)


def build(nc, d, out):
    ctx = ExitStack()
    with ctx:
        k = Kernel(nc, ctx)
        w = {name: k.sb(name, shape, dtype) for name, shape, dtype in [
            ("X", [P, NT, C], F32), ("wT", [P, 12, C], F32), ("ident", [P, P], F32), ("ident16", [P, P], BF16),
            ("mask_qk", [P, P], BF16), ("mask_kq", [P, P], BF16), ("keep_kq", [P, P], F32), ("ones", [P, 1], F32),
            ("cos", [P, NT, D], F32), ("sin", [P, NT, D], F32), ("headmask", [P, H], F32),
            ("bd16", [P, H * VD], F32), ("bd9", [P, H * (D + 1)], F32),
            ("qdecay", [P, NT, H], F32), ("kdecay", [P, NT, H], F32), ("qn", [P, D], F32), ("kn", [P, D], F32),
            ("w_qkv_r", [P, BANK], F32), ("b_qkv_r", [P, BANK], F32), ("w_g", [P, H * VD], F32), ("b_g", [P, H * VD], F32),
            ("w_o_r", [P, 2, C], F32), ("b_o", [P, C], F32),
            ("Win", [P, M0], F32), ("bin", [P, 1], F32), ("W1", [P, INNER], F32), ("b1", [P, INNER], F32),
            ("W2", [P, INNER], F32), ("b2", [P, 1], F32), ("Wout", [P, C], F32), ("bout", [P, C], F32),
            ("mix", [P, 3], F32), ("decay", [P, 1], F32), ("first", [P, 1], F32),
            ("ln1_w", [P, C], F32), ("ln1_b", [P, C], F32), ("ln2_w", [P, C], F32), ("ln2_b", [P, C], F32),
            ("conv_w", [P, 3], F32), ("attn_w", [P, 3 * C], F32), ("proj_w", [P, C], F32), ("router", [P, E], F32),
            ("expert_wv", [P, E, 2 * DFF], F32), ("expert_proj", [P, E, DFF // P, C], F32),
            ("q_max", [P, 2, T], BF16), ("k_max", [P, 2, T], BF16), ("q_exp", [P, 2, T], BF16), ("k_exp", [P, 2, T], BF16)]}
        parts_dram = [nc.dram_tensor(f"{n}_parts", (PARTS, C, T), BF16, kind="Internal").ap() for n in "qk"]
        x = w["X"]
        load_stage(k, d, w)
        with ExitStack() as inner:
            xn = k.sb("xn", [P, NT, C], F32, inner)
            xn_t = k.sb("xn_t", [P, T], F32, inner)
            layer_norm(k, x, xn, w["ident"], xn_t)
            softmax_layer(k, w, xn_t, w["wT"][:, 0:3, :].rearrange("p b c -> p (b c)"), w["wT"][:, 3, :], parts_dram, True, x)
        spline_layer(k, w, x)
        retention_layer(k, w, x, parts_dram)
        spline_layer(k, w, x)
        linear_layer(k, w, x)
        conv_moe_layer(k, w, x, parts_dram)
        rwkv_layer(k, w, x)
        conv_moe_layer(k, w, x, parts_dram)
        store_stage(k, x, out)


def shape_constants():
    t = np.arange(T, dtype=np.float32)
    freq = (1.0 / np.float32(10000.0) ** (np.arange(0, D // 2, dtype=np.float32) * np.float32(2.0) / np.float32(D))).astype(np.float32)
    ang = (t[:, None] * freq[None, :]).astype(np.float32)
    cos, sin = np.cos(ang), np.sin(ang)

    def tiles(a):
        return np.ascontiguousarray(a.reshape(NT, P, -1).transpose(1, 0, 2)).astype(np.float32)

    n = np.arange(P)
    head = np.arange(H, dtype=np.float64)
    gamma = np.log1p(-2.0 ** (-5.0 - head))
    pos = np.arange(T, dtype=np.float64)[:, None]
    decay_sum = -np.expm1(gamma * (pos + 1)) / -np.expm1(gamma)
    row = n // D
    return {
        "c_mask_qk": np.where(n[None, :] > n[:, None], NEG, 0.0).astype(np.float32),
        "c_mask_kq": np.where(n[:, None] > n[None, :], NEG, 0.0).astype(np.float32),
        "c_keep_kq": (n[:, None] <= n[None, :]).astype(np.float32),
        "c_ident": np.eye(P, dtype=np.float32),
        "c_cos": tiles(np.concatenate([cos, cos], 1)),
        "c_sin": tiles(np.concatenate([-sin, sin], 1)),
        "c_headmask": (row[:, None] == np.arange(H)[None, :]).astype(np.float32),
        "c_bd16": (row[:, None] == np.arange(H * VD)[None, :] // VD).astype(np.float32),
        "c_bd9": (row[:, None] == np.arange(H * (D + 1))[None, :] // (D + 1)).astype(np.float32),
        "c_qdecay": tiles(np.exp(gamma * (pos - T // 2)) / np.sqrt(decay_sum)),
        "c_kdecay": tiles(np.exp(gamma * (T // 2 - pos))),
    }


def kernel(**inputs):
    import numpy as _np
    import concourse.bacc as _bacc
    from concourse import mybir as _mybir
    from concourse.bass_utils import run_bass_kernel_spmd as _run

    nc = _bacc.Bacc("TRN2", target_bir_lowering=False, num_devices=1)
    arrays, d = {}, {}
    for name, value in list(inputs.items()) + list(shape_constants().items()):
        a = _np.ascontiguousarray(value)
        arrays[f"in_{name}"] = a
        key = "x" if name == "L0_attn_a_x" else name
        d[key] = nc.dram_tensor(f"in_{name}", a.shape, _mybir.dt.from_np(a.dtype), kind="ExternalInput").ap()
    out = nc.dram_tensor("out_0", (1, T, C), F32, kind="ExternalOutput").ap()
    build(nc, d, out)
    r = _run(nc, [arrays], core_ids=[0])
    return r.results[0]["out_0"]
```

```python
import numpy as np
import concourse.bass as bass
from concourse import mybir
from contextlib import ExitStack

F32 = mybir.dt.float32
BF16 = mybir.dt.bfloat16
ACT = mybir.ActivationFunctionType
ALU = mybir.AluOpType
AX = mybir.AxisListType

T, C, H = 2048, 128, 16
P = 128
NT = T // P
D = C // H
BANK = 512
QC = BANK // P
NQ = T // BANK
NEG = -1e30
PARTS = 3
KROWS = PARTS * PARTS * D
SHIFT = 2
VD = 16
M0, INNER = 64, 16
E, DFF = 4, 512


class Counter:

    def __init__(self, sem):
        self.sem, self.sent = sem, 0

    def at(self, n):
        return n + self.sent if self.sent else n

    def done(self, n):
        self.sent += n


class Kernel:

    def __init__(self, nc, ctx):
        self.nc, self.ctx, self.counters, self.count = nc, ctx, {}, 0

    def counter(self, name):
        if name not in self.counters:
            self.counters[name] = Counter(self.ctx.enter_context(self.nc.semaphore(name)))
        return self.counters[name]

    def sb(self, name, shape, dtype=F32, ctx=None):
        self.count += 1
        return (ctx or self.ctx).enter_context(self.nc.sbuf_tensor(f"{name}_{self.count}", shape, dtype))

    def ps(self, name, shape, ctx, dtype=F32):
        self.count += 1
        return ctx.enter_context(self.nc.psum_tensor(f"{name}_{self.count}", shape, dtype))


class Chain:

    def __init__(self, eng, counter):
        self.eng, self.counter, self.n = eng, counter, 0

    def __call__(self, ins):
        self.n += 1
        ins.then_inc(self.counter.sem, 1)
        self.eng.wait_ge(self.counter.sem, self.counter.at(self.n))


def bcast(ap, axis, n):
    a = ap.unsqueeze(axis)
    shape = list(a.shape)
    shape[axis] = n
    return a.broadcast_to(shape)




def load_stage(k, d, w):
    nc = k.nc
    with ExitStack() as ctx:
        maskf = k.sb("mask_f32", [P, P], F32, ctx)
        tp = k.ps("weight_t", [P, BANK], ctx)
        padded = [k.counter(f"rows_padded_{n}") for n in "qk"]
        loaded, turned, kept = k.counter("loaded"), k.counter("weights_turned"), k.counter("weights_kept")
        plain = [
            (w["X"][:], d["x"].rearrange("o (t p) c -> p (o t) c", p=P)),
            (w["raw"][:, 0:3, :], d["L0_attn_a_w_qkv"].rearrange("(b p) c -> p b c", p=P)),
            (w["raw"][:, 3, :], d["L0_attn_a_w_out"]),
            (maskf[:], d["c_mask_qk"]),
            (w["ident"][:], d["c_ident"]),
            (w["cos"][:], d["c_cos"]),
            (w["sin"][:], d["c_sin"]),
            (w["qn"][:], d["L0_attn_a_q_norm_w"].partition_broadcast(P)),
            (w["kn"][:], d["L0_attn_a_k_norm_w"].partition_broadcast(P)),
        ]
        with nc.Block() as block:

            @block.sync
            def _(sp):
                with nc.allow_non_contiguous_dma(reason="per-channel vectors"):
                    for dst, src in plain:
                        sp.dma_start(dst, src).then_inc(loaded.sem, 16)
                sp.wait_ge(loaded.sem, loaded.at(16 * len(plain)))

            @block.tensor
            def _(pe):
                pe.wait_ge(loaded.sem, loaded.at(16 * len(plain)))
                for b in range(QC):
                    ins = nc.tensor.transpose(tp[:, b * P:(b + 1) * P], w["raw"][:, b, :], w["ident"][:])
                ins.then_inc(turned.sem, 1)

            @block.scalar
            def _(act):
                act.wait_ge(turned.sem, turned.at(1))
                nc.scalar.copy(w["wT"][:, 0:QC, :].rearrange("p a b -> p (a b)"), tp[:]).then_inc(kept.sem, 1)

            @block.vector
            def _(dve):
                for n, name in enumerate(("q_max", "q_exp")):
                    nc.vector.memset(w[name][64:P, :, :], 0.0).then_inc(padded[0].sem, 1)
                dve.wait_ge(loaded.sem, loaded.at(16 * len(plain)))
                nc.vector.tensor_copy(w["mask16"][:], maskf[:]).then_inc(kept.sem, 1)
                nc.vector.tensor_copy(w["ident16"][:], w["ident"][:]).then_inc(kept.sem, 1)

            @block.gpsimd
            def _(pool):
                for n, name in enumerate(("k_max", "k_exp")):
                    nc.gpsimd.memset(w[name][64:P, :, :], -1.0).then_inc(padded[1].sem, 1)
                    pool.wait_ge(padded[1].sem, padded[1].at(n + 1))

        loaded.done(16 * len(plain))
        for sig in padded:
            sig.done(2)
        turned.done(1)
        kept.done(3)


def rest_loads(d, w):
    plain = [
        (w["raw"][:, 4:7, :], d["L1_attn_a_W_qkv"].rearrange("(b p) c -> p b c", p=P)),
        (w["raw"][:, 7, :], d["L1_attn_a_W_out"]),
        (w["raw"][:, 8, :], d["L1_attn_b_Wk"]),
        (w["raw"][:, 9, :], d["L1_attn_b_Wv"]),
        (w["raw"][:, 10, :], d["L1_attn_b_Wr"]),
        (w["raw"][:, 11, :], d["L1_attn_b_Wo"]),
        (w["keep_kq"][:], d["c_keep_kq"]),
        (w["headmask"][:], d["c_headmask"]),
        (w["bd16"][:], d["c_bd16"]),
        (w["bd9"][:], d["c_bd9"]),
        (w["qdecay"][:], d["c_qdecay"]),
        (w["kdecay"][:], d["c_kdecay"]),
        (w["w_qkv_r"][:, 0:2 * C], d["L0_attn_b_W_qk"]),
        (w["w_qkv_r"][:, 2 * C:], d["L0_attn_b_W_v"]),
        (w["b_qkv_r"][:, 0:2 * C], d["L0_attn_b_b_qk"].partition_broadcast(P)),
        (w["b_qkv_r"][:, 2 * C:], d["L0_attn_b_b_v"].partition_broadcast(P)),
        (w["w_g"][:], d["L0_attn_b_W_g"]),
        (w["b_g"][:], d["L0_attn_b_b_g"].partition_broadcast(P)),
        (w["w_o_r"][:], d["L0_attn_b_W_o"].rearrange("(b p) c -> p b c", p=P)),
        (w["b_o"][:], d["L0_attn_b_b_o"].partition_broadcast(P)),
        (w["Win"][:], d["L0_ffn_Win"]),
        (w["bout"][:], d["L0_ffn_bout"].partition_broadcast(P)),
        (w["mix"][:, 0:1], d["L1_attn_b_time_mix_k"].rearrange("a b c -> c (a b)")),
        (w["mix"][:, 1:2], d["L1_attn_b_time_mix_v"].rearrange("a b c -> c (a b)")),
        (w["mix"][:, 2:3], d["L1_attn_b_time_mix_r"].rearrange("a b c -> c (a b)")),
        (w["decay"][:], d["L1_attn_b_time_decay"].rearrange("(c o) -> c o", o=1)),
        (w["first"][:], d["L1_attn_b_time_first"].rearrange("(c o) -> c o", o=1)),
        (w["ln1_w"][:], d["L1_ffn_ln1_w"].rearrange("(c o) -> c o", o=1)),
        (w["ln1_b"][:], d["L1_ffn_ln1_b"].rearrange("(c o) -> c o", o=1)),
        (w["ln2_w"][:], d["L1_ffn_ln2_w"].rearrange("(c o) -> c o", o=1)),
        (w["ln2_b"][:], d["L1_ffn_ln2_b"].rearrange("(c o) -> c o", o=1)),
        (w["conv_w"][:], d["L1_ffn_conv_w"].rearrange("c o j -> c (o j)")),
        (w["attn_w"][:], d["L1_ffn_attn_w"]),
        (w["proj_w"][:], d["L1_ffn_proj_w"]),
        (w["router"][:], d["L1_ffn_router_w"]),
        (w["expert_wv"][:], d["L1_ffn_expert_wv"].rearrange("e c f -> c e f")),
        (w["expert_proj"][:], d["L1_ffn_expert_proj"].rearrange("e (b p) c -> p e b c", p=P)),
    ]
    for half in range(2):
        at = slice(half * M0, half * M0 + M0)
        plain += [
            (w["bin"][at, :], d["L0_ffn_bin_"].rearrange("(m o) -> m o", o=1)),
            (w["W1"][at, :], d["L0_ffn_W1"]),
            (w["b1"][at, :], d["L0_ffn_b1"]),
            (w["W2"][at, :], d["L0_ffn_W2"]),
            (w["b2"][at, :], d["L0_ffn_b2"].rearrange("(m o) -> m o", o=1)),
            (w["Wout"][at, :], d["L0_ffn_Wout"]),
        ]
    return plain




def layer_norm(k, src, dst, ident, dst_t=None, affine=None, eps=1e-5):
    nc = k.nc
    with ExitStack() as ctx:
        stats = k.sb("ln_stats", [P, NT, 6], F32, ctx)
        mv = k.sb("ln_mean_var", [P, NT, 2], F32, ctx)
        std = k.sb("ln_std", [P, NT], F32, ctx)
        rstd = k.sb("ln_rstd", [P, NT], F32, ctx)
        shift = k.sb("ln_shift", [P, NT], F32, ctx)
        tp = k.ps("ln_t", [P, NQ, BANK], ctx)
        step, var_ready, std_ready, scale_ready = (k.counter("ln_" + n) for n in ("step", "var", "std", "scale"))
        names = ("dve", "act")
        rows, turned, kept = ([k.counter(f"ln_{what}_{n}") for n in names] for what in ("rows", "turned", "kept"))
        half = NQ // 2
        with nc.Block() as block:

            @block.vector
            def _(dve):
                chain = Chain(dve, step)
                for i in range(NT):
                    ins = nc.vector.bn_stats(stats[:, i, :], src[:, i, :])
                chain(ins)
                for i in range(NT):
                    ins = nc.vector.bn_aggr(mv[:, i, :], stats[:, i, :])
                chain(ins)
                nc.vector.tensor_scalar(std[:], mv[:, :, 1], eps, None, ALU.add).then_inc(var_ready.sem, 1)
                dve.wait_ge(std_ready.sem, std_ready.at(1))
                chain(nc.vector.reciprocal(rstd[:], std[:]))
                nc.vector.scalar_tensor_tensor(shift[:], mv[:, :, 0], -1.0, rstd[:], ALU.mult, ALU.mult).then_inc(scale_ready.sem, 1)
                for q in range(half):
                    for i in range(QC * q, QC * q + QC):
                        ins = nc.vector.tensor_scalar(dst[:, i, :], src[:, i, :], mv[:, i, 0:1], rstd[:, i:i + 1],
                                                      ALU.subtract, ALU.mult)
                    ins.then_inc(rows[0].sem, 1)
                if dst_t is not None:
                    for q in range(half):
                        dve.wait_ge(turned[0].sem, turned[0].at(q + 1))
                        out = dst_t[:, q * BANK:(q + 1) * BANK]
                        if affine is None:
                            nc.vector.tensor_copy(out, tp[:, q, :]).then_inc(kept[0].sem, 1)
                        else:
                            nc.vector.tensor_scalar(out, tp[:, q, :], affine[0][:, 0:1], affine[1][:, 0:1], ALU.mult, ALU.add).then_inc(kept[0].sem, 1)

            @block.scalar
            def _(act):
                act.wait_ge(var_ready.sem, var_ready.at(1))
                nc.scalar.sqrt(std[:], std[:]).then_inc(std_ready.sem, 1)
                act.wait_ge(scale_ready.sem, scale_ready.at(1))
                for q in range(half, NQ):
                    for i in range(QC * q, QC * q + QC):
                        ins = nc.scalar.activation(dst[:, i, :], src[:, i, :], ACT.Identity, bias=shift[:, i:i + 1], scale=rstd[:, i:i + 1])
                    ins.then_inc(rows[1].sem, 1)
                if dst_t is not None:
                    for q in range(half, NQ):
                        act.wait_ge(turned[1].sem, turned[1].at(q - half + 1))
                        out = dst_t[:, q * BANK:(q + 1) * BANK]
                        if affine is None:
                            nc.scalar.copy(out, tp[:, q, :]).then_inc(kept[1].sem, 1)
                        else:
                            nc.scalar.activation(out, tp[:, q, :], ACT.Identity, bias=affine[1][:, 0:1], scale=affine[0][:, 0:1]).then_inc(kept[1].sem, 1)

            @block.tensor
            def _(pe):
                if dst_t is not None:
                    for n in range(half):
                        for who in range(2):
                            q = n + who * half
                            pe.wait_ge(rows[who].sem, rows[who].at(n + 1))
                            for i in range(QC):
                                ins = nc.tensor.transpose(tp[:, q, i * P:(i + 1) * P], dst[:, QC * q + i, :], ident[:])
                            ins.then_inc(turned[who].sem, 1)

        step.done(3)
        for s in (var_ready, std_ready, scale_ready):
            s.done(1)
        for who in range(2):
            rows[who].done(half)
            if dst_t is not None:
                turned[who].done(half)
                kept[who].done(half)


def transpose_stage(k, jobs, ident):
    nc = k.nc
    with ExitStack() as ctx:
        tp = k.ps("turn", [P, 4, BANK], ctx)
        turned, kept = k.counter("turned"), k.counter("turn_kept")
        units = [(src, dst, q) for src, dst in jobs for q in range(src.shape[1] // QC)]
        with nc.Block() as block:

            @block.tensor
            def _(pe):
                for n, (src, dst, q) in enumerate(units):
                    if n >= 4:
                        pe.wait_ge(kept.sem, kept.at(n - 3))
                    for i in range(QC):
                        ins = nc.tensor.transpose(tp[:, n % 4, i * P:(i + 1) * P], src[:, QC * q + i, :], ident[:])
                    ins.then_inc(turned.sem, 1)

            @block.scalar
            def _(act):
                for n, (src, dst, q) in enumerate(units):
                    act.wait_ge(turned.sem, turned.at(n + 1))
                    nc.scalar.copy(dst[:, q * BANK:(q + 1) * BANK], tp[:, n % 4, :]).then_inc(kept.sem, 1)

        turned.done(len(units))
        kept.done(len(units))


def output_stage(k, w, pairs, x, turns=()):
    nc = k.nc
    with ExitStack() as ctx:
        src_t = [k.sb(f"turned{n}", [P, T], F32, ctx) for n in range(len(pairs))]
        tp = k.ps("turn", [P, 4, BANK], ctx)
        out = k.ps("project", [P, 4, BANK], ctx)
        turned, kept = k.counter("turned"), k.counter("turn_kept")
        ready, used = k.counter("projected"), k.counter("project_kept")
        NP = len(pairs)
        units = [(pairs[m][0][:, QC * q:QC * q + QC, :], src_t[m][:, q * BANK:(q + 1) * BANK]) for q in range(NQ) for m in range(NP)]
        units += turns
        with nc.Block() as block:

            @block.tensor
            def _(pe):
                def turn(n):
                    if n >= 4:
                        pe.wait_ge(kept.sem, kept.at(n - 3))
                    for i in range(QC):
                        ins = nc.tensor.transpose(tp[:, n % 4, i * P:(i + 1) * P], units[n][0][:, i, :], w["ident"][:])
                    ins.then_inc(turned.sem, 1)

                def project(q):
                    pe.wait_ge(kept.sem, kept.at((q + 1) * NP))
                    for i in range(QC * q, QC * q + QC):
                        if i >= 4:
                            pe.wait_ge(used.sem, used.at(i - 3))
                        for m in range(NP):
                            ins = nc.tensor.matmul(out[:, i % 4, 0:C], src_t[m][:, i * P:(i + 1) * P], pairs[m][1],
                                                   start=m == 0, stop=m == NP - 1)
                        ins.then_inc(ready.sem, 1)

                for q in range(NQ):
                    for n in range(q * NP, q * NP + NP):
                        turn(n)
                    if q > 0:
                        project(q - 1)
                for n in range(NQ * NP, len(units)):
                    turn(n)
                project(NQ - 1)

            @block.scalar
            def _(act):
                for n, (_, dst) in enumerate(units):
                    act.wait_ge(turned.sem, turned.at(n + 1))
                    nc.scalar.copy(dst, tp[:, n % 4, :]).then_inc(kept.sem, 1)

            @block.vector
            def _(dve):
                for i in range(NT):
                    dve.wait_ge(ready.sem, ready.at(i + 1))
                    nc.vector.tensor_tensor(x[:, i, :], out[:, i % 4, 0:C], x[:, i, :], ALU.add).then_inc(used.sem, 1)

        turned.done(len(units))
        kept.done(len(units))
        ready.done(NT)
        used.done(NT)


def project_stage(k, jobs, add_to=False):
    nc = k.nc
    with ExitStack() as ctx:
        out = k.ps("project", [P, 8, BANK], ctx)
        ready, kept = k.counter("projected"), k.counter("project_kept")
        units = [(job, i) for i in range(NT) for job in jobs]
        with nc.Block() as block:

            @block.tensor
            def _(pe):
                for n, ((chunks, dst, bias), i) in enumerate(units):
                    if n >= 8:
                        pe.wait_ge(kept.sem, kept.at(n - 7))
                    width = chunks[0][1].shape[-1]
                    for c, (x_t, wgt) in enumerate(chunks):
                        ins = nc.tensor.matmul(out[:, n % 8, 0:width], x_t[:, i * P:(i + 1) * P], wgt,
                                               start=(c == 0), stop=(c == len(chunks) - 1))
                    ins.then_inc(ready.sem, 1)

            @block.vector
            def _(dve):
                for n, ((chunks, dst, bias), i) in enumerate(units):
                    width = chunks[0][1].shape[-1]
                    dve.wait_ge(ready.sem, ready.at(n + 1))
                    o = out[:, n % 8, 0:width]
                    if add_to:
                        ins = nc.vector.tensor_tensor(dst[:, i, :], o, dst[:, i, :], ALU.add)
                    elif bias is not None:
                        ins = nc.vector.tensor_tensor(dst[:, i, :], o, bias, ALU.add)
                    else:
                        ins = nc.vector.tensor_copy(dst[:, i, :], o)
                    ins.then_inc(kept.sem, 1)

        ready.done(len(units))
        kept.done(len(units))


def qkv_stage(k, w, jobs, qkv, parts_dram, mode, loads=()):
    nc = k.nc
    half = D // 2
    BANKS = 4
    units = [(job, i) for i in range(NT) for job in jobs]
    NU = len(jobs) * QC
    norm = mode == "norm"
    biased = jobs[0][2] is not None
    act_copies = (0, 1, 2) if mode == "decay" else (0, 2)
    with ExitStack() as ctx:
        parts = k.sb("parts", [P, 2, 2, PARTS, QC, C], BF16, ctx)
        rest = k.sb("parts_rest", [P, 2, 2, QC, C], F32, ctx)
        turned_sb = k.sb("parts_t", [P, 2, PARTS, T], BF16, ctx)
        work = k.sb("rope_work", [P, 2, QC, C], F32, ctx)
        out = [k.ps(f"project{n}", [P, BANK], ctx) for n in range(BANKS)]
        tp = [k.ps(f"parts_turn{a}", [P, 2, BANK], ctx, BF16) for a in range(PARTS)]
        loaded = k.counter("loaded")
        projected, evacuated = k.counter("qkv_projected"), k.counter("qkv_evacuated")
        ready = [k.counter(f"qk_ready_{n}") for n in "qk"]
        rounded = [k.counter(f"part_rounded{a}") for a in range(2)]
        left = [k.counter(f"part_left_{n}") for n in "qk"]
        turned = [k.counter(f"part_turned{a}") for a in range(PARTS)]
        copied = [k.counter(f"part_copied{a}") for a in range(PARTS)]
        stored, step_v, step_p = k.counter("parts_stored"), k.counter("qk_step_dve"), k.counter("qk_step_pool")
        tables = {n: (w["cos"], w["sin"]) for n in "qk"}
        if norm:
            tables = {n: (k.sb(f"cos_{n}", [P, NT, D], F32, ctx), k.sb(f"sin_{n}", [P, NT, D], F32, ctx)) for n in "qk"}
            sq = k.sb("qk_squared", [P, 2, QC, 2 * C], F32, ctx)
            ms = k.sb("qk_mean_square", [P, NQ, QC, 2, H], F32, ctx)
            rms = k.sb("qk_inv_rms", [P, NQ, QC, 2, H], F32, ctx)
            weighted, squared, ms_ready, rms_ready, inverted = (k.counter("qk_" + n) for n in ("tables", "squared", "ms", "rms", "inverted"))
        counts = []

        def tiles(c):
            return slice(QC * c, QC * c + QC)

        def x_of(s, c):
            return qkv[:, tiles(c), s * C:(s + 1) * C]

        def wait_raw(eng, c):
            eng.wait_ge(evacuated.sem, evacuated.at(NU * c + NU))

        def rotate(eng, chain, s, c, tmp):
            cos, sin = (t[:, tiles(c), :] for t in tables["qk"[s]])
            xs = x_of(s, c).rearrange("p t (h d) -> p t h d", d=D)
            ws = tmp.rearrange("p t (h d) -> p t h d", d=D)
            eng.tensor_tensor(ws[:, :, :, 0:half], xs[:, :, :, half:], bcast(sin[:, :, 0:half], 2, H), ALU.mult)
            chain(eng.tensor_tensor(ws[:, :, :, half:], xs[:, :, :, 0:half], bcast(sin[:, :, half:], 2, H), ALU.mult))
            chain(eng.tensor_tensor(xs, xs, bcast(cos, 2, H), ALU.mult))
            return eng.tensor_tensor(x_of(s, c), x_of(s, c), tmp, ALU.add)

        def make_ready(eng, chain, s, c, tmp):
            if mode == "decay":
                xs = x_of(s, c).rearrange("p t (h d) -> p t h d", d=D)
                table = w["qdecay" if s == 0 else "kdecay"][:, tiles(c), :]
                last = eng.tensor_tensor(xs, xs, bcast(table, 3, D), ALU.mult)
            else:
                if c > 0:
                    eng.wait_ge(ready[s].sem, ready[s].at(c))
                last = rotate(eng, chain, s, c, tmp)
            if norm:
                chain(last)
            else:
                last.then_inc(ready[s].sem, 1)

        def normalise(eng, s, c):
            xs = x_of(s, c).rearrange("p t (h d) -> p t h d", d=D)
            eng.tensor_tensor(xs, xs, bcast(rms[:, c, :, s, :], 3, D), ALU.mult).then_inc(ready[s].sem, 1)

        with nc.Block() as block:

            @block.tensor
            def _(pe):
                def project(c):
                    for n in range(NU * c, NU * c + NU):
                        (chunks, _, _), i = units[n]
                        if n >= BANKS:
                            pe.wait_ge(evacuated.sem, evacuated.at(n + 1 - BANKS))
                        width = chunks[0][1].shape[-1]
                        for m, (x_t, wgt) in enumerate(chunks):
                            ins = nc.tensor.matmul(out[n % BANKS][:, 0:width], x_t[:, i * P:(i + 1) * P], wgt,
                                                   start=(m == 0), stop=(m == len(chunks) - 1))
                        ins.then_inc(projected.sem, 1)

                def turn(c):
                    for a in range(PARTS):
                        if c > 0:
                            pe.wait_ge(copied[a].sem, copied[a].at(c))
                        for s in range(2):
                            if a < 2:
                                pe.wait_ge(rounded[a].sem, rounded[a].at(2 * c + s + 1))
                            else:
                                pe.wait_ge(left[s].sem, left[s].at(2 * c + 2))
                            for i in range(QC):
                                ins = nc.tensor.transpose(tp[a][:, s, i * P:(i + 1) * P], parts[:, c % 2, s, a, i, :], w["ident16"][:])
                        ins.then_inc(turned[a].sem, 1)

                for n in range(NQ + 2):
                    if n < NQ:
                        project(n)
                    if n >= 2:
                        turn(n - 2)

            def copy_out(eng, copy, a, c):
                eng.wait_ge(turned[a].sem, turned[a].at(c + 1))
                copy(turned_sb[:, :, a, c * BANK:(c + 1) * BANK], tp[a][:]).then_inc(copied[a].sem, 1)

            @block.scalar
            def _(act):
                for n in range(NQ + 2):
                    c = n - 1
                    if 0 <= c < NQ:
                        for s in range(2):
                            act.wait_ge(ready[s].sem, ready[s].at(c + 1))
                            if c >= 2:
                                act.wait_ge(turned[0].sem, turned[0].at(c - 1))
                            nc.scalar.copy(parts[:, c % 2, s, 0], x_of(s, c)).then_inc(rounded[0].sem, 1)
                    if n < NQ and not biased:
                        for u in range(NU * n, NU * n + NU):
                            (_, dst, _), i = units[u]
                            act.wait_ge(projected.sem, projected.at(u + 1))
                            nc.scalar.copy(dst[:, i, :], out[u % BANKS][:, 0:dst.shape[-1]]).then_inc(evacuated.sem, 1)
                    if n < NQ and norm:
                        wait_raw(act, n)
                        if n >= 2:
                            act.wait_ge(ms_ready.sem, ms_ready.at(n - 1))
                        nc.scalar.activation(sq[:, n % 2], qkv[:, tiles(n), 0:2 * C], ACT.Square).then_inc(squared.sem, 1)
                    if 0 <= c < NQ:
                        for s in range(2):
                            act.wait_ge(left[s].sem, left[s].at(2 * c + 1))
                            if c >= 2:
                                act.wait_ge(turned[1].sem, turned[1].at(c - 1))
                            nc.scalar.copy(parts[:, c % 2, s, 1], rest[:, c % 2, s]).then_inc(rounded[1].sem, 1)
                    if n < NQ and norm:
                        act.wait_ge(ms_ready.sem, ms_ready.at(n + 1))
                        nc.scalar.sqrt(rms[:, n], ms[:, n]).then_inc(rms_ready.sem, 1)
                    if n >= 2:
                        for a in act_copies:
                            copy_out(act, nc.scalar.copy, a, n - 2)

            def cut_rest(eng, ops, s, c):
                if 0 <= c < NQ:
                    eng.wait_ge(rounded[0].sem, rounded[0].at(2 * c + s + 1))
                    ops.tensor_tensor(rest[:, c % 2, s], x_of(s, c), parts[:, c % 2, s, 0], ALU.subtract).then_inc(left[s].sem, 1)

            def cut_last(eng, ops, s, c):
                if 0 <= c < NQ:
                    eng.wait_ge(rounded[1].sem, rounded[1].at(2 * c + s + 1))
                    if c >= 2:
                        eng.wait_ge(turned[2].sem, turned[2].at(c - 1))
                    ops.tensor_tensor(parts[:, c % 2, s, 2], rest[:, c % 2, s], parts[:, c % 2, s, 1], ALU.subtract).then_inc(left[s].sem, 1)

            @block.vector
            def _(dve):
                chain = Chain(dve, step_v)
                if norm:
                    for n in "qk":
                        for table, src in zip(tables[n], (w["cos"], w["sin"])):
                            ins = nc.vector.tensor_tensor(table[:], src[:], bcast(w[n + "n"][:], 1, NT), ALU.mult)
                    ins.then_inc(weighted.sem, 1)
                    dve.wait_ge(weighted.sem, weighted.at(1))
                for n in range(NQ + 2):
                    cut_rest(dve, nc.vector, 0, n - 1)
                    if n < NQ:
                        if biased:
                            for u in range(NU * n, NU * n + NU):
                                (_, dst, bias), i = units[u]
                                dve.wait_ge(projected.sem, projected.at(u + 1))
                                nc.vector.tensor_tensor(dst[:, i, :], out[u % BANKS][:, 0:dst.shape[-1]], bias, ALU.add).then_inc(evacuated.sem, 1)
                        if norm:
                            dve.wait_ge(squared.sem, squared.at(n + 1))
                            chain(nc.vector.tensor_reduce(ms[:, n].rearrange("p t s h -> p t (s h)"),
                                                          sq[:, n % 2].rearrange("p t (g d) -> p t g d", d=D), AX.X, ALU.add))
                            nc.vector.tensor_scalar(ms[:, n], ms[:, n], 1.0 / D, 1e-6, ALU.mult, ALU.add).then_inc(ms_ready.sem, 1)
                        wait_raw(dve, n)
                        make_ready(nc.vector, chain, 0, n, work[:, 0])
                    cut_last(dve, nc.vector, 0, n - 1)
                    if n < NQ and norm:
                        dve.wait_ge(rms_ready.sem, rms_ready.at(n + 1))
                        nc.vector.reciprocal(rms[:, n], rms[:, n]).then_inc(inverted.sem, 1)
                        dve.wait_ge(inverted.sem, inverted.at(n + 1))
                        normalise(nc.vector, 0, n)
                    if n >= 2:
                        for a in range(PARTS):
                            if a not in act_copies:
                                copy_out(dve, nc.vector.tensor_copy, a, n - 2)
                counts.append(chain.n)

            @block.gpsimd
            def _(pool):
                chain = Chain(pool, step_p)
                if norm:
                    pool.wait_ge(weighted.sem, weighted.at(1))
                for n in range(NQ + 1):
                    cut_rest(pool, nc.gpsimd, 1, n - 1)
                    if n < NQ:
                        wait_raw(pool, n)
                        if norm:
                            pool.wait_ge(squared.sem, squared.at(n + 1))
                        make_ready(nc.gpsimd, chain, 1, n, work[:, 1])
                    cut_last(pool, nc.gpsimd, 1, n - 1)
                    if n < NQ and norm:
                        pool.wait_ge(inverted.sem, inverted.at(n + 1))
                        normalise(nc.gpsimd, 1, n)
                counts.append(chain.n)

            @block.sync
            def _(sp):
                with nc.allow_non_contiguous_dma(reason="per-channel vectors"):
                    for dst, src in loads:
                        sp.dma_start(dst, src).then_inc(loaded.sem, 16)
                for c in range(NQ):
                    for a in range(PARTS):
                        sp.wait_ge(copied[a].sem, copied[a].at(c + 1))
                    cols = slice(c * BANK, (c + 1) * BANK)
                    for s in range(2):
                        sp.dma_start(parts_dram[s].rearrange("a c t -> c a t")[:, :, cols], turned_sb[:, s, :, cols]).then_inc(stored.sem, 16)
                sp.wait_ge(stored.sem, stored.at(16 * 2 * NQ))
                if loads:
                    sp.wait_ge(loaded.sem, loaded.at(16 * len(loads)))

        loaded.done(16 * len(loads))
        projected.done(len(units))
        evacuated.done(len(units))
        for a in range(2):
            ready[a].done(NQ)
            rounded[a].done(2 * NQ)
            left[a].done(2 * NQ)
        for a in range(PARTS):
            turned[a].done(NQ)
            copied[a].done(NQ)
        stored.done(16 * 2 * NQ)
        step_v.done(counts[0])
        step_p.done(counts[1])
        if norm:
            weighted.done(1)
            for sig in (squared, ms_ready, rms_ready, inverted):
                sig.done(NQ)




def attention_stage(k, w, v, parts_dram, scale, y):
    nc = k.nc
    MAXU = []
    for i in range(NT):
        pieces = [(c * BANK, min(BANK, (i + 1) * P - c * BANK)) for c in range(i // QC + 1)]
        if i == NT - 1:
            pieces[0:1] = [(0, BANK // 2), (BANK // 2, BANK // 2)]
        MAXU += [(i, at, width, n) for n, (at, width) in enumerate(pieces)]
    EXPU = []
    for j in range(NQ):
        for u in range(2 * j):
            EXPU.append((j, [(2 * u, 0), (2 * u + 1, 0)]))
        EXPU.append((j, [(QC * j, 0), (QC * j + 1, 1)]))
        EXPU.append((j, [(QC * j + 2, 2), (QC * j + 3, 3)]))
    NM, NE = len(MAXU), len(EXPU)
    OWN = [e for e in range(NE) if EXPU[e][1][0][0] >= QC * EXPU[e][0]]
    VT = NT // len(OWN)
    VN = len(OWN) - 1
    GROUPS = [(0, 2), (2, 3), (3, 4)]
    NG = len(GROUPS)
    MAX_END = [sum(i < QC * hi for i, *_ in MAXU) for _, hi in GROUPS]
    FIRST_EXP = [min(e for e in range(NE) if EXPU[e][0] == lo) for lo, _ in GROUPS]
    OWN_AT, NEXT_AT, OUT_AT = 2, (9, 15), 0
    PLAN = []
    for e in range(NE):
        if e == OWN_AT:
            PLAN.append((e, "own_shift", NG - 1))
        for g, at in enumerate(NEXT_AT):
            if e == at:
                PLAN.append((e, "next_shift", g))
        PLAN += [(e, "max", u) for u in range(e * NM // NE, (e + 1) * NM // NE)]
        if e == OUT_AT:
            PLAN.append((e, "out", None))
    HEAD0_PLAN = [p for p in PLAN if p[1] != "out"]
    LAST_PLAN = [p for p in PLAN if p[1] in ("own_shift", "out")] + [(NE, "own_out", None)]
    FIRST_PLAN = [(0, "max", u) for u in range(NM)] + [(0, "next_shift", g) for g in range(NG - 1)]
    STATU, PRE = len(PLAN), len(FIRST_PLAN)
    AT, AT0 = ({(kind, arg): n for n, (_, kind, arg) in enumerate(plan)} for plan in (PLAN, HEAD0_PLAN))
    for g, at in enumerate(NEXT_AT):
        assert AT["max", MAX_END[g] - 1] < AT["next_shift", g]
    RING, PSLOTS = 3, 4
    assert STATU % RING == 0 and NE % PSLOTS == 0 and NE % 2 == 0
    TAIL = PRE - 1 + (H - 1) * STATU
    counts = []
    with ExitStack() as ctx:
        qm, km, qe, ke = w["q_max"], w["k_max"], w["q_exp"], w["k_exp"]
        probs = k.sb("probs", [P, PSLOTS, 2 * BANK], F32, ctx)
        vh = k.sb("v_head", [P, 2, NT, 32], F32, ctx)
        early = k.sb("v_early", [P, 2 * VT, D], F32, ctx)
        mpart = k.sb("max_part", [P, 2, NT, NQ + 1], F32, ctx)
        mx = k.sb("row_max", [P, 2, NT], F32, ctx)
        mxb = k.sb("row_max_parts", [P, 2, SHIFT * NT], BF16, ctx)
        mxt = [k.sb(f"row_max_turned{g}", [SHIFT * QC * (hi - lo), 2, P], BF16, ctx) for g, (lo, hi) in enumerate(GROUPS)]
        ot = k.sb("out_turned", [P, 2, BANK], F32, ctx)
        rden = k.sb("inv_denominator", [P, 2, NT], F32, ctx)
        ring = [k.ps(f"stat{n}", [P, BANK], ctx) for n in range(RING)]
        sc = [k.ps(f"score{n}", [P, 2 * BANK], ctx) for n in range(2)]
        acc = k.ps("pv", [P, BANK], ctx)

        m_loaded = [k.counter(f"max_rows_loaded{n}") for n in range(2)]
        e_loaded = [k.counter(f"exp_rows_loaded{n}") for n in range(2)]
        shift_in = [[k.counter(f"shift_rows_loaded{n}_{g}") for g in range(NG)] for n in range(2)]
        stat_full, stat_used = k.counter("stat_bank_full"), k.counter("stat_bank_used")
        max_step, max_ready = k.counter("max_step"), k.counter("row_max_ready")
        scored, expd, pv_done = k.counter("scores_ready"), k.counter("probs_ready"), k.counter("pv_done")
        out_copied, v_ready, cut = k.counter("pv_copied_out"), k.counter("v_head_ready"), k.counter("probs_masked")
        v_early = k.counter("v_early_rows")
        q_rows, k_rows = (parts_dram[s].rearrange("a (h d) t -> h a d t", d=D) for s in range(2))

        def load_rows(sp, qt, kt, par, h, loaded):
            for a in range(PARTS):
                at = slice(a * PARTS * D, (a + 1) * PARTS * D)
                sp.dma_start(qt[at, par, :], bcast(q_rows[h, a], 0, PARTS)).then_inc(loaded.sem, 16)
                sp.dma_start(kt[at, par, :], k_rows[h]).then_inc(loaded.sem, 16)

        NL = 2 * PARTS * 16
        NS = SHIFT * 16

        def base(h):
            return PRE if isinstance(h, int) and h == 0 else h * STATU + (PRE - 1)

        with nc.Block() as block:

            @block.sync
            def _(sp):
                def load_max(h, par):
                    load_rows(sp, qm, km, par, h, m_loaded[par])

                def load_exp(h, par, prev):
                    if prev is not None:
                        sp.wait_ge(scored.sem, scored.at(NE * prev + NE))
                    load_rows(sp, qe, ke, par, h, e_loaded[par])

                def load_shift(par, g, used):
                    sp.wait_ge(stat_used.sem, stat_used.at(used))
                    lo, hi = GROUPS[g]
                    nt = QC * (hi - lo)
                    for n in range(SHIFT):
                        r = KROWS + n
                        sp.dma_start(qe[r:r + 1, par, lo * BANK:hi * BANK].rearrange("o (i q) -> o i q", q=P),
                                     mxt[g][n * nt:(n + 1) * nt, par, :]).then_inc(shift_in[par][g].sem, 16)

                load_max(0, 0)
                load_max(1, 1)
                load_exp(0, 0, None)
                for g in range(NG - 1):
                    load_shift(0, g, NM + g + 1)

                def body(h, par, prev=True, max_load=True):
                    nxt = 1 - par
                    if max_load:
                        sp.wait_ge(stat_full.sem, stat_full.at(base(h)))
                        load_max(h + 2, par)
                    load_exp(h + 1, nxt, h - 1 if prev else None)
                    at = AT0 if isinstance(h, int) and h == 0 else AT
                    load_shift(par, NG - 1, base(h) + (at["own_shift", NG - 1] + 1))
                    for g in range(NG - 1):
                        load_shift(nxt, g, base(h) + (at["next_shift", g] + 1))

                body(0, 0, prev=False)
                body(1, 1)
                with sp.Fori(1, H // 2 - 1) as i:
                    for par in range(2):
                        body(2 * i + par, par)
                body(H - 2, 0, max_load=False)
                load_shift(1, NG - 1, TAIL + [kind for _, kind, _ in LAST_PLAN].index("own_shift") + 1)

            @block.gpsimd
            def _(pool):
                nc.gpsimd.memset(vh[:], 0.0).then_inc(v_ready.sem, 1)
                pool.wait_ge(v_ready.sem, v_ready.at(1))
                nc.gpsimd.memset(vh[:, :, :, D:D + 1], 1.0).then_inc(v_ready.sem, 1)
                pool.wait_ge(v_ready.sem, v_ready.at(2))

                def gather(h, dst, tiles, done):
                    nc.gpsimd.tensor_copy(dst, v[:, tiles, bass.ds(2 * C + h * D, D)]).then_inc(done.sem, 1)

                def body(h, par, more=True):
                    for n, e in enumerate(OWN):
                        pool.wait_ge(expd.sem, expd.at(h * NE + (e + 1)))
                        tiles = slice(n * VT, (n + 1) * VT)
                        if more and n < 2:
                            if n == 0 and not (isinstance(h, int) and h == 1):
                                pool.wait_ge(v_ready.sem, v_ready.at(h * VN + (2 - VN)))
                            gather(h + 1, early[:, tiles, :], tiles, v_early)
                        elif more:
                            if n == 2:
                                pool.wait_ge(pv_done.sem, pv_done.at(h * NE))
                                pool.wait_ge(v_early.sem, v_early.at(2 * h))
                            gather(h + 1, vh[:, 1 - par, tiles, 0:D], tiles, v_ready)
                            if n == 2:
                                nc.gpsimd.tensor_copy(vh[:, 1 - par, 0:2 * VT, 0:D], early[:]).then_inc(v_ready.sem, 1)
                        second = BANK - EXPU[e][1][0][1] * P
                        tile = probs[:, e % PSLOTS, 0:2 * second].rearrange("p (u q) -> p u q", q=second)[:, :, 0:P]
                        nc.gpsimd.affine_select(tile, tile, [[0, 2], [1, P]], ALU.is_ge, 0.0, base=0, channel_multiplier=-1).then_inc(cut.sem, 1)

                for h in range(2):
                    gather(h, vh[:, h, :, 0:D], slice(0, NT), v_ready)
                for h in range(2):
                    body(h, h, more=h > 0)
                with pool.Fori(1, H // 2 - 1) as i:
                    for par in range(2):
                        body(2 * i + par, par)
                body(H - 2, 0)
                body(H - 1, 1, more=False)

            @block.scalar
            def _(act):
                def copy_out(h, par, first_two=False):
                    act.wait_ge(pv_done.sem, pv_done.at(NE * h + NE))
                    if not first_two:
                        act.wait_ge(stat_full.sem, stat_full.at(base(h)))
                    nc.scalar.copy(ot[:, par, :], acc[:]).then_inc(out_copied.sem, 1)

                def body(h, par, head=None):
                    for e, (j, tiles) in enumerate(EXPU):
                        if e == 2 and head != 0:
                            copy_out(h - 1, 1 - par, first_two=head in (1, 2))
                        n = NE * h + e
                        act.wait_ge(scored.sem, scored.at(n + 1))
                        if head != 0 or e >= PSLOTS:
                            act.wait_ge(pv_done.sem, pv_done.at(n + 1 - PSLOTS))
                        width = sum(BANK - f * P for _, f in tiles)
                        nc.scalar.activation(probs[:, e % PSLOTS, 0:width], sc[e % 2][:, 0:width], ACT.Exp,
                                             scale=scale).then_inc(expd.sem, 1)

                for h in range(3):
                    body(h, h % 2, head=h)
                with act.Fori(1, H // 2 - 1) as i:
                    body(2 * i + 1, 1)
                    body(2 * i + 2, 0)
                body(H - 1, 1)
                copy_out(H - 1, 1)

            @block.tensor
            def _(pe):
                def max_unit(n, unit, par):
                    i, at, width, _ = MAXU[unit]
                    out = ring[n % RING]
                    own = at + width > i * P
                    last = nc.tensor.matmul(out[:, 0:width], qm[:, par, i * P:(i + 1) * P],
                                            km[:, par, at:at + width], start=True, stop=not own)
                    if own:
                        last = nc.tensor.matmul(out[:, width - P:width], w["ident16"][:], w["mask16"][:], start=False, stop=True)
                    last.then_inc(stat_full.sem, 1)

                def shift_unit(n, par, g):
                    lo, hi = (SHIFT * QC * c for c in GROUPS[g])
                    nc.tensor.transpose(ring[n % RING][0:hi - lo, 0:P // 2].bitcast(BF16), mxb[:, par, lo:hi], w["ident16"][:]).then_inc(stat_full.sem, 1)

                def out_unit(n, par):
                    for j in range(NQ):
                        last = nc.tensor.transpose(ring[n % RING][:, j * P:(j + 1) * P], ot[:, par, j * P:(j + 1) * P], w["ident"][:])
                    last.then_inc(stat_full.sem, 1)

                def scores(e, par):
                    j, tiles = EXPU[e]
                    at = 0
                    for kt, f in tiles:
                        width = BANK - f * P
                        out = sc[e % 2][:, at:at + width]
                        last = nc.tensor.matmul(out, ke[:, par, kt * P:(kt + 1) * P],
                                                qe[:, par, j * BANK + f * P:(j + 1) * BANK], start=True, stop=True)
                        at += width
                    last.then_inc(scored.sem, 1)

                def pv(e, par):
                    j, tiles = EXPU[e]
                    at = 0
                    for kt, f in tiles:
                        for c in range(f, QC):
                            last = nc.tensor.matmul(acc[32 * c:32 * c + 32, j * P:(j + 1) * P], vh[:, par, kt, :],
                                                    probs[:, e % PSLOTS, at:at + P], start=kt == 0, stop=kt == QC * j + c,
                                                    tile_position=(0, 32 * c))
                            at += P
                    last.then_inc(pv_done.sem, 1)

                pe.wait_ge(m_loaded[0].sem, m_loaded[0].at(NL))
                for n, (_, kind, arg) in enumerate(FIRST_PLAN):
                    if kind == "next_shift":
                        pe.wait_ge(max_ready.sem, max_ready.at(arg + 1))
                    if n >= RING:
                        pe.wait_ge(stat_used.sem, stat_used.at(n + 1 - RING))
                    max_unit(n, arg, 0) if kind == "max" else shift_unit(n, 0, arg)
                pe.wait_ge(e_loaded[0].sem, e_loaded[0].at(NL))
                pe.wait_ge(shift_in[0][0].sem, shift_in[0][0].at(NS))
                scores(0, 0)
                scores(1, 0)

                def body(h, turn, par, plan=PLAN):
                    nxt = 1 - par
                    more = plan is not LAST_PLAN
                    pe.wait_ge(v_ready.sem, v_ready.at(3 if isinstance(h, int) and h == 0 else h * VN + (4 - VN)))
                    if more:
                        pe.wait_ge(m_loaded[nxt].sem, m_loaded[nxt].at(turn * NL + (1 + par) * NL))
                    first = 0 if plan is HEAD0_PLAN else -1
                    for e in range(NE + 1):
                        if e < NE:
                            pe.wait_ge(expd.sem, expd.at(h * NE + (e + 1)))
                            if e + 2 < NE:
                                if e + 2 in FIRST_EXP:
                                    g = FIRST_EXP.index(e + 2)
                                    pe.wait_ge(shift_in[par][g].sem, shift_in[par][g].at(turn * NS + NS))
                                scores(e + 2, par)
                            elif more:
                                if e + 2 == NE:
                                    pe.wait_ge(e_loaded[nxt].sem, e_loaded[nxt].at(turn * NL + (1 + par) * NL))
                                    pe.wait_ge(shift_in[nxt][0].sem, shift_in[nxt][0].at(turn * NS + (1 + par) * NS))
                                scores(e + 2 - NE, nxt)
                            if e not in OWN and e != OUT_AT:
                                pv(e, par)
                        for n, (at, kind, arg) in enumerate(plan):
                            if at != e:
                                continue
                            n += PRE + first
                            if kind == "out":
                                pe.wait_ge(out_copied.sem, out_copied.at(h))
                            elif kind == "own_out":
                                pe.wait_ge(out_copied.sem, out_copied.at(h + 1))
                            elif kind == "own_shift":
                                pe.wait_ge(max_ready.sem, max_ready.at(h * NG + (arg + 1)))
                            elif kind == "next_shift":
                                pe.wait_ge(max_ready.sem, max_ready.at(h * NG + (NG + arg + 1)))
                            pe.wait_ge(stat_used.sem, stat_used.at(h * STATU + (n + 1 - RING)))
                            if kind == "max":
                                max_unit(n, arg, nxt)
                            elif kind in ("out", "own_out"):
                                out_unit(n, nxt if kind == "out" else par)
                            else:
                                shift_unit(n, par if kind == "own_shift" else nxt, arg)
                        if e in OWN or e == OUT_AT:
                            if e in OWN:
                                pe.wait_ge(cut.sem, cut.at(h * len(OWN) + (OWN.index(e) + 1)))
                            pv(e, par)

                body(0, 0, 0, plan=HEAD0_PLAN)
                with pe.Fori(0, H // 2 - 1) as i:
                    body(2 * i + 1, i, 1)
                    body(2 * i + 2, i + 1, 0)
                body(H - 1, H // 2 - 1, 1, plan=LAST_PLAN)

            @block.vector
            def _(dve):
                chain = Chain(dve, max_step)

                steps = [0, 0]

                def step(ins):
                    steps[1] += 1
                    ins.then_inc(max_step.sem, 1)
                    dve.wait_ge(max_step.sem, max_step.at(steps[0] + steps[1]))

                def max_unit(n, at, unit, par):
                    i, _, width, col = MAXU[unit]
                    dve.wait_ge(stat_full.sem, stat_full.at(n + 1))
                    nc.vector.reduce_max(mpart[:, par, i, col:col + 1], ring[at % RING][:, 0:width], AX.X).then_inc(stat_used.sem, 1)
                    if unit + 1 in MAX_END:
                        dve.wait_ge(stat_used.sem, stat_used.at(n + 1))
                        row_max(par, MAX_END.index(unit + 1))

                def row_max(par, g):
                    lo, hi = (QC * c for c in GROUPS[g])
                    high, low = mxb[:, par, 2 * lo:lo + hi], mxb[:, par, lo + hi:2 * hi]
                    step(nc.vector.tensor_reduce(mx[:, par, lo:hi], mpart[:, par, lo:hi, :], AX.X, ALU.max))
                    step(nc.vector.tensor_copy(high, mx[:, par, lo:hi]))
                    nc.vector.tensor_tensor(low, mx[:, par, lo:hi], high, ALU.subtract).then_inc(max_ready.sem, 1)

                def shift_unit(n, at, par, g, earlier):
                    if earlier is not None:
                        dve.wait_ge(shift_in[par][g].sem, shift_in[par][g].at(earlier))
                    dve.wait_ge(stat_full.sem, stat_full.at(n + 1))
                    rows = mxt[g].shape[0]
                    nc.vector.tensor_copy(mxt[g][:, par, :], ring[at % RING][0:rows, 0:P // 2].bitcast(BF16)).then_inc(stat_used.sem, 1)

                def out_unit(n, at, h, par):
                    dve.wait_ge(stat_full.sem, stat_full.at(n + 1))
                    o = ring[at % RING][:].rearrange("p (t x) -> p t x", x=32)
                    step(nc.vector.reciprocal(rden[:, par, :], o[:, :, D]))
                    nc.vector.tensor_tensor(y[:, :, bass.ds(h * D, D)], o[:, :, 0:D], bcast(rden[:, par, :], 2, D),
                                            ALU.mult).then_inc(stat_used.sem, 1)

                step(nc.vector.memset(mpart[:], -3e38))
                for n, (_, kind, arg) in enumerate(FIRST_PLAN):
                    if kind == "max":
                        max_unit(n, n, arg, 0)
                    else:
                        shift_unit(n, n, 0, arg, None)

                def body(h, turn, par, plan=PLAN):
                    own = None if turn is None else turn * NS
                    nxt = turn * NS + par * NS if turn is not None else par * NS or None
                    for n, (_, kind, arg) in enumerate(plan):
                        n += PRE if plan is HEAD0_PLAN else PRE - 1
                        unit = h * STATU + n
                        if kind == "max":
                            max_unit(unit, n, arg, 1 - par)
                        elif kind == "out":
                            out_unit(unit, n, h - 1, 1 - par)
                        elif kind == "own_out":
                            out_unit(unit, n, h, par)
                        elif kind == "own_shift":
                            shift_unit(unit, n, par, arg, own)
                        else:
                            shift_unit(unit, n, 1 - par, arg, nxt)

                body(0, None, 0, plan=HEAD0_PLAN)
                before = steps[1]
                body(1, None, 1)
                per_head = steps[1] - before
                before = steps[1]
                with dve.Fori(1, H // 2 - 1) as i:
                    for par in range(2):
                        steps[0], steps[1] = i * (2 * per_head) + (before - 2 * per_head), par * per_head
                        body(2 * i + par, i, par)
                steps[0], steps[1] = before + (H - 4) * per_head, 0
                body(H - 2, H // 2 - 1, 0)
                body(H - 1, H // 2 - 1, 1, plan=LAST_PLAN)
                counts.append(steps[0] + steps[1])

        for par in range(2):
            m_loaded[par].done(NL * H // 2)
            e_loaded[par].done(NL * H // 2)
            for g in range(NG):
                shift_in[par][g].done(NS * H // 2)
        stat_full.done(TAIL + len(LAST_PLAN))
        stat_used.done(TAIL + len(LAST_PLAN))
        max_step.done(counts[0])
        max_ready.done(NG * H)
        scored.done(NE * H)
        expd.done(NE * H)
        pv_done.done(NE * H)
        out_copied.done(H)
        v_ready.done(4 + VN * (H - 2))
        v_early.done(2 * (H - 2))
        cut.done(len(OWN) * H)




def spline_ffn_stage(k, w, xn_t, x):
    nc = k.nc
    HALF = T // 2
    with ExitStack() as ctx:
        s2 = k.sb("spline_in", [P, HALF], F32, ctx)
        knot = k.sb("spline_knot", [P, 4, HALF], F32, ctx)
        g = k.sb("spline_sum", [P, 2, HALF], F32, ctx)
        sp_in = k.ps("spline_in_ps", [P, 2, BANK], ctx)
        out = k.ps("spline_out_ps", [P, 4, BANK], ctx)
        fed, s_ready, knots, summed = k.counter("spline_fed"), k.counter("spline_s"), k.counter("spline_knots"), k.counter("spline_summed")
        out_ready, biased, out_used = k.counter("spline_out"), k.counter("spline_biased"), k.counter("spline_out_used")
        with nc.Block() as block:

            @block.tensor
            def _(pe):
                for c in range(2):
                    for half in range(2):
                        ins = nc.tensor.matmul(sp_in[half * M0:half * M0 + M0, c, :], w["Win"][:],
                                               xn_t[:, half * HALF + c * BANK:half * HALF + (c + 1) * BANK], start=True, stop=True,
                                               tile_position=(0, half * M0))
                    ins.then_inc(fed.sem, 1)
                pe.wait_ge(summed.sem, summed.at(INNER))
                for q in range(NQ):
                    half = q // 2
                    at = slice(half * M0, half * M0 + M0)
                    for i in range(QC):
                        t0 = (q % 2) * BANK + i * P
                        ins = nc.tensor.matmul(out[:, q, i * P:(i + 1) * P], g[at, (INNER - 1) % 2, t0:t0 + P], w["Wout"][at, :],
                                               start=True, stop=True)
                    ins.then_inc(out_ready.sem, 1)

            @block.scalar
            def _(act):
                for c in range(2):
                    act.wait_ge(fed.sem, fed.at(c + 1))
                    nc.scalar.activation(s2[:, c * BANK:(c + 1) * BANK], sp_in[:, c, :], ACT.Identity,
                                         bias=w["bin"][:, 0:1]).then_inc(s_ready.sem, 1)
                act.wait_ge(s_ready.sem, s_ready.at(2))
                for h in range(INNER):
                    if h >= 4:
                        act.wait_ge(summed.sem, summed.at(h - 3))
                    nc.scalar.activation(knot[:, h % 4, :], s2[:], ACT.Relu, bias=w["b1"][:, h:h + 1],
                                         scale=w["W1"][:, h:h + 1]).then_inc(knots.sem, 1)

            @block.gpsimd
            def _(pool):
                nc.gpsimd.tensor_tensor(x[:], x[:], bcast(w["bout"][:], 1, NT), ALU.add).then_inc(biased.sem, 1)

            @block.vector
            def _(dve):
                for h in range(INNER):
                    dve.wait_ge(knots.sem, knots.at(h + 1))
                    if h == 0:
                        ins = nc.vector.tensor_scalar(g[:, 0, :], knot[:, 0, :], w["W2"][:, 0:1], w["b2"][:, 0:1], ALU.mult, ALU.add)
                    else:
                        dve.wait_ge(summed.sem, summed.at(h))
                        ins = nc.vector.scalar_tensor_tensor(g[:, h % 2, :], knot[:, h % 4, :], w["W2"][:, h:h + 1],
                                                             g[:, (h - 1) % 2, :], ALU.mult, ALU.add)
                    ins.then_inc(summed.sem, 1)
                dve.wait_ge(biased.sem, biased.at(1))
                for q in range(NQ):
                    dve.wait_ge(out_ready.sem, out_ready.at(q + 1))
                    part = x[:, QC * q:QC * q + QC, :]
                    nc.vector.tensor_tensor(part, out[:, q, :].rearrange("p (i c) -> p i c", c=C), part, ALU.add).then_inc(out_used.sem, 1)

        fed.done(2)
        s_ready.done(2)
        knots.done(INNER)
        summed.done(INNER)
        out_ready.done(NQ)
        biased.done(1)
        out_used.done(NQ)




def chunk_stage(k, w, kk, v, q_t, k_t, width, keep, out, inner=True):
    nc = k.nc
    VW = H * width
    NB = H * P // BANK
    HP = H // 2
    SLOTS = 4
    with ExitStack() as ctx:
        qts = k.sb("tile_q_t", [P, SLOTS, P], F32, ctx)
        ks = k.sb("tile_k", [P, SLOTS, P], F32, ctx)
        vs = k.sb("tile_v", [P, SLOTS, H, 32 if inner else width], F32, ctx)
        state = k.sb("state", [P, SLOTS, VW], F32, ctx)
        o_ps = [k.ps(f"tile_out_ps{n}", [P, BANK], ctx) for n in range(2)]
        u_ps = k.ps("state_ps", [P, BANK], ctx)
        if inner:
            kts = k.sb("tile_k_t", [P, SLOTS, P], F32, ctx)
            qx = k.sb("tile_q_heads", [P, SLOTS, H, P], F32, ctx)
            sm = k.sb("tile_scores", [P, 2, NB, BANK], F32, ctx)
            ot = k.sb("tile_out_turned", [P, BANK], F32, ctx)
            pv_ps = k.ps("tile_pv_ps", [P, BANK], ctx)
            st_ps = [k.ps(f"tile_scores_ps{n}", [P, BANK], ctx) for n in range(NB)]
        staged, masked, s_full = k.counter("tile_staged"), k.counter("tile_masked"), k.counter("tile_scored")
        o_ready, o_used, u_ready, u_kept = k.counter("tile_out"), k.counter("tile_out_used"), k.counter("state_grown"), k.counter("state_kept")
        spread_act, cleared = k.counter("tile_spread_act"), k.counter("tile_v_cleared")
        pv_ready, pv_copied = k.counter("tile_pv"), k.counter("tile_pv_copied")
        NS = 5 if inner else 1
        staged_k, staged_v = k.counter("tile_staged_k"), k.counter("tile_staged_v")
        with nc.Block() as block:

            @block.gpsimd
            def _(pool):
                def body(i, slot, first=False):
                    if not first:
                        pool.wait_ge(o_ready.sem, o_ready.at(i - (SLOTS - 1)))
                    nc.gpsimd.tensor_copy(qts[:, slot, :], q_t[:, bass.ds(i * P, P)]).then_inc(staged.sem, 1)
                    if inner:
                        nc.gpsimd.tensor_copy(kts[:, slot, :], k_t[:, bass.ds(i * P, P)]).then_inc(staged.sem, 1)
                        pool.wait_ge(staged.sem, staged.at(i * NS + 1))
                        nc.gpsimd.tensor_tensor(qx[:, slot, 0:HP, :], bcast(qts[:, slot, :], 1, HP), bcast(w["headmask"][:, 0:HP], 2, P), ALU.mult).then_inc(staged.sem, 1)
                    if inner:
                        nc.gpsimd.tensor_copy(ks[:, slot, :], kk[:, bass.ds(i, 1), :]).then_inc(staged.sem, 1)
                        nc.gpsimd.tensor_copy(vs[:, slot, :, 0:width], v[:, bass.ds(i, 1), :].rearrange("p o (h e) -> p (o h) e", e=width)).then_inc(staged.sem, 1)

                if inner:
                    nc.gpsimd.memset(vs[:], 0.0).then_inc(cleared.sem, 1)
                    pool.wait_ge(cleared.sem, cleared.at(1))
                for slot in range(SLOTS):
                    body(slot, slot, first=True)
                with pool.Fori(1, NT // SLOTS) as n:
                    for slot in range(SLOTS):
                        body(SLOTS * n + slot, slot)

            @block.tensor
            def _(pe):
                def scores(i, slot, first=False):
                    pe.wait_ge(staged.sem, staged.at(i * NS + NS))
                    if not inner:
                        pe.wait_ge(staged_k.sem, staged_k.at(i + 1))
                        pe.wait_ge(staged_v.sem, staged_v.at(i + 1))
                    if inner:
                        if not first:
                            pe.wait_ge(masked.sem, masked.at(i * NB))
                        pe.wait_ge(spread_act.sem, spread_act.at(i + 1))
                        for b in range(NB):
                            nc.tensor.matmul(st_ps[b][:], kts[:, slot, :], qx[:, slot, b * QC:(b + 1) * QC, :].rearrange("p j t -> p (j t)"),
                                             start=True, stop=True).then_inc(s_full.sem, 1)
                    pe.wait_ge(u_kept.sem, u_kept.at(i + 1))
                    nc.tensor.matmul(u_ps[:, 0:VW].rearrange("p (h e) -> p h e", e=width), ks[:, slot, :], vs[:, slot, :, 0:width], start=first, stop=True, skip_group_check=True).then_inc(u_ready.sem, 1)

                def within(i, slot, first=False):
                    pe.wait_ge(masked.sem, masked.at(i * NB + NB))
                    if not first:
                        pe.wait_ge(pv_copied.sem, pv_copied.at(i))
                    for h in range(H):
                        g, j = h % QC, h // QC
                        ins = nc.tensor.matmul(pv_ps[32 * g:32 * g + 32, j * P:(j + 1) * P], vs[:, slot, h, :], sm[:, slot % 2, j, g * P:(g + 1) * P],
                                               start=True, stop=True, tile_position=(0, 32 * g))
                    ins.then_inc(pv_ready.sem, 1)

                def finish(i, slot, first_two=False):
                    if not first_two:
                        pe.wait_ge(o_used.sem, o_used.at(i - 1))
                    o = o_ps[slot % 2]
                    ins = nc.tensor.matmul(o[:, 0:VW], qts[:, slot, :], state[:, slot, :], start=True, stop=not inner)
                    if inner:
                        pe.wait_ge(pv_copied.sem, pv_copied.at(i + 1))
                        rows = w["ident"][:].rearrange("p (g e) -> p g e", e=32)[:, :, 0:width]
                        for j in range(H // QC):
                            ins = nc.tensor.matmul(o[:, j * QC * width:(j + 1) * QC * width].rearrange("p (g e) -> p g e", e=width),
                                                   ot[:, j * P:(j + 1) * P], rows, start=False, stop=j == H // QC - 1)
                    ins.then_inc(o_ready.sem, 1)

                def body(i, slot, step=None):
                    scores(i, slot, first=step == 0)
                    if step is None or step >= 2:
                        finish(i - 2, (slot - 2) % SLOTS, first_two=step in (2, 3))
                    if inner and step != 0:
                        within(i - 1, (slot - 1) % SLOTS, first=step == 1)

                for i in range(SLOTS):
                    body(i, i, step=i)
                with pe.Fori(1, NT // SLOTS) as n:
                    for slot in range(SLOTS):
                        body(SLOTS * n + slot, slot)
                finish(NT - 2, SLOTS - 2)
                if inner:
                    within(NT - 1, SLOTS - 1)
                finish(NT - 1, SLOTS - 1)

            @block.vector
            def _(dve):
                nc.vector.memset(state[:, 0, :], 0.0).then_inc(u_kept.sem, 1)

                def stage_k(i, slot, first=False):
                    if not first:
                        dve.wait_ge(o_ready.sem, o_ready.at(i - (SLOTS - 1)))
                    nc.vector.tensor_copy(ks[:, slot, :], kk[:, bass.ds(i, 1), :]).then_inc(staged_k.sem, 1)

                if not inner:
                    for slot in range(2):
                        stage_k(slot, slot, first=True)

                def body(i, slot, first_two=False, early=False, last=False, ahead=True):
                    par = slot % 2
                    if inner:
                        for b in range(NB):
                            dve.wait_ge(s_full.sem, s_full.at(i * NB + (b + 1)))
                            if b == 0 and not first_two:
                                dve.wait_ge(pv_ready.sem, pv_ready.at(i - 1))
                            nc.vector.tensor_tensor(sm[:, par, b, :].rearrange("p (j t) -> p j t", t=P), st_ps[b][:].rearrange("p (j t) -> p j t", t=P),
                                                    bcast(w["keep_kq"][:], 1, QC), ALU.mult).then_inc(masked.sem, 1)
                    if not last:
                        dve.wait_ge(u_ready.sem, u_ready.at(i + 1))
                        if not early:
                            dve.wait_ge(o_ready.sem, o_ready.at(i - 2))
                        nc.vector.tensor_tensor(state[:, (slot + 1) % SLOTS, :], u_ps[:, 0:VW], keep, ALU.mult).then_inc(u_kept.sem, 1)
                    if not inner and ahead:
                        stage_k(i + 2, (slot + 2) % SLOTS, first=first_two)

                for i in range(SLOTS):
                    body(i, i, first_two=i < 2, early=i < 3)
                with dve.Fori(1, NT // SLOTS - 1) as n:
                    for slot in range(SLOTS):
                        body(SLOTS * n + slot, slot)
                for slot in range(SLOTS):
                    body(NT - SLOTS + slot, slot, last=slot == SLOTS - 1, ahead=slot < 2)

            @block.scalar
            def _(act):
                def spread_heads(i, slot):
                    act.wait_ge(staged.sem, staged.at(i * NS + 1))
                    for h in range(HP, H):
                        ins = nc.scalar.activation(qx[:, slot, h, :], qts[:, slot, :], ACT.Copy, scale=w["headmask"][:, h:h + 1])
                    ins.then_inc(spread_act.sem, 1)

                def copy_pv(i, first=False):
                    act.wait_ge(pv_ready.sem, pv_ready.at(i + 1))
                    if not first:
                        act.wait_ge(o_ready.sem, o_ready.at(i))
                    nc.scalar.copy(ot[:], pv_ps[:]).then_inc(pv_copied.sem, 1)

                def take_out(i, par):
                    act.wait_ge(o_ready.sem, o_ready.at(i + 1))
                    nc.scalar.copy(out[:, bass.ds(i, 1), :], o_ps[par][:, 0:VW]).then_inc(o_used.sem, 1)

                if inner:
                    for slot in range(SLOTS):
                        spread_heads(slot, slot)
                def stage_v(i, slot):
                    nc.scalar.copy(vs[:, slot, :, 0:width], v[:, bass.ds(i, 1), :].rearrange("p o (h e) -> p (o h) e", e=width)).then_inc(staged_v.sem, 1)

                if not inner:
                    for slot in range(SLOTS):
                        stage_v(slot, slot)

                def body(i, slot, first=False, more=True):
                    if inner:
                        copy_pv(i, first=first)
                        if more:
                            spread_heads(i + SLOTS, slot)
                    take_out(i, slot % 2)
                    if not inner and more:
                        stage_v(i + SLOTS, slot)

                body(0, 0, first=True)
                for slot in range(1, SLOTS):
                    body(slot, slot)
                with act.Fori(1, NT // SLOTS - 1) as n:
                    for slot in range(SLOTS):
                        body(SLOTS * n + slot, slot)
                for slot in range(SLOTS):
                    body(NT - SLOTS + slot, slot, more=False)

        staged.done(NS * NT)
        if not inner:
            staged_k.done(NT)
            staged_v.done(NT)
        if inner:
            spread_act.done(NT)
            cleared.done(1)
            pv_ready.done(NT)
            pv_copied.done(NT)
            s_full.done(NB * NT)
            masked.done(NB * NT)
        o_ready.done(NT)
        o_used.done(NT)
        u_ready.done(NT)
        u_kept.done(NT)


def linear_features_stage(k, w, qkv, v9):
    nc = k.nc
    with ExitStack() as ctx:
        low = k.sb("elu_exp", [P, NT, 2 * C], F32, ctx)
        clipped, exped, step, v_step = k.counter("elu_clipped"), k.counter("elu_exp"), k.counter("elu_step"), k.counter("v9_step")
        v_act = k.counter("v9_act")
        SHARE = 10
        counts = []
        with nc.Block() as block:

            @block.vector
            def _(dve):
                chain = Chain(dve, step)
                for n in range(2):
                    nc.vector.tensor_scalar(low[:, :, n * C:(n + 1) * C], qkv[:, :, n * C:(n + 1) * C], 0.0, None, ALU.min).then_inc(clipped.sem, 1)
                for n in range(2):
                    dve.wait_ge(exped.sem, exped.at(n + 1))
                    part = qkv[:, :, n * C:(n + 1) * C]
                    chain(nc.vector.scalar_tensor_tensor(part, part, 0.0, low[:, :, n * C:(n + 1) * C], ALU.max, ALU.add))
                chain(nc.vector.tensor_scalar(qkv[:, :, 0:C], qkv[:, :, 0:C], float(D) ** -0.5, None, ALU.mult))
                counts.append(chain.n)

            @block.scalar
            def _(act):
                for n in range(2):
                    act.wait_ge(clipped.sem, clipped.at(n + 1))
                    part = low[:, :, n * C:(n + 1) * C]
                    nc.scalar.activation(part, part, ACT.Exp).then_inc(exped.sem, 1)
                act.wait_ge(v_step.sem, v_step.at(1))
                for i in range(SHARE, NT):
                    ins = nc.scalar.copy(v9[:, i, :].rearrange("p (h e) -> p h e", e=D + 1)[:, :, 0:D],
                                         qkv[:, i, 2 * C:3 * C].rearrange("p (h d) -> p h d", d=D))
                ins.then_inc(v_act.sem, 1)

            @block.gpsimd
            def _(pool):
                nc.gpsimd.memset(v9[:], 1.0).then_inc(v_step.sem, 1)
                pool.wait_ge(v_step.sem, v_step.at(1))
                for i in range(SHARE):
                    ins = nc.gpsimd.tensor_copy(v9[:, i, :].rearrange("p (h e) -> p h e", e=D + 1)[:, :, 0:D],
                                                qkv[:, i, 2 * C:3 * C].rearrange("p (h d) -> p h d", d=D))
                ins.then_inc(v_step.sem, 1)

        clipped.done(2)
        exped.done(2)
        step.done(counts[0])
        v_step.done(2)
        v_act.done(1)


def linear_divide_stage(k, num, y):
    nc = k.nc
    with ExitStack() as ctx:
        den = k.sb("linear_den", [P, NT, H], F32, ctx)
        step = k.counter("linear_divide")
        counts = []
        with nc.Block() as block:

            @block.vector
            def _(dve):
                chain = Chain(dve, step)
                n = num[:].rearrange("p t (h e) -> p t h e", e=D + 1)
                chain(nc.vector.tensor_scalar(den[:], n[:, :, :, D], 1e-6, None, ALU.max))
                chain(nc.vector.reciprocal(den[:], den[:]))
                chain(nc.vector.tensor_tensor(y.rearrange("p t (h d) -> p t h d", d=D), n[:, :, :, 0:D], bcast(den[:], 3, D), ALU.mult))
                counts.append(chain.n)

        step.done(counts[0])




def retention_heads_stage(k, w, v, parts_dram, part, diag, ret):
    nc = k.nc
    LONG = 2 * BANK
    ACTU = [(i, 0, min(i * P, LONG)) for i in range(5, NT)]
    DVEU = []
    for i in range(1, NT):
        at = 0 if i < 5 else LONG
        while at < i * P:
            DVEU.append((i, at, min(BANK, i * P - at)))
            at += BANK
    ND = NT // QC
    NA, NV = len(ACTU), ND + len(DVEU)
    DRING = 3
    assert NV % DRING == 0
    OW = 32
    with ExitStack() as ctx:
        qm, km = w["q_max"], w["k_max"]
        sm = k.sb("own_scores", [P, 2, T], F32, ctx)
        sa = k.sb("own_positive", [P, 2, T], F32, ctx)
        vh = k.sb("ret_v_head", [P, 2, NT, OW], F32, ctx)
        twice = k.sb("twice_sum", [P, OW], F32, ctx)
        ot = k.sb("own_out_turned", [P, BANK], F32, ctx)
        a_ps = [k.ps(f"abs_act_ps{n}", [P, LONG], ctx) for n in range(2)]
        d_ps = [k.ps(f"abs_dve_ps{n}", [P, BANK], ctx) for n in range(DRING)]
        o_ps = k.ps("own_out_ps", [P, BANK], ctx)
        loaded = [k.counter(f"ret_rows_loaded{n}") for n in range(2)]
        a_full, a_used, d_full, d_used = (k.counter("abs_" + n) for n in ("act_full", "act_used", "dve_full", "dve_used"))
        v_ready, abs_ready = k.counter("ret_v_ready"), k.counter("own_abs_ready")
        o_ready, o_used, cleared = k.counter("own_out_ready"), k.counter("own_out_used"), k.counter("abs_cleared")
        o_copied, o_turned = k.counter("own_out_copied"), k.counter("own_out_turned")
        NL = 2 * PARTS * 16
        q_rows, k_rows = (parts_dram[s].rearrange("a (h d) t -> h a d t", d=D) for s in range(2))
        order = []
        for n in range(NV):
            order += [("a", m) for m in range(n * NA // NV, (n + 1) * NA // NV)]
            order.append(("d", n))
        PV_AT, TURN_AT, READ_AT = 8, 14, 16
        COPY_AT = (PV_AT + NQ) * NA // NV
        with nc.Block() as block:

            @block.sync
            def _(sp):
                def body(h, par, first=False):
                    if not first:
                        sp.wait_ge(a_full.sem, a_full.at(h * NA - NA))
                        sp.wait_ge(d_full.sem, d_full.at(h * NV - NV))
                    for a in range(PARTS):
                        at = slice(a * PARTS * D, (a + 1) * PARTS * D)
                        sp.dma_start(qm[at, par, :], bcast(q_rows[h, a], 0, PARTS)).then_inc(loaded[par].sem, 16)
                        sp.dma_start(km[at, par, :], k_rows[h]).then_inc(loaded[par].sem, 16)

                body(0, 0, first=True)
                body(1, 1, first=True)
                with sp.Fori(1, H // 2) as n:
                    for par in range(2):
                        body(2 * n + par, par)

            @block.gpsimd
            def _(pool):
                nc.gpsimd.memset(part[:], 0.0).then_inc(cleared.sem, 1)
                pool.wait_ge(cleared.sem, cleared.at(1))
                nc.gpsimd.memset(twice[:], 0.0).then_inc(cleared.sem, 1)
                pool.wait_ge(cleared.sem, cleared.at(2))
                nc.gpsimd.memset(twice[:, VD:VD + 1], 2.0).then_inc(cleared.sem, 1)
                pool.wait_ge(cleared.sem, cleared.at(3))
                nc.gpsimd.memset(vh[:], 0.0).then_inc(cleared.sem, 1)
                pool.wait_ge(cleared.sem, cleared.at(4))
                nc.gpsimd.memset(vh[:, :, :, VD:VD + 1], -1.0).then_inc(cleared.sem, 1)
                pool.wait_ge(cleared.sem, cleared.at(5))

                def body(h, par, first=False):
                    if not first:
                        pool.wait_ge(o_ready.sem, o_ready.at(h - 1))
                    pool.wait_ge(d_used.sem, d_used.at(h * NV + ND))
                    nc.gpsimd.tensor_copy(vh[:, par, :, 0:VD], v[:, :, bass.ds(h * VD, VD)]).then_inc(v_ready.sem, 1)
                    nc.gpsimd.tensor_scalar(sa[:, par, :], sm[:, par, :], 0.0, None, ALU.max).then_inc(abs_ready.sem, 1)
                    pool.wait_ge(abs_ready.sem, abs_ready.at(h + 1))

                body(0, 0, first=True)
                body(1, 1, first=True)
                with pool.Fori(1, H // 2) as n:
                    for par in range(2):
                        body(2 * n + par, par)

            @block.tensor
            def _(pe):
                def own_out(h, par, piece, first=False):
                    if piece == 0:
                        pe.wait_ge(v_ready.sem, v_ready.at(h + 1))
                        pe.wait_ge(abs_ready.sem, abs_ready.at(h + 1))
                        if not first:
                            pe.wait_ge(o_used.sem, o_used.at(2 * h))
                    for i in range(piece * QC, piece * QC + QC):
                        j, g, at = i // QC, i % QC, slice(i * P, (i + 1) * P)
                        o = o_ps[g * OW:(g + 1) * OW, j * P:(j + 1) * P]
                        nc.tensor.matmul(o, vh[:, par, i, :], sm[:, par, at], start=True, stop=False, tile_position=(0, g * OW))
                        ins = nc.tensor.matmul(o, twice[:], sa[:, par, at], start=False, stop=True, tile_position=(0, g * OW))
                    if piece == NQ - 1:
                        ins.then_inc(o_ready.sem, 1)

                def turn_out(h):
                    pe.wait_ge(o_copied.sem, o_copied.at(h + 1))
                    for j in range(NQ):
                        ins = nc.tensor.transpose(o_ps[:, j * P:(j + 1) * P], ot[:, j * P:(j + 1) * P], w["ident"][:])
                    ins.then_inc(o_turned.sem, 1)

                def body(h, turn, par, first=False, second=False):
                    pe.wait_ge(loaded[par].sem, loaded[par].at(turn * NL + NL))
                    for kind, n in order:
                        if kind == "a":
                            slot = (par * NA + n) % 2
                            if not first or n >= 2:
                                pe.wait_ge(a_used.sem, a_used.at(h * NA + (n - 1)))
                            i, at, width = ACTU[n]
                            for b in range(0, width, BANK):
                                ins = nc.tensor.matmul(a_ps[slot][:, b:min(b + BANK, width)], qm[:, par, i * P:(i + 1) * P],
                                                       km[:, par, at + b:at + min(b + BANK, width)], start=True, stop=True)
                            ins.then_inc(a_full.sem, 1)
                            continue
                        if not first or n >= DRING:
                            pe.wait_ge(d_used.sem, d_used.at(h * NV + (n + 1 - DRING)))
                        out = d_ps[n % DRING]
                        if n < ND:
                            for s in range(QC):
                                i = n * QC + s
                                ins = nc.tensor.matmul(out[:, s * P:(s + 1) * P], km[:, par, i * P:(i + 1) * P],
                                                       qm[:, par, i * P:(i + 1) * P], start=True, stop=True)
                        else:
                            i, at, width = DVEU[n - ND]
                            ins = nc.tensor.matmul(out[:, 0:width], qm[:, par, i * P:(i + 1) * P], km[:, par, at:at + width], start=True, stop=True)
                        ins.then_inc(d_full.sem, 1)
                        if PV_AT <= n < PV_AT + NQ and not first:
                            own_out(h - 1, 1 - par, n - PV_AT, first=second)
                        if n == TURN_AT and not first:
                            turn_out(h - 1)

                body(0, 0, 0, first=True)
                body(1, 0, 1, second=True)
                with pe.Fori(1, H // 2) as n:
                    for par in range(2):
                        body(2 * n + par, n, par)
                for piece in range(NQ):
                    own_out(H - 1, 1, piece)
                turn_out(H - 1)

            @block.scalar
            def _(act):
                act.wait_ge(cleared.sem, cleared.at(1))
                def copy_out(h):
                    act.wait_ge(o_ready.sem, o_ready.at(h + 1))
                    if not isinstance(h, int) or h > 0:
                        act.wait_ge(o_turned.sem, o_turned.at(h))
                    nc.scalar.copy(ot[:], o_ps[:]).then_inc(o_copied.sem, 1)

                def body(h, par, first=False):
                    for n, (i, at, width) in enumerate(ACTU):
                        if n == COPY_AT and not first:
                            copy_out(h - 1)
                        act.wait_ge(a_full.sem, a_full.at(h * NA + (n + 1)))
                        ps = a_ps[(par * NA + n) % 2][:, 0:width]
                        nc.scalar.activation(ps, ps, ACT.Abs, accum_out=part[:, bass.ds(h, 1), i, 0:1]).then_inc(a_used.sem, 1)

                body(0, 0, first=True)
                body(1, 1)
                with act.Fori(1, H // 2) as m:
                    for par in range(2):
                        body(2 * m + par, par)
                copy_out(H - 1)

            @block.vector
            def _(dve):
                dve.wait_ge(cleared.sem, cleared.at(1))

                def take_out(h):
                    dve.wait_ge(o_turned.sem, o_turned.at(h + 1))
                    o = o_ps[:].rearrange("p (t e) -> p t e", e=OW)
                    r = ret[:, :, bass.ds(h * VD, VD)]
                    nc.vector.tensor_tensor(r, o[:, :, 0:VD], r, ALU.add).then_inc(o_used.sem, 1)
                    nc.vector.tensor_copy(diag[:, bass.ds(h, 1), :], o[:, :, VD]).then_inc(o_used.sem, 1)

                def body(h, par, first=False, first_two=False):
                    for n in range(NV):
                        dve.wait_ge(d_full.sem, d_full.at(h * NV + (n + 1)))
                        if n < ND:
                            if n == 0 and not first_two:
                                dve.wait_ge(o_ready.sem, o_ready.at(h - 1))
                            nc.vector.tensor_tensor(sm[:, par, n * BANK:(n + 1) * BANK].rearrange("p (s t) -> p s t", t=P),
                                                    d_ps[n % DRING][:].rearrange("p (s t) -> p s t", t=P), bcast(w["keep_kq"][:], 1, QC),
                                                    ALU.mult).then_inc(d_used.sem, 1)
                        else:
                            i, at, width = DVEU[n - ND]
                            slot = 1 + (at // BANK) % 2
                            nc.vector.tensor_reduce(part[:, bass.ds(h, 1), i, slot:slot + 1], d_ps[n % DRING][:, 0:width], AX.X, ALU.add,
                                                    apply_absolute_value=True).then_inc(d_used.sem, 1)
                        if n == READ_AT and not first:
                            take_out(h - 1)

                body(0, 0, first=True, first_two=True)
                body(1, 1, first_two=True)
                with dve.Fori(1, H // 2) as n:
                    for par in range(2):
                        body(2 * n + par, par)
                take_out(H - 1)

        for par in range(2):
            loaded[par].done(NL * H // 2)
        cleared.done(5)
        a_full.done(NA * H)
        a_used.done(NA * H)
        d_full.done(NV * H)
        d_used.done(NV * H)
        v_ready.done(H)
        abs_ready.done(H)
        o_ready.done(H)
        o_copied.done(H)
        o_turned.done(H)
        o_used.done(2 * H)


def retention_norm_stage(k, w, part, diag, ret, gate, x):
    nc = k.nc
    eps = float(np.finfo(np.float32).eps)
    with ExitStack() as ctx:
        den = k.sb("ret_den", [P, NT, H], F32, ctx)
        sq = k.sb("ret_sq", [P, NT, H * VD], F32, ctx)
        ms = k.sb("ret_ms", [P, NT, H], F32, ctx)
        step, squared, ms_ready, std_ready, gated, biased = (k.counter("ret_" + n) for n in ("step", "squared", "ms", "std", "gated", "biased"))
        counts = []
        with nc.Block() as block:

            @block.scalar
            def _(act):
                nc.scalar.activation(sq[:], ret[:], ACT.Square).then_inc(squared.sem, 1)
                act.wait_ge(ms_ready.sem, ms_ready.at(1))
                nc.scalar.sqrt(ms[:], ms[:]).then_inc(std_ready.sem, 1)

            @block.gpsimd
            def _(pool):
                nc.gpsimd.tensor_tensor(gate[:], gate[:], ret[:], ALU.mult).then_inc(gated.sem, 1)
                nc.gpsimd.tensor_tensor(x[:], x[:], bcast(w["b_o"][:], 1, NT), ALU.add).then_inc(biased.sem, 1)

            @block.vector
            def _(dve):
                chain = Chain(dve, step)
                by_head = den[:].rearrange("p t h -> p h t")
                chain(nc.vector.tensor_reduce(by_head, part[:], AX.X, ALU.add))
                chain(nc.vector.tensor_tensor(by_head, by_head, diag[:], ALU.add))
                chain(nc.vector.tensor_scalar(den[:], den[:], 1.0, 50000.0, ALU.max, ALU.min))
                chain(nc.vector.reciprocal(den[:], den[:]))
                dve.wait_ge(squared.sem, squared.at(1))
                chain(nc.vector.tensor_reduce(ms[:], sq[:].rearrange("p t (h v) -> p t h v", v=VD), AX.X, ALU.add))
                chain(nc.vector.scalar_tensor_tensor(ms[:], ms[:], 1.0 / VD, den[:], ALU.mult, ALU.mult))
                chain(nc.vector.tensor_tensor(ms[:], ms[:], den[:], ALU.mult))
                nc.vector.tensor_scalar(ms[:], ms[:], eps, None, ALU.add).then_inc(ms_ready.sem, 1)
                dve.wait_ge(std_ready.sem, std_ready.at(1))
                chain(nc.vector.reciprocal(ms[:], ms[:]))
                chain(nc.vector.tensor_tensor(ms[:], ms[:], den[:], ALU.mult))
                dve.wait_ge(gated.sem, gated.at(1))
                gv = gate[:].rearrange("p t (h v) -> p t h v", v=VD)
                chain(nc.vector.tensor_tensor(gv, gv, bcast(ms[:], 3, VD), ALU.mult))
                counts.append(chain.n)

        step.done(counts[0])
        for s in (squared, ms_ready, std_ready, gated, biased):
            s.done(1)




def rwkv_stage(k, w, xn_t, out_t):
    nc = k.nc
    with ExitStack() as ctx:
        xm = k.sb("mixed", [P, 3, T], F32, ctx)
        om = k.sb("one_minus_mix", [P, 3], F32, ctx)
        kvr = k.sb("kvr", [P, 3, T], F32, ctx)
        wneg = k.sb("neg_decay", [P, 1], F32, ctx)
        pmax = k.sb("exp_max", [P, T + 1], F32, ctx)
        num = k.sb("wkv_num", [P, T + 1], F32, ctx)
        den = k.sb("wkv_den", [P, T + 1], F32, ctx)
        grow = k.sb("carry_factor", [P, T], F32, ctx)
        add = k.sb("new_factor", [P, T], F32, ctx)
        e1, e2 = xm[:, 0, :], xm[:, 1, :]
        top = xm[:, 2, :]
        wt = k.sb("decay_row", [P, T], F32, ctx)
        ps = k.ps("kvr_ps", [P, 4, BANK], ctx)
        step, mixed, fed, kept, w_ready = (k.counter("rwkv_" + n) for n in ("step", "mixed", "fed", "kept", "w"))
        args, exps = k.counter("rwkv_args"), k.counter("rwkv_exps")
        scaled, max_ready, den_ready, num_ready, add_ready, over = (k.counter("rwkv_" + n) for n in ("scaled", "max", "den", "num", "add", "over"))
        counts = []
        kk, vv, rr = kvr[:, 0, :], kvr[:, 1, :], kvr[:, 2, :]
        with nc.Block() as block:

            @block.vector
            def _(dve):
                chain = Chain(dve, step)
                chain(nc.vector.tensor_scalar(om[:], w["mix"][:], -1.0, 1.0, ALU.mult, ALU.add))
                for n in range(3):
                    dve.wait_ge(scaled.sem, scaled.at(n + 1))
                    nc.vector.scalar_tensor_tensor(xm[:, n, 1:], xn_t[:, 0:T - 1], om[:, n:n + 1], xm[:, n, 1:],
                                                   ALU.mult, ALU.add).then_inc(mixed.sem, 1)
                nc.vector.memset(pmax[:, 0:1], -1e38)
                nc.vector.memset(num[:, 0:1], 0.0)
                chain(nc.vector.memset(den[:, 0:1], 0.0))
                dve.wait_ge(w_ready.sem, w_ready.at(3))
                dve.wait_ge(kept.sem, kept.at(4))
                nc.vector.tensor_tensor_scan(pmax[:, 1:], wt[:], kk, -1e38, ALU.add, ALU.max).then_inc(max_ready.sem, 1)
                dve.wait_ge(max_ready.sem, max_ready.at(1))
                nc.vector.scalar_tensor_tensor(grow[:], pmax[:, 0:T], wneg[:, 0:1], pmax[:, 1:], ALU.add, ALU.subtract).then_inc(args.sem, 1)
                chain(nc.vector.scalar_tensor_tensor(wt[:], kk, w["first"][:, 0:1], pmax[:, 0:T], ALU.add, ALU.max))
                dve.wait_ge(kept.sem, kept.at(2 * NQ))
                nc.vector.tensor_tensor(e1, pmax[:, 0:T], wt[:], ALU.subtract).then_inc(args.sem, 1)
                nc.vector.scalar_tensor_tensor(e2, kk, w["first"][:, 0:1], wt[:], ALU.add, ALU.subtract).then_inc(args.sem, 1)
                dve.wait_ge(exps.sem, exps.at(2))
                nc.vector.tensor_tensor_scan(den[:, 1:], grow[:], add[:], 0.0, ALU.mult, ALU.add).then_inc(den_ready.sem, 1)
                dve.wait_ge(den_ready.sem, den_ready.at(1))
                chain(nc.vector.tensor_tensor(add[:], add[:], vv, ALU.mult))
                nc.vector.tensor_tensor_scan(num[:, 1:], grow[:], add[:], 0.0, ALU.mult, ALU.add).then_inc(num_ready.sem, 1)
                dve.wait_ge(exps.sem, exps.at(4))
                dve.wait_ge(num_ready.sem, num_ready.at(1))
                chain(nc.vector.tensor_tensor(grow[:], e1, den[:, 0:T], ALU.mult))
                chain(nc.vector.tensor_tensor(grow[:], grow[:], e2, ALU.add))
                dve.wait_ge(kept.sem, kept.at(3 * NQ))
                chain(nc.vector.scalar_tensor_tensor(grow[:], rr, 1.0, grow[:], ALU.add, ALU.mult))
                chain(nc.vector.reciprocal(grow[:], grow[:]))
                dve.wait_ge(over.sem, over.at(3))
                chain(nc.vector.tensor_tensor(out_t[:], top, grow[:], ALU.mult))
                counts.append(chain.n)

            @block.gpsimd
            def _(pool):
                pool.wait_ge(max_ready.sem, max_ready.at(1))
                nc.gpsimd.tensor_tensor(add[:], kk, pmax[:, 1:], ALU.subtract).then_inc(add_ready.sem, 1)
                pool.wait_ge(exps.sem, exps.at(4))
                pool.wait_ge(num_ready.sem, num_ready.at(1))
                nc.gpsimd.tensor_tensor(top, e1, num[:, 0:T], ALU.mult).then_inc(over.sem, 1)
                nc.gpsimd.tensor_tensor(vv, e2, vv, ALU.mult).then_inc(over.sem, 1)
                pool.wait_ge(over.sem, over.at(2))
                nc.gpsimd.tensor_tensor(top, top, vv, ALU.add).then_inc(over.sem, 1)

            @block.tensor
            def _(pe):
                for n in range(3):
                    pe.wait_ge(mixed.sem, mixed.at(n + 1))
                    for q in range(NQ):
                        u = n * NQ + q
                        if u >= 4:
                            pe.wait_ge(kept.sem, kept.at(u - 3))
                        nc.tensor.matmul(ps[:, u % 4, :], w["wT"][:, 8 + n, :], xm[:, n, q * BANK:(q + 1) * BANK],
                                         start=True, stop=True).then_inc(fed.sem, 1)

            @block.scalar
            def _(act):
                nc.scalar.activation(wneg[:], w["decay"][:], ACT.Exp).then_inc(w_ready.sem, 1)
                for n in range(3):
                    nc.scalar.activation(xm[:, n, :], xn_t[:], ACT.Copy, scale=w["mix"][:, n:n + 1]).then_inc(scaled.sem, 1)
                act.wait_ge(w_ready.sem, w_ready.at(1))
                nc.scalar.activation(wneg[:], wneg[:], ACT.Copy, scale=-1.0).then_inc(w_ready.sem, 1)
                act.wait_ge(w_ready.sem, w_ready.at(2))
                nc.scalar.activation(wt[:], xn_t[:], ACT.Identity, bias=wneg[:, 0:1], scale=0.0).then_inc(w_ready.sem, 1)
                for u in range(3 * NQ):
                    act.wait_ge(fed.sem, fed.at(u + 1))
                    dst = kvr[:, u // NQ, (u % NQ) * BANK:(u % NQ + 1) * BANK]
                    if u < 2 * NQ:
                        nc.scalar.copy(dst, ps[:, u % 4, :]).then_inc(kept.sem, 1)
                    else:
                        nc.scalar.activation(dst, ps[:, u % 4, :], ACT.Exp, scale=-1.0).then_inc(kept.sem, 1)
                act.wait_ge(args.sem, args.at(1))
                act.wait_ge(add_ready.sem, add_ready.at(1))
                for a in (grow[:], add[:]):
                    nc.scalar.activation(a, a, ACT.Exp).then_inc(exps.sem, 1)
                act.wait_ge(args.sem, args.at(3))
                for a in (e1, e2):
                    nc.scalar.activation(a, a, ACT.Exp).then_inc(exps.sem, 1)

        step.done(counts[0])
        mixed.done(3)
        fed.done(3 * NQ)
        kept.done(3 * NQ)
        w_ready.done(3)
        args.done(3)
        scaled.done(3)
        over.done(3)
        for sig in (max_ready, den_ready, num_ready, add_ready):
            sig.done(1)
        exps.done(4)




def conv_stage(k, w, h_t, hc_t):
    nc = k.nc
    step = k.counter("conv_step")
    counts = []
    with nc.Block() as block:

        @block.vector
        def _(dve):
            chain = Chain(dve, step)
            chain(nc.vector.tensor_scalar(hc_t[:], h_t[:], w["conv_w"][:, 2:3], None, ALU.mult))
            for tap in (1, 0):
                lag = 2 - tap
                chain(nc.vector.scalar_tensor_tensor(hc_t[:, lag:], h_t[:, 0:T - lag], w["conv_w"][:, tap:tap + 1], hc_t[:, lag:], ALU.mult, ALU.add))
            counts.append(chain.n)

    step.done(counts[0])


def experts_stage(k, w, h_t, y, x):
    nc = k.nc
    NF = DFF // P
    with ExitStack() as ctx:
        logits = k.sb("logits", [P, NT, E], F32, ctx)
        best = k.sb("best", [P, NT], F32, ctx)
        pick = k.sb("pick", [P, NT, E], F32, ctx)
        free = k.sb("not_picked", [P, NT], F32, ctx)
        gate = k.sb("gate", [P, 4, BANK], F32, ctx)
        hid = k.sb("hidden", [P, 2, NF, BANK], F32, ctx)
        lp = k.ps("logits_ps", [P, BANK], ctx)
        gp = [k.ps(f"gate_ps{n}", [P, BANK], ctx) for n in range(2)]
        vp = [k.ps(f"value_ps{n}", [P, BANK], ctx) for n in range(2)]
        op = [k.ps(f"expert_ps{n}", [P, BANK], ctx) for n in range(2)]
        routed, step, added = k.counter("routed"), k.counter("route_step"), k.counter("moe_added")
        upped, gated, hid_ready, downed, out_used = (k.counter("expert_" + n) for n in ("up", "gate", "hidden", "down", "used"))
        counts = []
        with nc.Block() as block:

            @block.tensor
            def _(pe):
                for i in range(NT):
                    ins = nc.tensor.matmul(lp[:, i * E:(i + 1) * E], h_t[:, i * P:(i + 1) * P], w["router"][:], start=True, stop=True)
                ins.then_inc(routed.sem, 1)

                def down(n, e):
                    pe.wait_ge(hid_ready.sem, hid_ready.at(n * (E * NF) + (e + 1) * NF))
                    for s in range(QC):
                        for f in range(NF):
                            ins = nc.tensor.matmul(op[e % 2][:, s * P:(s + 1) * P], hid[:, e % 2, f, s * P:(s + 1) * P],
                                                   w["expert_proj"][:, e % E, f, :], start=f == 0, stop=f == NF - 1)
                    ins.then_inc(downed.sem, 1)

                def body(n, first=False):
                    for g in range(E * NF):
                        e, f = g // NF, g % NF
                        if not first or g >= 2:
                            pe.wait_ge(hid_ready.sem, hid_ready.at(n * (E * NF) + (g - 1)))
                        rhs = h_t[:, bass.ds(n * BANK, BANK)]
                        nc.tensor.matmul(gp[g % 2][:], w["expert_wv"][:, e, f * P:(f + 1) * P], rhs, start=True, stop=True).then_inc(upped.sem, 1)
                        nc.tensor.matmul(vp[g % 2][:], w["expert_wv"][:, e, DFF + f * P:DFF + (f + 1) * P], rhs, start=True, stop=True).then_inc(upped.sem, 1)
                        if f == 1 and not (first and e == 0):
                            if not first or e >= 3:
                                pe.wait_ge(out_used.sem, out_used.at(n * (E * QC) + (e - 2) * QC))
                            down(n, e - 1)

                body(0, first=True)
                with pe.Fori(1, NQ) as n:
                    body(n)
                pe.wait_ge(out_used.sem, out_used.at(NQ * E * QC - 2 * QC))
                down(NQ, -1)

            @block.gpsimd
            def _(pool):
                nc.gpsimd.tensor_tensor(x[:], x[:], y[:], ALU.add).then_inc(added.sem, 1)

            @block.scalar
            def _(act):
                def body(n, first=False):
                    for g in range(E * NF):
                        act.wait_ge(upped.sem, upped.at(n * (2 * E * NF) + (2 * g + 1)))
                        if not first or g >= 4:
                            act.wait_ge(hid_ready.sem, hid_ready.at(n * (E * NF) + (g - 3)))
                        nc.scalar.activation(gate[:, g % 4, :], gp[g % 2][:], ACT.Silu).then_inc(gated.sem, 1)

                body(0, first=True)
                with act.Fori(1, NQ) as n:
                    body(n)

            @block.vector
            def _(dve):
                chain = Chain(dve, step)
                dve.wait_ge(routed.sem, routed.at(1))
                lv = lp[:, 0:NT * E].rearrange("p (t e) -> p t e", e=E)
                chain(nc.vector.tensor_copy(logits[:], lv))
                nc.vector.memset(free[:], 1.0)
                chain(nc.vector.tensor_reduce(best[:], logits[:], AX.X, ALU.max))
                for e in range(E):
                    chain(nc.vector.tensor_tensor(pick[:, :, e], logits[:, :, e], best[:], ALU.is_equal))
                    chain(nc.vector.tensor_tensor(pick[:, :, e], pick[:, :, e], free[:], ALU.mult))
                    chain(nc.vector.tensor_tensor(free[:], free[:], pick[:, :, e], ALU.subtract))

                dve.wait_ge(added.sem, added.at(1))

                def add_out(n, e):
                    dve.wait_ge(downed.sem, downed.at(n * E + (e + 1)))
                    for s in range(QC):
                        i = n * QC + s - (QC if e < 0 else 0)
                        if e != 0:
                            dve.wait_ge(out_used.sem, out_used.at(n * (E * QC) + ((e - 1) * QC + s + 1)))
                        xi = x[:, bass.ds(i, 1), :].rearrange("p o c -> p (o c)")
                        nc.vector.scalar_tensor_tensor(xi, op[e % 2][:, s * P:(s + 1) * P], pick[:, bass.ds(i, 1), e % E], xi,
                                                       ALU.mult, ALU.add).then_inc(out_used.sem, 1)

                def body(n, first=False):
                    for e in range(E):
                        for f in range(NF):
                            g = e * NF + f
                            dve.wait_ge(gated.sem, gated.at(n * (E * NF) + (g + 1)))
                            dve.wait_ge(upped.sem, upped.at(n * (2 * E * NF) + (2 * g + 2)))
                            if f == 0 and (not first or e >= 2):
                                dve.wait_ge(downed.sem, downed.at(n * E + (e - 1)))
                            nc.vector.tensor_tensor(hid[:, e % 2, f, :], vp[g % 2][:], gate[:, g % 4, :], ALU.mult).then_inc(hid_ready.sem, 1)
                            if f == 1 and not (first and e == 0):
                                add_out(n, e - 1)

                body(0, first=True)
                with dve.Fori(1, NQ) as n:
                    body(n)
                add_out(NQ, -1)
                counts.append(chain.n)

        routed.done(1)
        added.done(1)
        step.done(counts[0])
        upped.done(2 * NQ * E * NF)
        gated.done(NQ * E * NF)
        hid_ready.done(NQ * E * NF)
        downed.done(NQ * E)
        out_used.done(NQ * E * QC)


def store_stage(k, x, out):
    nc = k.nc
    stored = k.counter("stored")
    with nc.Block() as block:

        @block.sync
        def _(sp):
            sp.dma_start(out.rearrange("o (t p) c -> p (o t) c", p=P), x[:]).then_inc(stored.sem, 16)
            sp.wait_ge(stored.sem, stored.at(16))

    stored.done(16)




def softmax_layer(k, w, h_t, wqkv, wo, parts_dram, norm, x, loads=(), turns=()):
    with ExitStack() as ctx:
        qkv = k.sb("qkv", [P, NT, 3 * C], F32, ctx)
        qkv_stage(k, w, [([(h_t, wqkv)], qkv, None)], qkv, parts_dram, "norm" if norm else "rope", loads)
        y = k.sb("attn_out", [P, NT, C], F32, ctx)
        attention_stage(k, w, qkv, parts_dram, float(D) ** -0.5, y)
        output_stage(k, w, [(y, wo)], x, turns)


def spline_layer(k, w, x):
    with ExitStack() as ctx:
        xn = k.sb("xn", [P, NT, C], F32, ctx)
        xn_t = k.sb("xn_t", [P, T], F32, ctx)
        layer_norm(k, x, xn, w["ident"], xn_t)
        spline_ffn_stage(k, w, xn_t, x)


def retention_layer(k, w, x, parts_dram):
    with ExitStack() as ctx:
        qkv = k.sb("ret_qkv", [P, NT, BANK], F32, ctx)
        gate = k.sb("ret_gate", [P, NT, H * VD], F32, ctx)
        with ExitStack() as inner:
            xn = k.sb("xn", [P, NT, C], F32, inner)
            xn_t = k.sb("xn_t", [P, T], F32, inner)
            layer_norm(k, x, xn, w["ident"], xn_t)
            jobs = [([(xn_t, w["w_qkv_r"][:])], qkv, w["b_qkv_r"][:]), ([(xn_t, w["w_g"][:])], gate, w["b_g"][:])]
            qkv_stage(k, w, jobs, qkv, parts_dram, "decay")
        part = k.sb("abs_part", [P, H, NT, 3], F32, ctx)
        diag = k.sb("abs_diag", [P, H, NT], F32, ctx)
        ret = k.sb("ret_out", [P, NT, H * VD], F32, ctx)
        with ExitStack() as inner:
            q_t = k.sb("ret_q_t", [P, T], F32, inner)
            transpose_stage(k, [(qkv[:, :, 0:C], q_t)], w["ident"])
            chunk_stage(k, w, qkv[:, :, C:2 * C], qkv[:, :, 2 * C:], q_t, None, VD, w["bd16"][:], ret, inner=False)
        retention_heads_stage(k, w, qkv[:, :, 2 * C:], parts_dram, part, diag, ret)
        retention_norm_stage(k, w, part, diag, ret, gate, x)
        output_stage(k, w, [(gate[:, :, b * C:(b + 1) * C], w["w_o_r"][:, b, :]) for b in range(2)], x)


def linear_layer(k, w, x):
    with ExitStack() as ctx:
        xn_t = k.sb("xn_t", [P, T], F32, ctx)
        with ExitStack() as inner:
            xn = k.sb("xn", [P, NT, C], F32, inner)
            layer_norm(k, x, xn, w["ident"], xn_t)
        with ExitStack() as inner:
            qkv = k.sb("lin_qkv", [P, NT, 3 * C], F32, inner)
            v9 = k.sb("v9", [P, NT, H * (D + 1)], F32, inner)
            project_stage(k, [([(xn_t, w["wT"][:, 4:7, :].rearrange("p b c -> p (b c)"))], qkv, None)])
            linear_features_stage(k, w, qkv, v9)
            q_t = xn_t
            k_t = k.sb("lin_k_t", [P, T], F32, inner)
            transpose_stage(k, [(qkv[:, :, 0:C], q_t), (qkv[:, :, C:2 * C], k_t)], w["ident"])
            chunk_stage(k, w, qkv[:, :, C:2 * C], v9, q_t, k_t, D + 1, w["bd9"][:], v9)
            linear_divide_stage(k, v9, qkv[:, :, 0:C])
            output_stage(k, w, [(qkv[:, :, 0:C], w["wT"][:, 7, :])], x)


def rwkv_layer(k, w, x):
    with ExitStack() as ctx:
        xn_t = k.sb("xn_t", [P, T], F32, ctx)
        out_t = k.sb("rwkv_t", [P, T], F32, ctx)
        with ExitStack() as inner:
            xn = k.sb("xn", [P, NT, C], F32, inner)
            layer_norm(k, x, xn, w["ident"], xn_t)
        rwkv_stage(k, w, xn_t, out_t)
        project_stage(k, [([(out_t, w["wT"][:, 11, :])], x, None)], add_to=True)


def conv_moe_layer(k, w, x, parts_dram):
    nc = k.nc
    with ExitStack() as ctx:
        y = k.sb("moe_y", [P, NT, C], F32, ctx)
        layer_norm(k, x, y, w["ident"])
        with ExitStack() as inner:
            hc_t = k.sb("conv_t", [P, T], F32, inner)
            with ExitStack() as first:
                h = k.sb("ln1", [P, NT, C], F32, first)
                h_t = k.sb("ln1_t", [P, T], F32, first)
                layer_norm(k, y, h, w["ident"], h_t, affine=(w["ln1_w"], w["ln1_b"]))
                conv_stage(k, w, h_t, hc_t)
            softmax_layer(k, w, hc_t, w["attn_w"][:], w["proj_w"][:], parts_dram, False, y)
        with ExitStack() as inner:
            h = k.sb("ln2", [P, NT, C], F32, inner)
            h_t = k.sb("ln2_t", [P, T], F32, inner)
            layer_norm(k, y, h, w["ident"], h_t, affine=(w["ln2_w"], w["ln2_b"]))
            experts_stage(k, w, h_t, y, x)


def build(nc, d, out):
    ctx = ExitStack()
    with ctx:
        k = Kernel(nc, ctx)
        w = {name: k.sb(name, shape, dtype) for name, shape, dtype in [
            ("X", [P, NT, C], F32), ("wT", [P, 12, C], F32), ("ident", [P, P], F32), ("ident16", [P, P], BF16),
            ("mask16", [P, P], BF16), ("keep_kq", [P, P], F32),
            ("cos", [P, NT, D], F32), ("sin", [P, NT, D], F32), ("headmask", [P, H], F32),
            ("bd16", [P, H * VD], F32), ("bd9", [P, H * (D + 1)], F32),
            ("qdecay", [P, NT, H], F32), ("kdecay", [P, NT, H], F32), ("qn", [P, D], F32), ("kn", [P, D], F32),
            ("w_qkv_r", [P, BANK], F32), ("b_qkv_r", [P, BANK], F32), ("w_g", [P, H * VD], F32), ("b_g", [P, H * VD], F32),
            ("w_o_r", [P, 2, C], F32), ("b_o", [P, C], F32),
            ("Win", [P, M0], F32), ("bin", [P, 1], F32), ("W1", [P, INNER], F32), ("b1", [P, INNER], F32),
            ("W2", [P, INNER], F32), ("b2", [P, 1], F32), ("Wout", [P, C], F32), ("bout", [P, C], F32),
            ("mix", [P, 3], F32), ("decay", [P, 1], F32), ("first", [P, 1], F32),
            ("ln1_w", [P, 1], F32), ("ln1_b", [P, 1], F32), ("ln2_w", [P, 1], F32), ("ln2_b", [P, 1], F32),
            ("conv_w", [P, 3], F32), ("attn_w", [P, 3 * C], F32), ("proj_w", [P, C], F32), ("router", [P, E], F32),
            ("expert_wv", [P, E, 2 * DFF], F32), ("expert_proj", [P, E, DFF // P, C], F32),
            ("q_max", [P, 2, T], BF16), ("k_max", [P, 2, T], BF16), ("q_exp", [P, 2, T], BF16), ("k_exp", [P, 2, T], BF16)]}
        parts_dram = [nc.dram_tensor(f"{n}_parts", (PARTS, C, T), BF16, kind="Internal").ap() for n in "qk"]
        x = w["X"]
        with ExitStack() as inner:
            w["raw"] = k.sb("raw_weights", [P, 12, C], F32, inner)
            xn = k.sb("xn", [P, NT, C], F32, inner)
            xn_t = k.sb("xn_t", [P, T], F32, inner)
            load_stage(k, d, w)
            layer_norm(k, x, xn, w["ident"], xn_t)
            turns = [(w["raw"][:, b:b + QC, :], w["wT"][:, b:b + QC, :].rearrange("p a b -> p (a b)")) for b in (QC, 2 * QC)]
            softmax_layer(k, w, xn_t, w["wT"][:, 0:3, :].rearrange("p b c -> p (b c)"), w["wT"][:, 3, :], parts_dram, True, x,
                          rest_loads(d, w), turns)
        spline_layer(k, w, x)
        retention_layer(k, w, x, parts_dram)
        spline_layer(k, w, x)
        linear_layer(k, w, x)
        conv_moe_layer(k, w, x, parts_dram)
        rwkv_layer(k, w, x)
        conv_moe_layer(k, w, x, parts_dram)
        store_stage(k, x, out)


def shape_constants():
    t = np.arange(T, dtype=np.float32)
    freq = (1.0 / np.float32(10000.0) ** (np.arange(0, D // 2, dtype=np.float32) * np.float32(2.0) / np.float32(D))).astype(np.float32)
    ang = (t[:, None] * freq[None, :]).astype(np.float32)
    cos, sin = np.cos(ang), np.sin(ang)

    def tiles(a):
        return np.ascontiguousarray(a.reshape(NT, P, -1).transpose(1, 0, 2)).astype(np.float32)

    n = np.arange(P)
    head = np.arange(H, dtype=np.float64)
    gamma = np.log1p(-2.0 ** (-5.0 - head))
    pos = np.arange(T, dtype=np.float64)[:, None]
    decay_sum = -np.expm1(gamma * (pos + 1)) / -np.expm1(gamma)
    row = n // D
    return {
        "c_mask_qk": np.where(n[None, :] > n[:, None], NEG, 0.0).astype(np.float32),
        "c_keep_kq": (n[:, None] <= n[None, :]).astype(np.float32),
        "c_ident": np.eye(P, dtype=np.float32),
        "c_cos": tiles(np.concatenate([cos, cos], 1)),
        "c_sin": tiles(np.concatenate([-sin, sin], 1)),
        "c_headmask": (row[:, None] == np.arange(H)[None, :]).astype(np.float32),
        "c_bd16": (row[:, None] == np.arange(H * VD)[None, :] // VD).astype(np.float32),
        "c_bd9": (row[:, None] == np.arange(H * (D + 1))[None, :] // (D + 1)).astype(np.float32),
        "c_qdecay": tiles(np.exp(gamma * (pos - T // 2)) / np.sqrt(decay_sum)),
        "c_kdecay": tiles(np.exp(gamma * (T // 2 - pos))),
    }


def kernel(**inputs):
    import numpy as _np
    import concourse.bacc as _bacc
    from concourse import mybir as _mybir
    from concourse.bass_utils import run_bass_kernel_spmd as _run

    nc = _bacc.Bacc("TRN2", target_bir_lowering=False, num_devices=1)
    arrays, d = {}, {}
    for name, value in list(inputs.items()) + list(shape_constants().items()):
        a = _np.ascontiguousarray(value)
        arrays[f"in_{name}"] = a
        key = "x" if name == "L0_attn_a_x" else name
        d[key] = nc.dram_tensor(f"in_{name}", a.shape, _mybir.dt.from_np(a.dtype), kind="ExternalInput").ap()
    out = nc.dram_tensor("out_0", (1, T, C), F32, kind="ExternalOutput").ap()
    build(nc, d, out)
    r = _run(nc, [arrays], core_ids=[0])
    return r.results[0]["out_0"]
```
